# Optimizing a Trainium2 kernel written in Bass

```python
import numpy as np
import jax
import jax.numpy as jnp

def _softmax(x, axis=-1):
    return jax.nn.softmax(x, axis=axis)

def _gelu(x):
    return jax.nn.gelu(x, approximate=True)

def _silu(x):
    return jax.nn.silu(x)

def _sigmoid(x):
    return jax.nn.sigmoid(x)

def _layernorm(x, axis=-1, eps=1e-05):
    m = jnp.mean(x, axis=axis, keepdims=True)
    v = jnp.var(x, axis=axis, keepdims=True)
    return (x - m) / jnp.sqrt(v + eps)

def _scatter_add(tgt, idx, src, axis=0):
    return tgt.at[idx].add(src)

def _segment_sum(src, seg, n):
    return jax.ops.segment_sum(src, seg, n)
kernel_name = 'mk_vit_tower_postln_d2_tok_img256_r4_fbe535'

def setup_inputs(seed: int=0):
    np.random.seed(seed)
    _w = jnp.asarray

    def _rec_inputs():
        import jax
        import jax.numpy as jnp
        _rk = jax.random.key(seed)
        x = -0.000202321 + 1.00025 * jax.random.normal(jax.random.fold_in(_rk, 1), (4, 64, 56, 56), jnp.float32)
        return x
    x = _rec_inputs()

    def _L0_tok_setup():
        import jax, jax.numpy as jnp
        import numpy as np
        B, C, H, W = (8, 64, 56, 56)
        K = 3

        def _unfold3x3(x):
            b, c, h, w = x.shape
            xp = jnp.pad(x, ((0, 0), (0, 0), (1, 1), (1, 1)))
            patches = jnp.stack([xp[:, :, i:i + h, j:j + w] for i in range(K) for j in range(K)], axis=2)
            return patches.reshape(b, c * K * K, h * w).transpose(0, 2, 1)
        key = jax.random.key(seed)
        ks = jax.random.split(key, 8)
        d = C * K * K
        s1 = 1.0 / np.sqrt(d)
        s2 = 1.0 / np.sqrt(C)
        return {'x': jax.random.normal(ks[0], (B, C, H, W), jnp.float32), 'W1': jax.random.uniform(ks[1], (d, C), jnp.float32, -s1, s1), 'b1': jax.random.uniform(ks[2], (C,), jnp.float32, -s1, s1), 'W2': jax.random.uniform(ks[3], (C, d), jnp.float32, -s2, s2), 'b2': jax.random.uniform(ks[4], (d,), jnp.float32, -s2, s2), 'W3': jax.random.uniform(ks[5], (d, C), jnp.float32, -s1, s1), 'b3': jax.random.uniform(ks[6], (C,), jnp.float32, -s1, s1)}
    _L0_tok_all = _L0_tok_setup()
    _L0_tok_in = {k: v for k, v in _L0_tok_all.items() if k in ('W1', 'b1', 'W2', 'b2', 'W3', 'b3')}
    del _L0_tok_all

    def _L0_attn_setup():
        import jax, jax.numpy as jnp
        import numpy as np
        DIM = 64
        D_STATE = 32
        EXPAND = 2
        E = EXPAND * DIM
        DT_RANK = (DIM + 15) // 16
        D_CONV = 4
        B = 4
        L = 256

        def layernorm(x, g, b, eps=1e-05):
            m = jnp.mean(x, axis=-1, keepdims=True)
            v = jnp.var(x, axis=-1, keepdims=True)
            return (x - m) / jnp.sqrt(v + eps) * g + b

        def dwconv(x_bcl, w, b, pad):
            y = jax.lax.conv_general_dilated(x_bcl, w, window_strides=(1,), padding=[pad], feature_group_count=x_bcl.shape[1], dimension_numbers=('NCW', 'OIW', 'NCW'))
            return y + b[None, :, None]

        def selective_scan(u, dt, A, Bm, Cm, D):
            dA = jnp.exp(dt[..., None] * A)
            dBu = dt[..., None] * Bm[:, :, None, :] * u[..., None]

            def step(h, inp):
                dA_t, dBu_t = inp
                h = dA_t * h + dBu_t
                return (h, h)
            h0 = jnp.zeros((u.shape[0], E, D_STATE), u.dtype)
            _, hs = jax.lax.scan(step, h0, (dA.transpose(1, 0, 2, 3), dBu.transpose(1, 0, 2, 3)))
            y = jnp.einsum('lben,bln->ble', hs, Cm)
            return y + u * D

        def mamba(x, in_proj_w, ssm_conv_w, ssm_conv_b, x_proj_w, dt_proj_w, dt_proj_b, A_log, Dp, out_proj_w):
            xz = x @ in_proj_w.T
            xin, z = (xz[..., :E], xz[..., E:])
            xc = dwconv(xin.transpose(0, 2, 1), ssm_conv_w, ssm_conv_b, (D_CONV - 1, 0))
            u = jax.nn.silu(xc).transpose(0, 2, 1)
            dbl = u @ x_proj_w.T
            dt_r = dbl[..., :DT_RANK]
            Bm = dbl[..., DT_RANK:DT_RANK + D_STATE]
            Cm = dbl[..., DT_RANK + D_STATE:]
            dt = jax.nn.softplus(dt_r @ dt_proj_w.T + dt_proj_b)
            A = -jnp.exp(A_log)
            y = selective_scan(u, dt, A, Bm, Cm, Dp)
            y = y * jax.nn.silu(z)
            return y @ out_proj_w.T
        key = jax.random.key(seed)
        ks = jax.random.split(key, 12)
        f = lambda k, s, sc=0.02: jax.random.normal(k, s, jnp.float32) * sc
        dt_init = jnp.exp(jax.random.uniform(ks[10], (E,), jnp.float32, np.log(0.001), np.log(0.1)))
        dt_bias = dt_init + jnp.log(-jnp.expm1(-dt_init))
        A_log = jnp.log(jnp.tile(jnp.arange(1, D_STATE + 1, dtype=jnp.float32), (E, 1)))
        return {'x': jax.random.normal(ks[0], (B, L, DIM), jnp.float32), 'norm1_g': jnp.ones((DIM,), jnp.float32), 'norm1_b': jnp.zeros((DIM,), jnp.float32), 'conv_w': f(ks[1], (DIM, 1, 3), 0.1), 'conv_b': jnp.zeros((DIM,), jnp.float32), 'in_proj_w': f(ks[2], (2 * E, DIM)), 'ssm_conv_w': f(ks[3], (E, 1, D_CONV), 0.1), 'ssm_conv_b': jnp.zeros((E,), jnp.float32), 'x_proj_w': f(ks[4], (DT_RANK + 2 * D_STATE, E)), 'dt_proj_w': f(ks[5], (E, DT_RANK), 0.1), 'dt_proj_b': dt_bias, 'A_log': A_log, 'Dp': jnp.ones((E,), jnp.float32), 'out_proj_w': f(ks[6], (DIM, E)), 'norm2_g': jnp.ones((DIM,), jnp.float32), 'norm2_b': jnp.zeros((DIM,), jnp.float32), 'mlp_w1': f(ks[7], (4 * DIM, DIM)), 'mlp_b1': jnp.zeros((4 * DIM,), jnp.float32), 'mlp_w2': f(ks[8], (DIM, 4 * DIM)), 'mlp_b2': jnp.zeros((DIM,), jnp.float32)}
    _L0_attn_all = _L0_attn_setup()
    _L0_attn_in = {k: v for k, v in _L0_attn_all.items() if k in ('norm1_g', 'norm1_b', 'conv_w', 'conv_b', 'in_proj_w', 'ssm_conv_w', 'ssm_conv_b', 'x_proj_w', 'dt_proj_w', 'dt_proj_b', 'A_log', 'Dp', 'out_proj_w', 'norm2_g', 'norm2_b', 'mlp_w1', 'mlp_b1', 'mlp_w2', 'mlp_b2')}
    del _L0_attn_all

    def _L0_ffn_setup():
        import jax, jax.numpy as jnp
        import numpy as np
        C = 64
        HID = 256
        E = 8
        TEMP = 1.0
        key = jax.random.key(seed)
        ks = jax.random.split(key, 7)
        x = jax.random.normal(ks[0], (8, 4096, C), dtype=jnp.float32)
        W1 = jax.random.normal(ks[1], (C, HID), dtype=jnp.float32) * 0.02
        b1 = jnp.zeros((HID,), dtype=jnp.float32)
        Wg = jax.random.normal(ks[2], (HID, E), dtype=jnp.float32) * 0.02
        bg = jnp.zeros((E,), dtype=jnp.float32)
        Wd = jax.random.normal(ks[3], (E, HID, C), dtype=jnp.float32) * 0.02
        bd = jnp.zeros((E, C), dtype=jnp.float32)
        return {'x': x, 'W1': W1, 'b1': b1, 'Wg': Wg, 'bg': bg, 'Wd': Wd, 'bd': bd}
    _L0_ffn_all = _L0_ffn_setup()
    _L0_ffn_in = {k: v for k, v in _L0_ffn_all.items() if k in ('W1', 'b1', 'Wg', 'bg', 'Wd', 'bd')}
    del _L0_ffn_all

    def _L1_attn_setup():
        import jax, jax.numpy as jnp
        import numpy as np
        DIM = 64
        NUM_HEADS = 8
        B = 4
        N = 512
        HEAD_DIM = DIM // NUM_HEADS
        SCALE = HEAD_DIM ** (-0.5)
        MASK_NEG = -1000.0

        def _block_mask(n):
            half = n // 2
            top = jnp.concatenate([jnp.ones((half, half)), jnp.zeros((half, half))], axis=1)
            bot = jnp.tril(jnp.ones((half, n)), k=half)
            m = jnp.concatenate([top, bot], axis=0)
            return jnp.where(m != 0, 0.0, MASK_NEG).astype(jnp.float32)
        key = jax.random.key(seed)
        k1, k2 = jax.random.split(key, 2)
        x = jax.random.normal(k1, (B, N, DIM), dtype=jnp.float32)
        W_qkv = jax.random.normal(k2, (DIM, 3 * DIM), dtype=jnp.float32) * DIM ** (-0.5)
        b_qkv = jnp.zeros((3 * DIM,), dtype=jnp.float32)
        return {'x': x, 'W_qkv': W_qkv, 'b_qkv': b_qkv}
    _L1_attn_all = _L1_attn_setup()
    _L1_attn_in = {k: v for k, v in _L1_attn_all.items() if k in ('W_qkv', 'b_qkv')}
    del _L1_attn_all

    def _L1_ffn_setup():
        import jax, jax.numpy as jnp
        import numpy as np
        B, S, D = (8, 1024, 64)
        H = 4 * D
        CAPACITY = 0.5
        key = jax.random.key(seed)
        ks = jax.random.split(key, 6)
        x = jax.random.normal(ks[0], (B, S, D), dtype=jnp.float32)
        attention_mask = jnp.zeros((B, 1, 1, S), dtype=jnp.float32)
        wr = jax.random.normal(ks[1], (D, 1), dtype=jnp.float32) * 0.02
        br = jnp.zeros((1,), dtype=jnp.float32)
        w1 = jax.random.normal(ks[2], (D, H), dtype=jnp.float32) * 0.02
        b1 = jnp.zeros((H,), dtype=jnp.float32)
        w2 = jax.random.normal(ks[3], (H, D), dtype=jnp.float32) * 0.02
        b2 = jnp.zeros((D,), dtype=jnp.float32)
        return {'x': x, 'attention_mask': attention_mask, 'wr': wr, 'br': br, 'w1': w1, 'b1': b1, 'w2': w2, 'b2': b2}
    _L1_ffn_all = _L1_ffn_setup()
    _L1_ffn_in = {k: v for k, v in _L1_ffn_all.items() if k in ('attention_mask', 'wr', 'br', 'w1', 'b1', 'w2', 'b2')}
    del _L1_ffn_all
    return {'x': x, 'L0_tok_W1': _L0_tok_in['W1'], 'L0_tok_b1': _L0_tok_in['b1'], 'L0_tok_W2': _L0_tok_in['W2'], 'L0_tok_b2': _L0_tok_in['b2'], 'L0_tok_W3': _L0_tok_in['W3'], 'L0_tok_b3': _L0_tok_in['b3'], 'L0_attn_norm1_g': _L0_attn_in['norm1_g'], 'L0_attn_norm1_b': _L0_attn_in['norm1_b'], 'L0_attn_conv_w': _L0_attn_in['conv_w'], 'L0_attn_conv_b': _L0_attn_in['conv_b'], 'L0_attn_in_proj_w': _L0_attn_in['in_proj_w'], 'L0_attn_ssm_conv_w': _L0_attn_in['ssm_conv_w'], 'L0_attn_ssm_conv_b': _L0_attn_in['ssm_conv_b'], 'L0_attn_x_proj_w': _L0_attn_in['x_proj_w'], 'L0_attn_dt_proj_w': _L0_attn_in['dt_proj_w'], 'L0_attn_dt_proj_b': _L0_attn_in['dt_proj_b'], 'L0_attn_A_log': _L0_attn_in['A_log'], 'L0_attn_Dp': _L0_attn_in['Dp'], 'L0_attn_out_proj_w': _L0_attn_in['out_proj_w'], 'L0_attn_norm2_g': _L0_attn_in['norm2_g'], 'L0_attn_norm2_b': _L0_attn_in['norm2_b'], 'L0_attn_mlp_w1': _L0_attn_in['mlp_w1'], 'L0_attn_mlp_b1': _L0_attn_in['mlp_b1'], 'L0_attn_mlp_w2': _L0_attn_in['mlp_w2'], 'L0_attn_mlp_b2': _L0_attn_in['mlp_b2'], 'L0_ffn_W1': _L0_ffn_in['W1'], 'L0_ffn_b1': _L0_ffn_in['b1'], 'L0_ffn_Wg': _L0_ffn_in['Wg'], 'L0_ffn_bg': _L0_ffn_in['bg'], 'L0_ffn_Wd': _L0_ffn_in['Wd'], 'L0_ffn_bd': _L0_ffn_in['bd'], 'L1_attn_W_qkv': _L1_attn_in['W_qkv'], 'L1_attn_b_qkv': _L1_attn_in['b_qkv'], 'L1_ffn_attention_mask': _L1_ffn_in['attention_mask'], 'L1_ffn_wr': _L1_ffn_in['wr'], 'L1_ffn_br': _L1_ffn_in['br'], 'L1_ffn_w1': _L1_ffn_in['w1'], 'L1_ffn_b1': _L1_ffn_in['b1'], 'L1_ffn_w2': _L1_ffn_in['w2'], 'L1_ffn_b2': _L1_ffn_in['b2']}

def reference(x, L0_tok_W1, L0_tok_b1, L0_tok_W2, L0_tok_b2, L0_tok_W3, L0_tok_b3, L0_attn_norm1_g, L0_attn_norm1_b, L0_attn_conv_w, L0_attn_conv_b, L0_attn_in_proj_w, L0_attn_ssm_conv_w, L0_attn_ssm_conv_b, L0_attn_x_proj_w, L0_attn_dt_proj_w, L0_attn_dt_proj_b, L0_attn_A_log, L0_attn_Dp, L0_attn_out_proj_w, L0_attn_norm2_g, L0_attn_norm2_b, L0_attn_mlp_w1, L0_attn_mlp_b1, L0_attn_mlp_w2, L0_attn_mlp_b2, L0_ffn_W1, L0_ffn_b1, L0_ffn_Wg, L0_ffn_bg, L0_ffn_Wd, L0_ffn_bd, L1_attn_W_qkv, L1_attn_b_qkv, L1_ffn_attention_mask, L1_ffn_wr, L1_ffn_br, L1_ffn_w1, L1_ffn_b1, L1_ffn_w2, L1_ffn_b2):
    import jax
    import jax.numpy as jnp

    def _L0_tok_ref(x, W1, b1, W2, b2, W3, b3):
        import jax, jax.numpy as jnp
        import numpy as np
        B, C, H, W = (8, 64, 56, 56)
        K = 3

        def _unfold3x3(x):
            b, c, h, w = x.shape
            xp = jnp.pad(x, ((0, 0), (0, 0), (1, 1), (1, 1)))
            patches = jnp.stack([xp[:, :, i:i + h, j:j + w] for i in range(K) for j in range(K)], axis=2)
            return patches.reshape(b, c * K * K, h * w).transpose(0, 2, 1)
        t = _unfold3x3(x)
        h1 = jax.nn.relu(jnp.einsum('bld,dc->blc', t, W1) + b1)
        s = jax.nn.sigmoid(jnp.einsum('blc,cd->bld', h1, W2) + b2)
        out = jnp.einsum('bld,dc->blc', t * s, W3) + b3
        return out

    def _L0_attn_ref(x, norm1_g, norm1_b, conv_w, conv_b, in_proj_w, ssm_conv_w, ssm_conv_b, x_proj_w, dt_proj_w, dt_proj_b, A_log, Dp, out_proj_w, norm2_g, norm2_b, mlp_w1, mlp_b1, mlp_w2, mlp_b2):
        import jax, jax.numpy as jnp
        import numpy as np
        DIM = 64
        D_STATE = 32
        EXPAND = 2
        E = EXPAND * DIM
        DT_RANK = (DIM + 15) // 16
        D_CONV = 4
        B = 4
        L = 256

        def layernorm(x, g, b, eps=1e-05):
            m = jnp.mean(x, axis=-1, keepdims=True)
            v = jnp.var(x, axis=-1, keepdims=True)
            return (x - m) / jnp.sqrt(v + eps) * g + b

        def dwconv(x_bcl, w, b, pad):
            y = jax.lax.conv_general_dilated(x_bcl, w, window_strides=(1,), padding=[pad], feature_group_count=x_bcl.shape[1], dimension_numbers=('NCW', 'OIW', 'NCW'))
            return y + b[None, :, None]

        def selective_scan(u, dt, A, Bm, Cm, D):
            dA = jnp.exp(dt[..., None] * A)
            dBu = dt[..., None] * Bm[:, :, None, :] * u[..., None]

            def step(h, inp):
                dA_t, dBu_t = inp
                h = dA_t * h + dBu_t
                return (h, h)
            h0 = jnp.zeros((u.shape[0], E, D_STATE), u.dtype)
            _, hs = jax.lax.scan(step, h0, (dA.transpose(1, 0, 2, 3), dBu.transpose(1, 0, 2, 3)))
            y = jnp.einsum('lben,bln->ble', hs, Cm)
            return y + u * D

        def mamba(x, in_proj_w, ssm_conv_w, ssm_conv_b, x_proj_w, dt_proj_w, dt_proj_b, A_log, Dp, out_proj_w):
            xz = x @ in_proj_w.T
            xin, z = (xz[..., :E], xz[..., E:])
            xc = dwconv(xin.transpose(0, 2, 1), ssm_conv_w, ssm_conv_b, (D_CONV - 1, 0))
            u = jax.nn.silu(xc).transpose(0, 2, 1)
            dbl = u @ x_proj_w.T
            dt_r = dbl[..., :DT_RANK]
            Bm = dbl[..., DT_RANK:DT_RANK + D_STATE]
            Cm = dbl[..., DT_RANK + D_STATE:]
            dt = jax.nn.softplus(dt_r @ dt_proj_w.T + dt_proj_b)
            A = -jnp.exp(A_log)
            y = selective_scan(u, dt, A, Bm, Cm, Dp)
            y = y * jax.nn.silu(z)
            return y @ out_proj_w.T
        res = x
        h = layernorm(x, norm1_g, norm1_b)
        h_conv = dwconv(h.transpose(0, 2, 1), conv_w, conv_b, (1, 1)).transpose(0, 2, 1)
        h = mamba(h_conv + h, in_proj_w, ssm_conv_w, ssm_conv_b, x_proj_w, dt_proj_w, dt_proj_b, A_log, Dp, out_proj_w)
        h = res + h
        m = layernorm(h, norm2_g, norm2_b)
        m = jax.nn.gelu(m @ mlp_w1.T + mlp_b1, approximate=False) @ mlp_w2.T + mlp_b2
        return h + m

    def _L0_ffn_ref(x, W1, b1, Wg, bg, Wd, bd):
        import jax, jax.numpy as jnp
        import numpy as np
        C = 64
        HID = 256
        E = 8
        TEMP = 1.0
        orig_shape = x.shape
        xf = x.reshape(-1, orig_shape[-1])
        H = jax.nn.gelu(xf @ W1 + b1, approximate=False)
        probs = jax.nn.softmax((H @ Wg + bg) / TEMP, axis=-1)
        assign = jnp.argmax(probs, axis=-1)
        out = jnp.zeros_like(xf)
        for e in range(Wd.shape[0]):
            y = H @ Wd[e] + bd[e]
            sel = (assign == e)[:, None]
            out = out + jnp.where(sel, probs[:, e:e + 1] * y, 0.0)
        return out.reshape(orig_shape)

    def _L1_attn_ref(x, W_qkv, b_qkv):
        import jax, jax.numpy as jnp
        import numpy as np
        DIM = 64
        NUM_HEADS = 8
        B = 4
        N = 512
        HEAD_DIM = DIM // NUM_HEADS
        SCALE = HEAD_DIM ** (-0.5)
        MASK_NEG = -1000.0

        def _block_mask(n):
            half = n // 2
            top = jnp.concatenate([jnp.ones((half, half)), jnp.zeros((half, half))], axis=1)
            bot = jnp.tril(jnp.ones((half, n)), k=half)
            m = jnp.concatenate([top, bot], axis=0)
            return jnp.where(m != 0, 0.0, MASK_NEG).astype(jnp.float32)
        B_, Nn, C = x.shape
        qkv = x @ W_qkv + b_qkv
        qkv = qkv.reshape(B_, Nn, 3, NUM_HEADS, C // NUM_HEADS)
        qkv = jnp.transpose(qkv, (2, 0, 3, 1, 4))
        q, k, v = (qkv[0] * SCALE, qkv[1], qkv[2])
        attn = jnp.einsum('bhqd,bhkd->bhqk', q, k) + _block_mask(Nn)
        attn = jax.nn.softmax(attn, axis=-1)
        out = jnp.einsum('bhqk,bhkd->bhqd', attn, v)
        return jnp.transpose(out, (0, 2, 1, 3)).reshape(B_, Nn, C)

    def _L1_ffn_ref(x, attention_mask, wr, br, w1, b1, w2, b2):
        import jax, jax.numpy as jnp
        import numpy as np
        B, S, D = (8, 1024, 64)
        H = 4 * D
        CAPACITY = 0.5
        b, s, d = x.shape
        weights = (jnp.einsum('bsd,do->bso', x, wr) + br)[..., 0]
        k = max(1, int(CAPACITY * s))
        kk = k - 1 if k > 1 else 1
        _, idx = jax.lax.top_k(weights, k)
        sel_idx = idx[:, :kk]
        sel = jnp.take_along_axis(x, sel_idx[:, :, None], axis=1)
        h = jax.nn.gelu(jnp.einsum('bkd,dh->bkh', sel, w1) + b1)
        y = jnp.einsum('bkh,hd->bkd', h, w2) + b2
        w_sel = jnp.take_along_axis(weights, sel_idx, axis=1)
        y = y * w_sel[..., None]
        batch_idx = jnp.arange(b)[:, None]
        processed = jnp.zeros_like(x).at[batch_idx, sel_idx].set(y)
        return processed + x
    h = _L0_tok_ref(x, L0_tok_W1, L0_tok_b1, L0_tok_W2, L0_tok_b2, L0_tok_W3, L0_tok_b3)
    h = _layernorm(h + _L0_attn_ref(h, L0_attn_norm1_g, L0_attn_norm1_b, L0_attn_conv_w, L0_attn_conv_b, L0_attn_in_proj_w, L0_attn_ssm_conv_w, L0_attn_ssm_conv_b, L0_attn_x_proj_w, L0_attn_dt_proj_w, L0_attn_dt_proj_b, L0_attn_A_log, L0_attn_Dp, L0_attn_out_proj_w, L0_attn_norm2_g, L0_attn_norm2_b, L0_attn_mlp_w1, L0_attn_mlp_b1, L0_attn_mlp_w2, L0_attn_mlp_b2), axis=-1)
    h = _layernorm(h + _L0_ffn_ref(h, L0_ffn_W1, L0_ffn_b1, L0_ffn_Wg, L0_ffn_bg, L0_ffn_Wd, L0_ffn_bd), axis=-1)
    h = _layernorm(h + _L1_attn_ref(h, L1_attn_W_qkv, L1_attn_b_qkv), axis=-1)
    h = _layernorm(h + _L1_ffn_ref(h, L1_ffn_attention_mask, L1_ffn_wr, L1_ffn_br, L1_ffn_w1, L1_ffn_b1, L1_ffn_w2, L1_ffn_b2), axis=-1)
    return h

_drawn_inputs = setup_inputs


def setup_inputs(seed=0):
    import zlib

    import numpy as np

    out = dict(_drawn_inputs(seed))
    spreads = {'L0_attn_norm1_g': (1.0, 0.6),
     'L0_attn_norm1_b': (0.0, 0.8),
     'L0_attn_conv_b': (0.0, 0.8),
     'L0_attn_ssm_conv_b': (0.0, 0.8),
     'L0_attn_Dp': (1.0, 0.6),
     'L0_attn_norm2_g': (1.0, 0.6),
     'L0_attn_norm2_b': (0.0, 2.0),
     'L0_attn_mlp_b1': (0.0, 0.368),
     'L0_attn_mlp_b2': (0.0, 0.1),
     'L0_ffn_b1': (0.0, 0.8),
     'L0_ffn_bg': (0.0, 0.401),
     'L0_ffn_bd': (0.0, 0.529),
     'L1_attn_b_qkv': (0.0, 0.1),
     'L1_ffn_b1': (0.0, 0.8),
     'L1_ffn_b2': (0.0, 0.8)}
    factors = {'L0_tok_b1': 8.0,
     'L0_attn_conv_w': 8.0,
     'L0_attn_in_proj_w': 8.0,
     'L0_attn_ssm_conv_w': 8.0,
     'L0_attn_x_proj_w': 8.0,
     'L0_attn_dt_proj_w': 8.0,
     'L0_attn_dt_proj_b': 8.0,
     'L0_attn_A_log': 8.0,
     'L0_attn_out_proj_w': 8.0,
     'L0_ffn_W1': 8.0,
     'L0_ffn_Wg': 8.0,
     'L0_ffn_Wd': 8.0,
     'L1_ffn_wr': 8.0,
     'L1_ffn_w1': 8.0,
     'L1_ffn_w2': 8.0}
    for name, (base, spread) in spreads.items():
        noise = np.random.default_rng([zlib.crc32(name.encode()), seed]).standard_normal(out[name].shape)
        drawn = base * np.exp(spread * noise) if base else spread * noise
        out[name] = jnp.asarray(drawn.astype(out[name].dtype))
    for name, factor in factors.items():
        out[name] = (out[name] * factor).astype(out[name].dtype)
    return out
```

```python
from contextlib import ExitStack

import concourse.bass as bass
import numpy as np
from concourse import mybir

ALU = mybir.AluOpType
ACT = mybir.ActivationFunctionType
F32 = mybir.dt.float32
BF16 = mybir.dt.bfloat16
U32 = mybir.dt.uint32
AX_X = mybir.AxisListType.X

B, C, IMG = 4, 64, 56
L = IMG * IMG
T = B * L
ROWS = 8
CH = ROWS * IMG
NJ = L // CH
PW = IMG + 2
E, N_STATE, DT_RANK = 128, 32, 4
HID = 256
N_EXP = 8
HEADS, HD = 8, 8
EPS = 1e-5
LEAD = 2


def pairs(eng):
    with eng.Fori(0, 2) as half:
        with eng.Fori(0, NJ) as j:
            yield half * NJ + j, half, j


class Done:

    def __init__(self, sem, lead=LEAD):
        self.sem, self.lead = sem, lead

    def start(self, eng):
        eng.sem_inc(self.sem, self.lead)

    def wait(self, eng, n):
        eng.wait_ge(self.sem, n + (1 + self.lead))

    def wait_free(self, eng, n, depth=None):
        eng.wait_ge(self.sem, n + (1 + self.lead - (depth or self.lead)))


class Order:

    def __init__(self, eng, sem, per_iteration):
        self.eng, self.sem, self.per = eng, sem, per_iteration

    def at(self, iteration):
        self.base, self.k = iteration * self.per, 0

    def __call__(self, ins):
        ins.then_inc(self.sem, 1)
        self.k += 1
        assert self.k <= self.per
        self.eng.wait_ge(self.sem, self.base + self.k)


class Place:

    def __init__(self, nc, stage, ctx, sems):
        self.nc, self.stage, self.ctx, self.sems = nc, stage, ctx, sems

    def sb(self, name, shape, dt=F32):
        return self.ctx.enter_context(self.nc.sbuf_tensor(f"sb_{self.stage}_{name}", shape, dt))

    def bank(self, name, dt=F32):
        return self.ctx.enter_context(self.nc.psum_tensor(f"{self.stage}_{name}", [128, 512], dt))

    def sem(self, name):
        self.sems.append(self.nc.alloc_semaphore(name=f"{self.stage}_{name}"))
        return self.sems[-1]

    def done(self, name, lead=LEAD):
        return Done(self.sem(name), lead)


def pad_image(nc, sems, A):
    with ExitStack() as ctx:
        m = Place(nc, "pad", ctx, sems)
        img = m.sb("img", [128, 2, PW, PW])
        zeroed, loaded, stored = m.sem("zeroed"), m.sem("loaded"), m.sem("stored")
        block = ctx.enter_context(nc.Block())

        @block.vector
        def _(dve):
            dve.memset(img[:], 0.0).then_inc(zeroed, 1)

        @block.sync
        def _(sp):
            sp.wait_ge(zeroed, 1)
            for h in range(2):
                for s in range(2):
                    sp.dma_start(img[C * s:C * s + C, h, 1:1 + IMG, 1:1 + IMG],
                                 A["x"][2 * h + s]).then_inc(loaded, 16)
            sp.wait_ge(loaded, 64)
            for h in range(2):
                sp.dma_start(A["xpad"][2 * h:2 * h + 2].rearrange("b c n -> (b c) n"),
                             img[:, h, :, :].rearrange("p a b -> p (a b)")).then_inc(stored, 16)
            sp.wait_ge(stored, 32)


def tokenize(nc, sems, A):
    NT = 5
    with ExitStack() as ctx:
        m = Place(nc, "tok", ctx, sems)
        w1, w3 = m.sb("w1", [128, NT, C]), m.sb("w3", [128, NT, 128])
        w2, b2 = m.sb("w2", [C, NT * 128]), m.sb("b2", [128, NT])
        b1, b3 = m.sb("b1", [C, 1]), m.sb("b3", [C, 1])
        left, right = m.sb("left", [128, 2, 10 * PW]), m.sb("right", [128, 2, 10 * PW])
        h1 = m.sb("h1", [C, 2, CH])
        gate, gated = m.sb("gate", [128, 2, CH]), m.sb("gated", [128, 2, CH])
        h0 = m.sb("h0", [C, 2, CH])
        psH = [m.bank(f"psH{i}") for i in range(2)]
        psS = [m.bank(f"psS{i}") for i in range(2)]
        psO = [m.bank(f"psO{i}") for i in range(2)]
        w_in = m.sem("w_in")
        patches_in = [m.sem(f"patches_in{p}") for p in range(2)]
        h0_out = [m.sem(f"h0_out{p}") for p in range(2)]
        hidden_mm, hidden, score_mm = m.done("hidden_mm"), m.done("hidden"), m.done("score_mm")
        gates, prods, out_mm, h0_done = m.done("gates"), m.done("prods"), m.done("out_mm", 2 * NT), m.done("h0_done")
        block = ctx.enter_context(nc.Block())
        rows = [128] * 4 + [64]

        def patch(p, k):
            src, off = (left, k * PW) if k < 3 else (right, 0 if k == 3 else 2 * PW)
            v = src[0:rows[k], p, off:off + ROWS * PW]
            return v.rearrange("c (r w) -> c r w", w=PW)[:, :, 0:IMG]

        @block.sync
        def _(sp):
            for k in range(NT):
                r = slice(128 * k, 128 * k + rows[k])
                sp.dma_start(w1[0:rows[k], k, :], A["tok_W1"][r, :]).then_inc(w_in, 16)
                sp.dma_start(w3[0:rows[k], k, :], A["tok_W3"][r, :]).then_inc(w_in, 16)
                sp.dma_start(b2[0:rows[k], k:k + 1], A["tok_b2"][r, :]).then_inc(w_in, 16)
            sp.dma_start(w2[:], A["tok_W2"]).then_inc(w_in, 16)
            sp.dma_start(b1[:], A["tok_b1"]).then_inc(w_in, 16)
            sp.dma_start(b3[:], A["tok_b3"]).then_inc(w_in, 16)
            for it, half, j in pairs(sp):
                for p in range(2):
                    n = it * 2 + p
                    out_mm.wait_free(sp, n * NT + (NT - 1), 2 * NT)
                    base = j * (ROWS * PW)
                    img = A["xpad"].rearrange("b c n -> c b n")
                    for tile, lo, off, ln in ((left, 0, 0, 580), (left, 64, 1, 579),
                                              (right, 0, 2, 578), (right, 64, PW + 2, 520)):
                        sp.dma_start(tile[lo:lo + 64, p, 0:ln],
                                     img[:, half * 2 + p, bass.ds(base + off, ln)]).then_inc(patches_in[p], 16)

        @block.tensor
        def _(pe):
            for d in (hidden_mm, score_mm, out_mm):
                d.start(pe)
            pe.wait_ge(w_in, 16 * 18)
            for it, half, j in pairs(pe):
                for p in range(2):
                    n = it * 2 + p
                    pe.wait_ge(patches_in[p], it * 64 + 64)
                    hidden.wait_free(pe, n)
                    for k in range(NT):
                        mm = pe.matmul(psH[p][0:C, 0:CH], w1[0:rows[k], k, :], patch(p, k),
                                       start=k == 0, stop=k == NT - 1)
                    mm.then_inc(hidden_mm.sem, 1)
                    hidden.wait(pe, n)
                    h0_done.wait_free(pe, n)
                    for k in range(NT + 1):
                        if k < NT:
                            q = n * NT + k
                            s = (p * NT + k) % 2
                            gates.wait_free(pe, q)
                            pe.matmul(psS[s][:, 0:CH], w2[:, 128 * k:128 * k + 128], h1[:, p, :],
                                      start=True, stop=True).then_inc(score_mm.sem, 1)
                        if k:
                            q = n * NT + (k - 1)
                            s = (p * NT + k - 1) % 2
                            prods.wait(pe, q)
                            pe.matmul(psO[p][:, 0:CH], w3[0:rows[k - 1], k - 1, :], gated[0:rows[k - 1], s, :],
                                      start=k == 1, stop=k == NT).then_inc(out_mm.sem, 1)

        @block.scalar
        def _(act):
            for d in (hidden, gates, h0_done):
                d.start(act)
            act.preload_act_table_set("sigmoid_and_others")
            act.wait_ge(w_in, 16 * 18)
            for it, half, j in pairs(act):
                for p in range(2):
                    n = it * 2 + p
                    hidden_mm.wait(act, n)
                    act.activation(h1[:, p, :], psH[p][0:C, 0:CH], ACT.Relu, bias=b1[:]).then_inc(hidden.sem, 1)
                    for k in range(NT):
                        q = n * NT + k
                        s = (p * NT + k) % 2
                        score_mm.wait(act, q)
                        prods.wait_free(act, q)
                        act.activation(gate[0:rows[k], s, :], psS[s][0:rows[k], 0:CH], ACT.Sigmoid,
                                       bias=b2[0:rows[k], k:k + 1]).then_inc(gates.sem, 1)
                    out_mm.wait(act, n * NT + (NT - 1))
                    act.wait_ge(h0_out[p], it * 16)
                    act.activation(h0[:, p, :], psO[p][0:C, 0:CH], ACT.Identity,
                                   bias=b3[:]).then_inc(h0_done.sem, 1)

        @block.vector
        def _(dve):
            prods.start(dve)
            for it, half, j in pairs(dve):
                for p in range(2):
                    n = it * 2 + p
                    dve.wait_ge(patches_in[p], it * 64 + 64)
                    for k in range(NT):
                        q = n * NT + k
                        s = (p * NT + k) % 2
                        gates.wait(dve, q)
                        out_mm.wait_free(dve, q, 2)
                        r = rows[k]
                        dve.tensor_tensor(gated[0:r, s, :].rearrange("c (r w) -> c r w", w=IMG), patch(p, k),
                                          gate[0:r, s, :].rearrange("c (r w) -> c r w", w=IMG),
                                          ALU.mult).then_inc(prods.sem, 1)

        @block.gpsimd
        def _(pool):
            for it, half, j in pairs(pool):
                for p in range(2):
                    h0_done.wait(pool, it * 2 + p)
                    pool.dma_start(A["h0"][:, bass.ds((half * 2 + p) * L + j * CH, CH)],
                                   h0[:, p, :]).then_inc(h0_out[p], 16)
            for p in range(2):
                pool.wait_ge(h0_out[p], 16 * 2 * NJ)


def layer_norm(nc, sems, A, name, src, dst, affine=None, pad=0):
    with ExitStack() as ctx:
        m = Place(nc, name, ctx, sems)
        center, mean = m.sb("center", [128, 128]), m.sb("mean", [128, 128])
        eps, gb, zero = m.sb("eps", [128, 1]), m.sb("gb", [128, 2]), m.sb("zero", [C, 2])
        x, sq, y = m.sb("x", [128, 2, CH]), m.sb("sq", [128, 2, CH]), m.sb("y", [128, 2, CH])
        std, rstd, nrm = m.sb("std", [128, 2, CH]), m.sb("rstd", [128, 2, CH]), m.sb("nrm", [128, 2, CH])
        ps_cen = [m.bank(f"ps_cen{p}") for p in range(2)]
        ps_var = [m.bank(f"ps_var{p}") for p in range(2)]
        w_in, ready = m.sem("w_in"), m.sem("ready")
        x_in = [m.sem(f"x_in{p}") for p in range(2)]
        y_out = [m.sem(f"y_out{p}") for p in range(2)]
        cen_mm, var_mm, squares, stds = m.done("cen_mm"), m.done("var_mm"), m.done("squares"), m.done("stds")
        y_done, steps = m.done("y_done"), m.sem("steps")
        block = ctx.enter_context(nc.Block())
        n_w = 3 if affine is None else 7
        span = L + 2 * pad

        @block.sync
        def _(sp):
            sp.dma_start(center[:], A["c_center"]).then_inc(w_in, 16)
            sp.dma_start(mean[:], A["c_mean"]).then_inc(w_in, 16)
            sp.dma_start(eps[:], A["c_eps"]).then_inc(w_in, 16)
            if affine is not None:
                for i, a in enumerate(affine):
                    for s in range(2):
                        sp.dma_start(gb[C * s:C * s + C, i:i + 1], A[a]).then_inc(w_in, 16)
            with sp.Fori(0, NJ) as j:
                for p in range(2):
                    cen_mm.wait_free(sp, j * 2 + p)
                    for s in range(2):
                        sp.dma_start(x[C * s:C * s + C, p, :],
                                     A[src][:, bass.ds(j * CH + (2 * s + p) * L, CH)]).then_inc(x_in[p], 16)

        @block.tensor
        def _(pe):
            cen_mm.start(pe)
            var_mm.start(pe)
            pe.wait_ge(w_in, 16 * n_w)
            with pe.Fori(0, NJ) as j:
                for p in range(2):
                    pe.wait_ge(x_in[p], j * 32 + 32)
                    y_done.wait_free(pe, j * 2 + p)
                    pe.matmul(ps_cen[p][:, 0:CH], center[:], x[:, p, :], start=True,
                              stop=True).then_inc(cen_mm.sem, 1)
                for p in range(2):
                    squares.wait(pe, j * 2 + p)
                    stds.wait_free(pe, j * 2 + p)
                    pe.matmul(ps_var[p][:, 0:CH], mean[:], sq[:, p, :], start=True,
                              stop=True).then_inc(var_mm.sem, 1)

        @block.scalar
        def _(act):
            squares.start(act)
            stds.start(act)
            act.preload_act_table_set("sqrt_and_others")
            act.wait_ge(w_in, 16 * n_w)
            with act.Fori(0, NJ) as j:
                for p in range(2):
                    cen_mm.wait(act, j * 2 + p)
                    var_mm.wait_free(act, j * 2 + p)
                    act.activation(sq[:, p, :], ps_cen[p][:, 0:CH], ACT.Square).then_inc(squares.sem, 1)
                for p in range(2):
                    var_mm.wait(act, j * 2 + p)
                    y_done.wait_free(act, j * 2 + p)
                    act.activation(std[:, p, :], ps_var[p][:, 0:CH], ACT.Sqrt, bias=eps[:]).then_inc(stds.sem, 1)

        @block.vector
        def _(dve):
            y_done.start(dve)
            if pad:
                dve.memset(zero[:], 0.0).then_inc(ready, 1)
            dve.wait_ge(w_in, 16 * n_w)
            per = 2 if affine is None else 4
            order = Order(dve, steps, per)
            with dve.Fori(0, NJ) as j:
                order.at(j)
                for p in range(2):
                    squares.wait(dve, j * 2 + p)
                    stds.wait(dve, j * 2 + p)
                    order(dve.reciprocal(rstd[:, p, :], std[:, p, :]))
                    dve.wait_ge(y_out[p], j * 32)
                    if affine is None:
                        dve.tensor_tensor(y[:, p, :], ps_cen[p][:, 0:CH], rstd[:, p, :],
                                          ALU.mult).then_inc(y_done.sem, 1)
                    else:
                        order(dve.tensor_tensor(nrm[:, p, :], ps_cen[p][:, 0:CH], rstd[:, p, :], ALU.mult))
                        dve.tensor_scalar(y[:, p, :], nrm[:, p, :], gb[:, 0:1], gb[:, 1:2], ALU.mult,
                                          ALU.add).then_inc(y_done.sem, 1)

        @block.gpsimd
        def _(pool):
            padded = m.sem("padded")
            if pad:
                pool.wait_ge(ready, 1)
                for b in range(B):
                    for at in (b * span, b * span + pad + L):
                        pool.dma_start(A[dst][:, at:at + pad], zero[:, 0:pad],).then_inc(padded, 16)
                pool.wait_ge(padded, 16 * 2 * B)
            with pool.Fori(0, NJ) as j:
                for p in range(2):
                    y_done.wait(pool, j * 2 + p)
                    for s in range(2):
                        pool.dma_start(A[dst][:, bass.ds(j * CH + (2 * s + p) * span + pad, CH)],
                                       y[C * s:C * s + C, p, :]).then_inc(y_out[p], 16)
            for p in range(2):
                pool.wait_ge(y_out[p], 32 * NJ)
def in_projection(nc, sems, A):
    with ExitStack() as ctx:
        m = Place(nc, "inp", ctx, sems)
        cw, cb = m.sb("cw", [C, 3]), m.sb("cb", [C, 1])
        w_in_proj = m.sb("w_in_proj", [C, 2 * E])
        sw, sbias = m.sb("sw", [E, 4]), m.sb("sbias", [E, 1])
        w_b, w_c = m.sb("w_b", [E, 128]), m.sb("w_c", [E, 128])
        w_dtr, w_dt, dt_b = m.sb("w_dtr", [E, DT_RANK]), m.sb("w_dt", [DT_RANK, E]), m.sb("dt_b", [E, 1])
        win = m.sb("win", [C, 2, CH + 2])
        acc = m.sb("acc", [C, 2, CH])
        hc = m.sb("hc", [C, 2, CH])
        xin = m.sb("xin", [E, B, CH + 3])
        cacc = m.sb("cacc", [E, 2, CH])
        u, sz = m.sb("u", [E, 2, CH]), m.sb("sz", [E, 2, CH])
        bb, cc = m.sb("bb", [128, 2, CH]), m.sb("cc", [128, 2, CH])
        dtr, dtp = m.sb("dtr", [DT_RANK, 2, CH]), m.sb("dtp", [E, 2, CH])
        ps_x = [m.bank(f"ps_x{p}") for p in range(2)]
        ps_z = [m.bank(f"ps_z{p}") for p in range(2)]
        ps_b, ps_c, ps_r, ps_d = m.bank("ps_b"), m.bank("ps_c"), m.bank("ps_r"), m.bank("ps_d")
        w_in = m.sem("w_in")
        win_in = [m.sem(f"win_in{p}") for p in range(2)]
        out = [m.sem(f"out{p}") for p in range(2)]
        hc_done, xz_mm, x_read, u_done = m.done("hc_done"), m.done("xz_mm"), m.done("x_read"), m.done("u_done")
        conv_done, z_done = m.done("conv_done"), m.done("z_done")
        bcr_mm, bc_done, dtr_done, dt_mm, dt_done = (m.done("bcr_mm"), m.done("bc_done"), m.done("dtr_done"),
                                                     m.done("dt_mm"), m.done("dt_done"))
        dve_steps, cleared = m.sem("dve_steps"), m.sem("cleared")
        block = ctx.enter_context(nc.Block())
        weights = [(cw, "conv_w"), (cb, "conv_b"), (w_in_proj, "in_proj_w"), (sw, "ssm_conv_w"),
                   (sbias, "ssm_conv_b"), (w_b, "xp_b"), (w_c, "xp_c"), (w_dtr, "xp_dt"),
                   (w_dt, "dt_proj_w"), (dt_b, "dt_proj_b")]
        NW = 16 * len(weights)

        @block.sync
        def _(sp):
            for t, a in weights:
                sp.dma_start(t[:], A[a]).then_inc(w_in, 16)
            with sp.Fori(0, NJ) as j:
                for b in range(B):
                    hc_done.wait_free(sp, j * B + b)
                    sp.dma_start(win[:, b % 2, :],
                                 A["hn"][:, bass.ds(j * CH + b * (L + 4) + 1, CH + 2)]).then_inc(win_in[b % 2], 16)

        @block.vector
        def _(dve):
            for d in (hc_done, x_read, conv_done):
                d.start(dve)
            dve.memset(xin[:, :, CH:CH + 3], 0.0).then_inc(cleared, 1)
            dve.wait_ge(cleared, 1)
            dve.wait_ge(w_in, NW)
            order = Order(dve, dve_steps, 7 * B)
            with dve.Fori(0, NJ) as j:
                order.at(j)
                for b in range(B):
                    p, n = b % 2, j * B + b
                    dve.wait_ge(win_in[p], j * 32 + 16 * (b // 2 + 1))
                    a = acc[:, p, :]
                    order(dve.tensor_scalar(a, win[:, p, 0:CH], cw[:, 0:1], cb[:, 0:1], ALU.mult, ALU.add))
                    order(dve.scalar_tensor_tensor(a, win[:, p, 1:CH + 1], cw[:, 1:2], a, ALU.mult, ALU.add))
                    order(dve.scalar_tensor_tensor(a, win[:, p, 2:CH + 2], cw[:, 2:3], a, ALU.mult, ALU.add))
                    xz_mm.wait_free(dve, n)
                    dve.tensor_tensor(hc[:, p, :], a, win[:, p, 1:CH + 1], ALU.add).then_inc(hc_done.sem, 1)
                    order(dve.tensor_copy(xin[:, b, 0:3], xin[:, b, CH:CH + 3]))
                    xz_mm.wait(dve, n)
                    dve.tensor_copy(xin[:, b, 3:CH + 3], ps_x[p][:, 0:CH]).then_inc(x_read.sem, 1)
                    x_read.wait(dve, n)
                    u_done.wait_free(dve, n)
                    a = cacc[:, p, :]
                    order(dve.tensor_scalar(a, xin[:, b, 0:CH], sw[:, 0:1], sbias[:], ALU.mult, ALU.add))
                    for k in (1, 2):
                        order(dve.scalar_tensor_tensor(a, xin[:, b, k:CH + k], sw[:, k:k + 1], a,
                                                       ALU.mult, ALU.add))
                    dve.scalar_tensor_tensor(a, xin[:, b, 3:CH + 3], sw[:, 3:4], a, ALU.mult,
                                             ALU.add).then_inc(conv_done.sem, 1)

        @block.tensor
        def _(pe):
            for d in (xz_mm, bcr_mm, dt_mm):
                d.start(pe)
            pe.wait_ge(w_in, NW)
            with pe.Fori(0, NJ) as j:
                for b in range(B):
                    p, n = b % 2, j * B + b
                    hc_done.wait(pe, n)
                    x_read.wait_free(pe, n)
                    z_done.wait_free(pe, n)
                    pe.matmul(ps_x[p][:, 0:CH], w_in_proj[:, 0:E], hc[:, p, :], start=True, stop=True)
                    pe.matmul(ps_z[p][:, 0:CH], w_in_proj[:, E:2 * E], hc[:, p, :], start=True,
                              stop=True).then_inc(xz_mm.sem, 1)
                    u_done.wait(pe, n)
                    bc_done.wait_free(pe, n, 1)
                    dtr_done.wait_free(pe, n, 1)
                    pe.matmul(ps_b[:, 0:CH], w_b[:], u[:, p, :], start=True, stop=True)
                    pe.matmul(ps_c[:, 0:CH], w_c[:], u[:, p, :], start=True, stop=True)
                    pe.matmul(ps_r[0:DT_RANK, 0:CH], w_dtr[:], u[:, p, :], start=True,
                              stop=True).then_inc(bcr_mm.sem, 1)
                    dtr_done.wait(pe, n)
                    dt_done.wait_free(pe, n, 1)
                    pe.matmul(ps_d[:, 0:CH], w_dt[:], dtr[:, p, :], start=True, stop=True).then_inc(dt_mm.sem, 1)

        @block.scalar
        def _(act):
            for d in (u_done, z_done, bc_done, dtr_done, dt_done):
                d.start(act)
            act.preload_act_table_set("silu_and_others")
            act.wait_ge(w_in, NW)
            with act.Fori(0, NJ) as j:
                for b in range(B):
                    p, n = b % 2, j * B + b
                    stored = 80 * (j * 2 + b // 2)
                    xz_mm.wait(act, n)
                    act.wait_ge(out[p], stored)
                    act.activation(sz[:, p, :], ps_z[p][:, 0:CH], ACT.Silu).then_inc(z_done.sem, 1)
                    conv_done.wait(act, n)
                    act.activation(u[:, p, :], cacc[:, p, :], ACT.Silu).then_inc(u_done.sem, 1)
                    bcr_mm.wait(act, n)
                    act.activation(dtr[:, p, :], ps_r[0:DT_RANK, 0:CH], ACT.Copy).then_inc(dtr_done.sem, 1)
                    act.activation(bb[:, p, :], ps_b[:, 0:CH], ACT.Copy)
                    act.activation(cc[:, p, :], ps_c[:, 0:CH], ACT.Copy).then_inc(bc_done.sem, 1)
                    dt_mm.wait(act, n)
                    act.activation(dtp[:, p, :], ps_d[:, 0:CH], ACT.Identity, bias=dt_b[:]).then_inc(dt_done.sem, 1)

        @block.gpsimd
        def _(pool):
            with pool.Fori(0, NJ) as j:
                for b in range(B):
                    p, n = b % 2, j * B + b
                    cols = bass.ds(j * CH + b * L, CH)
                    dt_done.wait(pool, n)
                    for t, a in ((sz, "sz"), (u, "u"), (bb, "Bn"), (cc, "Cn"), (dtp, "dtp")):
                        pool.dma_start(A[a][:, cols], t[:, p, :]).then_inc(out[p], 16)
            for p in range(2):
                pool.wait_ge(out[p], 80 * 2 * NJ)


def step_sizes(nc, sems, A):
    with ExitStack() as ctx:
        m = Place(nc, "dts", ctx, sems)
        x, u = m.sb("x", [E, 2, CH]), m.sb("u", [E, 2, CH])
        e, w, lw = m.sb("e", [E, 2, CH]), m.sb("w", [E, 2, CH]), m.sb("lw", [E, 2, CH])
        one, den = m.sb("one", [E, CH]), m.sb("den", [E, CH])
        val = m.sb("val", [E, 2, CH])
        rest = m.sb("rest", [E, 2, CH])
        parts = m.sb("parts", [E, 2, 2, 3, CH], BF16)
        x_in = [m.sem(f"x_in{p}") for p in range(2)]
        out = [m.sem(f"out{p}") for p in range(2)]
        e_done, w_done, l_done, all_done = m.done("e_done"), m.done("w_done"), m.done("l_done"), m.done("all_done")
        act_steps, dve_steps = m.sem("act_steps"), m.sem("dve_steps")
        block = ctx.enter_context(nc.Block())

        @block.sync
        def _(sp):
            with sp.Fori(0, T // CH // 2) as k:
                for p in range(2):
                    all_done.wait_free(sp, k * 2 + p)
                    for t, a in ((x, "dtp"), (u, "u")):
                        sp.dma_start(t[:, p, :], A[a][:, bass.ds(k * (2 * CH) + p * CH, CH)]).then_inc(x_in[p], 16)

        @block.scalar
        def _(act):
            e_done.start(act)
            l_done.start(act)
            act.preload_act_table_set("natural_log_exp_and_others")
            order = Order(act, act_steps, 2)
            with act.Fori(0, T // CH // 2) as k:
                order.at(k)
                for p in range(2):
                    act.wait_ge(x_in[p], k * 32 + 32)
                    all_done.wait_free(act, k * 2 + p)
                    order(act.activation(e[:, p, :], x[:, p, :], ACT.Abs))
                    act.activation(e[:, p, :], e[:, p, :], ACT.Exp, scale=-1.0).then_inc(e_done.sem, 1)
                for p in range(2):
                    w_done.wait(act, k * 2 + p)
                    act.activation(lw[:, p, :], w[:, p, :], ACT.Ln).then_inc(l_done.sem, 1)

        @block.vector
        def _(dve):
            w_done.start(dve)
            all_done.start(dve)
            order = Order(dve, dve_steps, 22)
            with dve.Fori(0, T // CH // 2) as k:
                order.at(k)
                for p in range(2):
                    e_done.wait(dve, k * 2 + p)
                    dve.tensor_scalar(w[:, p, :], e[:, p, :], 1.0, None, ALU.add).then_inc(w_done.sem, 1)
                for p in range(2):
                    w_done.wait(dve, k * 2 + p)
                    order(dve.tensor_scalar(one[:], w[:, p, :], 1.0, None, ALU.is_equal))
                    order(dve.scalar_tensor_tensor(den[:], w[:, p, :], -1.0, one[:], ALU.add, ALU.add))
                    order(dve.reciprocal(den[:], den[:]))
                    l_done.wait(dve, k * 2 + p)
                    order(dve.tensor_tensor(one[:], lw[:, p, :], one[:], ALU.add))
                    order(dve.tensor_tensor(one[:], one[:], den[:], ALU.mult))
                    order(dve.tensor_tensor(one[:], one[:], e[:, p, :], ALU.mult))
                    order(dve.scalar_tensor_tensor(val[:, 0, :], x[:, p, :], 0.0, one[:], ALU.max, ALU.add))
                    order(dve.tensor_tensor(val[:, 1, :], val[:, 0, :], u[:, p, :], ALU.mult))
                    dve.wait_ge(out[p], k * 96)
                    order(dve.tensor_copy(parts[:, p, :, 0, :], val[:]))
                    order(dve.tensor_tensor(rest[:], val[:], parts[:, p, :, 0, :], ALU.subtract))
                    order(dve.tensor_copy(parts[:, p, :, 1, :], rest[:]))
                    dve.tensor_tensor(parts[:, p, :, 2, :], rest[:], parts[:, p, :, 1, :],
                                      ALU.subtract).then_inc(all_done.sem, 1)

        @block.gpsimd
        def _(pool):
            with pool.Fori(0, T // CH // 2) as k:
                for p in range(2):
                    all_done.wait(pool, k * 2 + p)
                    for v, a in enumerate(("dt_parts", "du_parts")):
                        for i in range(3):
                            pool.dma_start(A[a][i][:, bass.ds(k * (2 * CH) + p * CH, CH)],
                                           parts[:, p, v, i, :]).then_inc(out[p], 16)
            for p in range(2):
                pool.wait_ge(out[p], 96 * (T // CH // 2))


def selective_scan(nc, sems, A):
    G = E // DT_RANK
    order_of = [8 * (i % 4) + i // 4 for i in range(G)]
    with ExitStack() as ctx:
        m = Place(nc, "scan", ctx, sems)
        sel = m.sb("sel", [96, 8, 128], BF16)
        ysel = m.sb("ysel", [128, 8, 32])
        a_neg, dp = m.sb("a_neg", [128, G]), m.sb("dp", [E, 1])
        dtq, duq = m.sb("dtq", [96, 2, 4, CH], BF16), m.sb("duq", [96, 2, 4, CH], BF16)
        bn, cn = m.sb("bn", [128, 2, CH]), m.sb("cn", [128, 2, CH])
        u, sz = m.sb("u", [E, 2, CH]), m.sb("sz", [E, 2, CH])
        last = m.sb("last", [128, B * G])
        decay = m.sb("decay", [128, 4, CH])
        drive = m.sb("drive", [128, 4, CH])
        h = m.sb("h", [128, 4, CH])
        ch = m.sb("ch", [128, 4, CH])
        y1, yz = m.sb("y1", [E, 2, CH]), m.sb("yz", [E, 2, CH])
        ps_dt = [m.bank(f"ps_dt{i}") for i in range(2)]
        ps_du = [m.bank(f"ps_du{i}") for i in range(4)]
        ps_y = [m.bank(f"ps_y{i}") for i in range(2)]
        w_in, a_ready, cleared = m.sem("w_in"), m.sem("a_ready"), m.sem("cleared")
        c_in = [m.sem(f"c_in{p}") for p in range(2)]
        out = [m.sem(f"out{p}") for p in range(2)]
        spread, driven, decays = m.done("spread"), m.done("driven", 4), m.done("decays")
        scans, weighted, y_mm = m.done("scans", 4), m.done("weighted", 4), m.done("y_mm", 4)
        kept = m.done("kept", B * G)
        y_done, steps = m.done("y_done"), m.sem("steps")
        block = ctx.enter_context(nc.Block())

        @block.sync
        def _(sp):
            for t, a in ((sel, "c_sel"), (ysel, "c_ysel"), (a_neg, "A_log"), (dp, "Dp")):
                sp.dma_start(t[:], A[a]).then_inc(w_in, 16)
            with sp.Fori(0, NJ) as j:
                for b in range(B):
                    p, n = b % 2, j * B + b
                    cols = bass.ds(j * CH + b * L, CH)
                    y_done.wait_free(sp, n)
                    for i in range(3):
                        for t, a in ((dtq, "dt_parts"), (duq, "du_parts")):
                            sp.dma_start(t[32 * i:32 * i + 32, p, :, :],
                                         A[a][i].rearrange("(q r) t -> r q t", r=32)[:, :, cols]).then_inc(c_in[p], 16)
                    for t, a in ((bn, "Bn"), (cn, "Cn"), (u, "u"), (sz, "sz")):
                        sp.dma_start(t[:, p, :], A[a][:, cols]).then_inc(c_in[p], 16)

        @block.tensor
        def _(pe):
            spread.start(pe)
            y_mm.start(pe)
            pe.wait_ge(w_in, 64)
            with pe.Fori(0, NJ) as j:
                for b in range(B):
                    p, n = b % 2, j * B + b
                    pe.wait_ge(c_in[p], (j * 2 + b // 2 + 1) * 160)
                    y_done.wait_free(pe, n)
                    for i in range(G + 3):
                        if i < G:
                            s = n * G + i
                            g = order_of[i]
                            decays.wait_free(pe, s)
                            driven.wait_free(pe, s)
                            pe.matmul(ps_dt[i % 2][:, 0:CH], sel[:, g % 8, :], dtq[:, p, g // 8, :],
                                      start=True, stop=True)
                            pe.matmul(ps_du[i % 4][:, 0:CH], sel[:, g % 8, :], duq[:, p, g // 8, :],
                                      start=True, stop=True).then_inc(spread.sem, 1)
                        if i >= 3:
                            s, i2 = n * G + (i - 3), i - 3
                            g = order_of[i2]
                            q, r = g // 8, g % 8
                            weighted.wait(pe, s)
                            pe.matmul(ps_y[p][32 * q:32 * q + 32, 0:CH], ysel[:, r, :], ch[:, i2 % 4, :],
                                      start=r == 0, stop=r == 7, tile_position=(0, 32 * q)).then_inc(y_mm.sem, 1)

        @block.scalar
        def _(act):
            decays.start(act)
            act.preload_act_table_set("natural_log_exp_and_others")
            act.wait_ge(w_in, 64)
            act.activation(a_neg[:], a_neg[:], ACT.Exp).then_inc(a_ready, 1)
            act.wait_ge(a_ready, 1)
            act.mul(a_neg[:], a_neg[:], -1.0).then_inc(a_ready, 1)
            act.wait_ge(a_ready, 2)
            act.wait_ge(cleared, 1)
            kept.start(act)
            with act.Fori(0, NJ) as j:
                for b in range(B):
                    n = j * B + b
                    for i in range(G + 2):
                        if i < G:
                            s = n * G + i
                            g = order_of[i]
                            spread.wait(act, s)
                            scans.wait_free(act, s, 4)
                            act.activation(decay[:, i % 4, :], ps_dt[i % 2][:, 0:CH], ACT.Exp,
                                           scale=a_neg[:, g:g + 1]).then_inc(decays.sem, 1)
                        if i >= 2:
                            scans.wait(act, n * G + (i - 2))
                            act.activation(last[:, b * G + i - 2:b * G + i - 1], h[:, (i - 2) % 4, CH - 1:CH],
                                           ACT.Copy).then_inc(kept.sem, 1)

        @block.vector
        def _(dve):
            for d in (driven, scans, y_done):
                d.start(dve)
            dve.memset(last[:], 0.0).then_inc(cleared, 1)
            dve.wait_ge(w_in, 64)
            order = Order(dve, steps, B)
            with dve.Fori(0, NJ) as j:
                order.at(j)
                for b in range(B):
                    p, n = b % 2, j * B + b
                    dve.wait_ge(c_in[p], (j * 2 + b // 2 + 1) * 160)
                    for i in range(G + 1):
                        if i < G:
                            s = n * G + i
                            spread.wait(dve, s)
                            scans.wait_free(dve, s, 4)
                            dve.tensor_tensor(drive[:, i % 4, :], ps_du[i % 4][:, 0:CH], bn[:, p, :],
                                              ALU.mult).then_inc(driven.sem, 1)
                        if i >= 1:
                            i2 = i - 1
                            s = n * G + i2
                            driven.wait(dve, s)
                            decays.wait(dve, s)
                            kept.wait_free(dve, s, B * G)
                            weighted.wait_free(dve, s, 4)
                            dve.tensor_tensor_scan(h[:, i2 % 4, :], decay[:, i2 % 4, :], drive[:, i2 % 4, :],
                                                   last[:, b * G + i2:b * G + i2 + 1], ALU.mult,
                                                   ALU.add).then_inc(scans.sem, 1)
                    y_mm.wait(dve, n * G + (G - 1))
                    order(dve.scalar_tensor_tensor(y1[:, p, :], u[:, p, :], dp[:], ps_y[p][:, 0:CH],
                                                   ALU.mult, ALU.add))
                    dve.wait_ge(out[p], (j * 2 + b // 2) * 16)
                    dve.tensor_tensor(yz[:, p, :], y1[:, p, :], sz[:, p, :], ALU.mult).then_inc(y_done.sem, 1)

        @block.gpsimd
        def _(pool):
            weighted.start(pool)
            with pool.Fori(0, NJ) as j:
                for b in range(B):
                    p, n = b % 2, j * B + b
                    for i in range(G):
                        s = n * G + i
                        scans.wait(pool, s)
                        y_mm.wait_free(pool, s, 4)
                        pool.tensor_tensor(ch[:, i % 4, :], h[:, i % 4, :], cn[:, p, :],
                                           ALU.mult).then_inc(weighted.sem, 1)
                    y_done.wait(pool, n)
                    pool.dma_start(A["yz"][:, bass.ds(j * CH + b * L, CH)], yz[:, p, :]).then_inc(out[p], 16)
            for p in range(2):
                pool.wait_ge(out[p], 16 * 2 * NJ)
def out_projection(nc, sems, A):
    with ExitStack() as ctx:
        m = Place(nc, "outp", ctx, sems)
        w = m.sb("w", [E, C])
        yz, h0, h1 = m.sb("yz", [E, 2, CH]), m.sb("h0", [C, 2, CH]), m.sb("h1", [C, 2, CH])
        ps = [m.bank(f"ps{p}") for p in range(2)]
        w_in = m.sem("w_in")
        x_in = [m.sem(f"x_in{p}") for p in range(2)]
        out = [m.sem(f"out{p}") for p in range(2)]
        mm, added = m.done("mm"), m.done("added")
        block = ctx.enter_context(nc.Block())

        @block.sync
        def _(sp):
            sp.dma_start(w[:], A["out_proj_w"]).then_inc(w_in, 16)
            with sp.Fori(0, T // CH // 2) as k:
                for p in range(2):
                    added.wait_free(sp, k * 2 + p)
                    for t, a in ((yz, "yz"), (h0, "h0")):
                        sp.dma_start(t[:, p, :], A[a][:, bass.ds(k * (2 * CH) + p * CH, CH)]).then_inc(x_in[p], 16)

        @block.tensor
        def _(pe):
            mm.start(pe)
            pe.wait_ge(w_in, 16)
            with pe.Fori(0, T // CH // 2) as k:
                for p in range(2):
                    pe.wait_ge(x_in[p], k * 32 + 32)
                    added.wait_free(pe, k * 2 + p)
                    pe.matmul(ps[p][0:C, 0:CH], w[:], yz[:, p, :], start=True, stop=True).then_inc(mm.sem, 1)

        @block.vector
        def _(dve):
            added.start(dve)
            with dve.Fori(0, T // CH // 2) as k:
                for p in range(2):
                    dve.wait_ge(x_in[p], k * 32 + 32)
                    dve.wait_ge(out[p], k * 16)
                    mm.wait(dve, k * 2 + p)
                    dve.tensor_tensor(h1[:, p, :], ps[p][0:C, 0:CH], h0[:, p, :], ALU.add).then_inc(added.sem, 1)

        @block.gpsimd
        def _(pool):
            with pool.Fori(0, T // CH // 2) as k:
                for p in range(2):
                    added.wait(pool, k * 2 + p)
                    pool.dma_start(A["h1"][:, bass.ds(k * (2 * CH) + p * CH, CH)], h1[:, p, :]).then_inc(out[p], 16)
            for p in range(2):
                pool.wait_ge(out[p], 16 * (T // CH // 2))


def mlp(nc, sems, A, name, src, adds, dst, weights, func, table, gate=None):
    NA = len(adds)
    with ExitStack() as ctx:
        m = Place(nc, name, ctx, sems)
        w1, w2 = m.sb("w1", [C, HID]), m.sb("w2", [128, 2, C])
        b1, b2 = m.sb("b1", [128, 2]), m.sb("b2", [C, 1])
        ones = m.sb("ones", [1, C])
        x, more = m.sb("x", [C, 2, CH]), m.sb("more", [C, 2, NA, CH])
        g, gs = m.sb("g", [1, 2, CH]), m.sb("gs", [C, 2, CH])
        hid = m.sb("hid", [128, 2, 2, CH])
        y1, y2 = m.sb("y1", [C, 2, CH]), m.sb("y2", [C, 2, CH])
        ps_h = [[m.bank(f"ps_h{p}{i}") for i in range(2)] for p in range(2)]
        ps_y = [m.bank(f"ps_y{p}") for p in range(2)]
        ps_g = m.bank("ps_g")
        w_in, filled = m.sem("w_in"), m.sem("filled")
        x_in = [m.sem(f"x_in{p}") for p in range(2)]
        out = [m.sem(f"out{p}") for p in range(2)]
        hid_mm, hidden, y_mm, y_done = m.done("hid_mm"), m.done("hidden"), m.done("y_mm"), m.done("y_done")
        gate_mm, gates, steps = m.done("gate_mm"), m.done("gates"), m.sem("steps")
        block = ctx.enter_context(nc.Block())
        n_in = 16 * (1 + NA + (gate is not None))
        K = T // CH // 2

        @block.sync
        def _(sp):
            for t, a in ((w1, weights[0]), (b2, weights[3])):
                sp.dma_start(t[:], A[a]).then_inc(w_in, 16)
            for i in range(2):
                sp.dma_start(b1[:, i:i + 1], A[weights[1]][128 * i:128 * i + 128, :]).then_inc(w_in, 16)
                sp.dma_start(w2[:, i, :], A[weights[2]][128 * i:128 * i + 128, :]).then_inc(w_in, 16)
            with sp.Fori(0, K) as k:
                for p in range(2):
                    cols = bass.ds(k * (2 * CH) + p * CH, CH)
                    y_done.wait_free(sp, k * 2 + p)
                    sp.dma_start(x[:, p, :], A[src][:, cols]).then_inc(x_in[p], 16)
                    for i, a in enumerate(adds):
                        sp.dma_start(more[:, p, i, :], A[a][:, cols]).then_inc(x_in[p], 16)
                    if gate is not None:
                        sp.dma_start(g[:, p, :], A[gate][:, cols]).then_inc(x_in[p], 16)

        @block.tensor
        def _(pe):
            for d in (hid_mm, y_mm, gate_mm):
                d.start(pe)
            pe.wait_ge(w_in, 16 * 6)
            if gate is not None:
                pe.wait_ge(filled, 1)
            with pe.Fori(0, K) as k:
                for p in range(2):
                    n = k * 2 + p
                    pe.wait_ge(x_in[p], k * n_in + n_in)
                    hidden.wait_free(pe, n)
                    for i in range(2):
                        mm = pe.matmul(ps_h[p][i][:, 0:CH], w1[:, 128 * i:128 * i + 128], x[:, p, :],
                                       start=True, stop=True)
                    mm.then_inc(hid_mm.sem, 1)
                    if gate is not None:
                        gates.wait_free(pe, n, 1)
                        pe.matmul(ps_g[0:C, 0:CH], ones[:], g[:, p, :], start=True, stop=True).then_inc(gate_mm.sem, 1)
                for p in range(2):
                    n = k * 2 + p
                    hidden.wait(pe, n)
                    y_done.wait_free(pe, n)
                    for i in range(2):
                        mm = pe.matmul(ps_y[p][0:C, 0:CH], w2[:, i, :], hid[:, p, i, :], start=i == 0, stop=i == 1)
                    mm.then_inc(y_mm.sem, 1)

        @block.scalar
        def _(act):
            hidden.start(act)
            gates.start(act)
            act.preload_act_table_set(table)
            act.wait_ge(w_in, 16 * 6)
            with act.Fori(0, K) as k:
                for p in range(2):
                    n = k * 2 + p
                    hid_mm.wait(act, n)
                    y_mm.wait_free(act, n)
                    for i in range(2):
                        a = act.activation(hid[:, p, i, :], ps_h[p][i][:, 0:CH], func, bias=b1[:, i:i + 1])
                    a.then_inc(hidden.sem, 1)
                    if gate is not None:
                        gate_mm.wait(act, n)
                        y_done.wait_free(act, n)
                        act.activation(gs[:, p, :], ps_g[0:C, 0:CH], ACT.Copy).then_inc(gates.sem, 1)

        @block.vector
        def _(dve):
            y_done.start(dve)
            if gate is not None:
                dve.memset(ones[:], 1.0).then_inc(filled, 1)
            dve.wait_ge(w_in, 16 * 6)
            per = 1 + (gate is not None) + (NA - 1)
            order = Order(dve, steps, 2 * per)
            with dve.Fori(0, K) as k:
                order.at(k)
                for p in range(2):
                    n = k * 2 + p
                    y_mm.wait(dve, n)
                    order(dve.tensor_scalar(y1[:, p, :], ps_y[p][0:C, 0:CH], b2[:], None, ALU.add))
                    if gate is not None:
                        gates.wait(dve, n)
                        order(dve.tensor_tensor(y1[:, p, :], y1[:, p, :], gs[:, p, :], ALU.mult))
                    for i in range(NA - 1):
                        order(dve.tensor_tensor(y1[:, p, :], y1[:, p, :], more[:, p, i, :], ALU.add))
                    dve.wait_ge(out[p], k * 16)
                    dve.tensor_tensor(y2[:, p, :], y1[:, p, :], more[:, p, NA - 1, :], ALU.add).then_inc(y_done.sem, 1)

        @block.gpsimd
        def _(pool):
            with pool.Fori(0, K) as k:
                for p in range(2):
                    y_done.wait(pool, k * 2 + p)
                    pool.dma_start(A[dst][:, bass.ds(k * (2 * CH) + p * CH, CH)], y2[:, p, :]).then_inc(out[p], 16)
            for p in range(2):
                pool.wait_ge(out[p], 16 * K)


def experts(nc, sems, A):
    TT, NTT = 112, 4
    with ExitStack() as ctx:
        m = Place(nc, "moe", ctx, sems)
        w1, b1 = m.sb("w1", [C, HID]), m.sb("b1", [128, 2])
        wg, bg = m.sb("wg", [128, 2, N_EXP]), m.sb("bg", [1, N_EXP])
        wd, bd = m.sb("wd", [128, 2, N_EXP * C]), m.sb("bd", [1, N_EXP * C])
        ones, ident = m.sb("ones", [1, TT]), m.sb("ident", [128, 128])
        rank = m.sb("rank", [TT, NTT, N_EXP])
        x, hid = m.sb("x", [C, 2, CH]), m.sb("hid", [128, 2, 2, CH])
        mx, sh, ex = m.sb("mx", [TT, NTT]), m.sb("sh", [TT, NTT, N_EXP]), m.sb("ex", [TT, NTT, N_EXP])
        sm, pm, first = m.sb("sm", [TT, NTT]), m.sb("pm", [TT, NTT]), m.sb("first", [TT, NTT])
        eq, wt = m.sb("eq", [TT, NTT, N_EXP]), m.sb("wt", [TT, NTT, N_EXP])
        picked, o = m.sb("picked", [TT, 2, N_EXP, C]), m.sb("o", [TT, 2, NTT, C])
        t2 = m.sb("t2", [C, 2, CH])
        ps_h = [m.bank(f"ps_h{i}") for i in range(2)]
        ps_l, ps_t = m.bank("ps_l"), [m.bank(f"ps_t{i}") for i in range(2)]
        ps_y = [m.bank(f"ps_y{i}") for i in range(2)]
        w_in, filled = m.sem("w_in"), m.sem("filled")
        x_in = [m.sem(f"x_in{p}") for p in range(2)]
        out = [m.sem(f"out{p}") for p in range(2)]
        hid_mm, hidden, logit_mm, shifted, exps = (m.done("hid_mm"), m.done("hidden"), m.done("logit_mm"),
                                                   m.done("shifted"), m.done("exps"))
        y_mm, y_read, wt_done, reduced, o_mm, t2_done = (m.done("y_mm"), m.done("y_read"), m.done("wt_done"),
                                                         m.done("reduced"), m.done("o_mm"), m.done("t2_done"))
        steps = m.sem("steps")
        block = ctx.enter_context(nc.Block())
        K = T // CH // 2
        NW = 16 * 11

        def bcast(a):
            return a.unsqueeze(2).broadcast_to([TT, NTT, N_EXP])

        @block.sync
        def _(sp):
            for t, a in ((w1, "moe_W1"), (bg, "moe_bg"), (bd, "moe_bd"), (ident, "c_ident"),
                         (rank, "c_rank")):
                sp.dma_start(t[:], A[a]).then_inc(w_in, 16)
            for i in range(2):
                r = slice(128 * i, 128 * i + 128)
                sp.dma_start(b1[:, i:i + 1], A["moe_b1"][r, :]).then_inc(w_in, 16)
                sp.dma_start(wg[:, i, :], A["moe_Wg"][r, :]).then_inc(w_in, 16)
                sp.dma_start(wd[:, i, :], A["moe_Wd"][r, :]).then_inc(w_in, 16)
            with sp.Fori(0, K) as k:
                for p in range(2):
                    t2_done.wait_free(sp, k * 2 + p)
                    sp.dma_start(x[:, p, :], A["a1"][:, bass.ds(k * (2 * CH) + p * CH, CH)]).then_inc(x_in[p], 16)

        @block.tensor
        def _(pe):
            for d in (hid_mm, logit_mm, y_mm, o_mm):
                d.start(pe)
            pe.wait_ge(w_in, NW)
            pe.wait_ge(filled, 1)
            with pe.Fori(0, K) as k:
                for p in range(2):
                    n = k * 2 + p
                    pe.wait_ge(x_in[p], k * 16 + 16)
                    hidden.wait_free(pe, n, 1)
                    for i in range(2):
                        mm = pe.matmul(ps_h[i][:, 0:CH], w1[:, 128 * i:128 * i + 128], x[:, p, :],
                                       start=True, stop=True)
                    mm.then_inc(hid_mm.sem, 1)
                    hidden.wait(pe, n)
                    shifted.wait_free(pe, n, 1)
                    for t in range(NTT):
                        tok = slice(TT * t, TT * t + TT)
                        dst = ps_l[0:TT, N_EXP * t:N_EXP * t + N_EXP]
                        for i in range(2):
                            pe.matmul(dst, hid[:, p, i, tok], wg[:, i, :], start=i == 0, stop=False)
                        mm = pe.matmul(dst, ones[:], bg[:], start=False, stop=True)
                    mm.then_inc(logit_mm.sem, 1)
                    for t in range(NTT):
                        tok = slice(TT * t, TT * t + TT)
                        y_read.wait_free(pe, n * NTT + t)
                        for i in range(2):
                            pe.matmul(ps_y[t % 2][0:TT, :], hid[:, p, i, tok], wd[:, i, :], start=i == 0, stop=False)
                        pe.matmul(ps_y[t % 2][0:TT, :], ones[:], bd[:], start=False, stop=True).then_inc(y_mm.sem, 1)
                    reduced.wait(pe, n * NTT + (NTT - 1))
                    t2_done.wait_free(pe, n)
                    for t in range(NTT):
                        mm = pe.matmul(ps_t[p][0:C, TT * t:TT * t + TT], o[:, p, t, :], ident[0:TT, 0:TT],
                                       start=True, stop=True)
                    mm.then_inc(o_mm.sem, 1)

        @block.scalar
        def _(act):
            hidden.start(act)
            exps.start(act)
            act.wait_ge(w_in, NW)
            with act.Fori(0, K) as k:
                for p in range(2):
                    n = k * 2 + p
                    hid_mm.wait(act, n)
                    for i in range(2):
                        a = act.activation(hid[:, p, i, :], ps_h[i][:, 0:CH], ACT.Gelu, bias=b1[:, i:i + 1])
                    a.then_inc(hidden.sem, 1)
                    shifted.wait(act, n)
                    act.activation(ex[:], sh[:], ACT.Exp).then_inc(exps.sem, 1)

        @block.vector
        def _(dve):
            for d in (shifted, y_read, wt_done, reduced, t2_done):
                d.start(dve)
            dve.memset(ones[:], 1.0).then_inc(filled, 1)
            dve.wait_ge(w_in, NW)
            order = Order(dve, steps, 2 * 9)
            with dve.Fori(0, K) as k:
                order.at(k)
                for p in range(2):
                    n = k * 2 + p
                    logit_mm.wait(dve, n)
                    logits = ps_l[0:TT, 0:NTT * N_EXP].rearrange("p (t e) -> p t e", e=N_EXP)
                    order(dve.reduce_max(mx[:], logits, AX_X))
                    dve.tensor_tensor(sh[:], logits, bcast(mx[:]), ALU.subtract).then_inc(shifted.sem, 1)
                    exps.wait(dve, n)
                    order(dve.reduce_sum(sm[:], ex[:], AX_X))
                    order(dve.reciprocal(sm[:], sm[:]))
                    order(dve.reduce_max(mx[:], ex[:], AX_X))
                    order(dve.tensor_tensor(eq[:], ex[:], bcast(mx[:]), ALU.is_ge))
                    order(dve.tensor_tensor(eq[:], eq[:], rank[:], ALU.mult))
                    order(dve.reduce_max(first[:], eq[:], AX_X))
                    order(dve.tensor_tensor(eq[:], eq[:], bcast(first[:]), ALU.is_equal))
                    order(dve.tensor_tensor(pm[:], mx[:], sm[:], ALU.mult))
                    dve.tensor_tensor(wt[:], eq[:], bcast(pm[:]), ALU.mult).then_inc(wt_done.sem, 1)
                    wt_done.wait(dve, n)
                    for t in range(NTT + 1):
                        if t < NTT:
                            y_mm.wait(dve, n * NTT + t)
                            reduced.wait_free(dve, n * NTT + t)
                            dve.tensor_tensor(picked[:, t % 2, :, :],
                                              ps_y[t % 2][0:TT, :].rearrange("p (e c) -> p e c", c=C),
                                              wt[:, t, :].unsqueeze(2).broadcast_to([TT, N_EXP, C]),
                                              ALU.mult).then_inc(y_read.sem, 1)
                        if t:
                            t1 = t - 1
                            y_read.wait(dve, n * NTT + t1)
                            if t == 1:
                                o_mm.wait_free(dve, n)
                            dve.reduce_sum(o[:, p, t1, :], picked[:, t1 % 2, :, :].rearrange("p e c -> p c e"),
                                           AX_X).then_inc(reduced.sem, 1)
                    dve.wait_ge(out[p], k * 16)
                    o_mm.wait(dve, n)
                    dve.tensor_tensor(t2[:, p, :], ps_t[p][0:C, 0:CH], x[:, p, :], ALU.add).then_inc(t2_done.sem, 1)

        @block.gpsimd
        def _(pool):
            with pool.Fori(0, K) as k:
                for p in range(2):
                    t2_done.wait(pool, k * 2 + p)
                    pool.dma_start(A["t2"][:, bass.ds(k * (2 * CH) + p * CH, CH)], t2[:, p, :]).then_inc(out[p], 16)
            for p in range(2):
                pool.wait_ge(out[p], 16 * K)
KT = 128
NKT = -(-L // KT)
LP = NKT * KT
PROD = 6 * HD
ROW_TOP, ROW_MAX = PROD, PROD + 1
KROWS = PROD + 3
STAIR = 1664
SCALE = HD ** -0.5


def qkv_parts(nc, sems, A):
    with ExitStack() as ctx:
        m = Place(nc, "qk", ctx, sems)
        w, b, sc = m.sb("w", [C, 2 * C]), m.sb("b", [2 * C, 1]), m.sb("sc", [2 * C, 1])
        x = m.sb("x", [C, 2, CH])
        qk, rest = m.sb("qk", [2 * C, 2, CH]), m.sb("rest", [2 * C, 2, CH])
        parts = m.sb("parts", [2 * C, 2, 3, CH], BF16)
        ps = [m.bank(f"ps{p}") for p in range(2)]
        w_in, steps = m.sem("w_in"), m.sem("steps")
        x_in = [m.sem(f"x_in{p}") for p in range(2)]
        out = [m.sem(f"out{p}") for p in range(2)]
        mm, read, split = m.done("mm"), m.done("read"), m.done("split")
        block = ctx.enter_context(nc.Block())
        K = T // CH // 2

        @block.sync
        def _(sp):
            for t, a in ((w, "W_qk"), (b, "b_qk"), (sc, "c_qscale")):
                sp.dma_start(t[:], A[a]).then_inc(w_in, 16)
            with sp.Fori(0, K) as k:
                for p in range(2):
                    mm.wait_free(sp, k * 2 + p)
                    sp.dma_start(x[:, p, :], A["a2"][:, bass.ds(k * (2 * CH) + p * CH, CH)]).then_inc(x_in[p], 16)

        @block.tensor
        def _(pe):
            mm.start(pe)
            pe.wait_ge(w_in, 48)
            with pe.Fori(0, K) as k:
                for p in range(2):
                    pe.wait_ge(x_in[p], k * 16 + 16)
                    read.wait_free(pe, k * 2 + p)
                    pe.matmul(ps[p][:, 0:CH], w[:], x[:, p, :], start=True, stop=True).then_inc(mm.sem, 1)

        @block.vector
        def _(dve):
            read.start(dve)
            split.start(dve)
            dve.wait_ge(w_in, 48)
            order = Order(dve, steps, 6)
            with dve.Fori(0, K) as k:
                order.at(k)
                for p in range(2):
                    n = k * 2 + p
                    mm.wait(dve, n)
                    dve.tensor_scalar(qk[:, p, :], ps[p][:, 0:CH], b[:], sc[:], ALU.add, ALU.mult).then_inc(read.sem, 1)
                    dve.wait_ge(out[p], k * 48)
                    read.wait(dve, n)
                    order(dve.tensor_copy(parts[:, p, 0, :], qk[:, p, :]))
                    order(dve.tensor_tensor(rest[:, p, :], qk[:, p, :], parts[:, p, 0, :], ALU.subtract))
                    order(dve.tensor_copy(parts[:, p, 1, :], rest[:, p, :]))
                    dve.tensor_tensor(parts[:, p, 2, :], rest[:, p, :], parts[:, p, 1, :],
                                      ALU.subtract).then_inc(split.sem, 1)

        @block.gpsimd
        def _(pool):
            with pool.Fori(0, K) as k:
                for p in range(2):
                    split.wait(pool, k * 2 + p)
                    for i in range(3):
                        pool.dma_start(A["qk_parts"][i][:, bass.ds(k * (2 * CH) + p * CH, CH)],
                                       parts[:, p, i, :]).then_inc(out[p], 16)
            for p in range(2):
                pool.wait_ge(out[p], 48 * K)


def values(nc, sems, A):
    with ExitStack() as ctx:
        m = Place(nc, "val", ctx, sems)
        w, bv, ones = m.sb("w", [C, C]), m.sb("bv", [1, C]), m.sb("ones", [1, KT])
        x = m.sb("x", [C, 2, LP])
        v = m.sb("v", [128, HEADS, NKT, 32])
        ps = [m.bank(f"ps{i}") for i in range(2)]
        w_in, out, filled = m.sem("w_in"), m.sem("out"), m.sem("filled")
        x_in = [m.sem(f"x_in{p}") for p in range(2)]
        mm, read = m.done("mm"), m.done("read")
        block = ctx.enter_context(nc.Block())
        groups = [range(g, min(g + 4, NKT)) for g in range(0, NKT, 4)]
        NG = len(groups)
        last_rows = L - (NKT - 1) * KT

        @block.sync
        def _(sp):
            sp.dma_start(w[:], A["W_v"]).then_inc(w_in, 16)
            sp.dma_start(bv[:], A["b_v"]).then_inc(w_in, 16)
            sp.wait_ge(filled, 2)
            for b in range(B):
                if b >= 2:
                    mm.wait(sp, (b - 1) * NG - 1)
                sp.dma_start(x[:, b % 2, 0:L], A["a2"][:, b * L:b * L + L]).then_inc(x_in[b % 2], 16)

        @block.tensor
        def _(pe):
            mm.start(pe)
            pe.wait_ge(w_in, 32)
            pe.wait_ge(filled, 4)
            for b in range(B):
                pe.wait_ge(x_in[b % 2], 16 * (b // 2 + 1))
                for g, tiles in enumerate(groups):
                    read.wait_free(pe, b * NG + g)
                    bank = ps[(b * NG + g) % 2]
                    for i, t in enumerate(tiles):
                        pe.matmul(bank[:, C * i:C * i + C], x[:, b % 2, KT * t:KT * t + KT], w[:],
                                  start=True, stop=False)
                        last = pe.matmul(bank[:, C * i:C * i + C], ones[:], bv[:], start=False, stop=True)
                    last.then_inc(mm.sem, 1)

        @block.vector
        def _(dve):
            read.start(dve)
            dve.memset(x[:, :, L:LP], 0.0).then_inc(filled, 2)
            dve.memset(v[:], 0.0).then_inc(filled, 1)
            dve.memset(ones[:], 1.0).then_inc(filled, 1)
            dve.wait_ge(filled, 4)
            dve.memset(v[:, :, 0:NKT - 1, HD:HD + 1], 1.0)
            dve.memset(v[0:last_rows, :, NKT - 1:NKT, HD:HD + 1], 1.0)
            for b in range(B):
                if b:
                    dve.wait_ge(out, 16 * b)
                for g, tiles in enumerate(groups):
                    mm.wait(dve, b * NG + g)
                    bank = ps[(b * NG + g) % 2]
                    full = [t for t in tiles if t < NKT - 1]
                    rows, n = (128, len(full)) if full else (last_rows, 1)
                    dve.tensor_copy(v[0:rows, :, tiles[0]:tiles[0] + n, 0:HD],
                                    bank[0:rows, 0:C * n].rearrange("p (t h d) -> p h t d", h=HEADS,
                                                                    d=HD)).then_inc(read.sem, 1)

        @block.gpsimd
        def _(pool):
            for b in range(B):
                read.wait(pool, b * NG + NG - 1)
                pool.dma_start(A["vals"][b * HEADS:b * HEADS + HEADS].rearrange("h p n -> p h n"),
                               v[:].rearrange("p h t d -> p h (t d)")).then_inc(out, 16)
            pool.wait_ge(out, 16 * B)


def heads(eng):
    with eng.Fori(0, B) as b:
        with eng.Fori(0, HEADS // 2) as h2:
            yield b * (HEADS // 2) + h2, b, h2


Q_PART = (0, 0, 1, 1, 0, 2)
K_PART = (0, 1, 0, 1, 2, 0)


def load_operands(sp, A, qb, kb, p, b, h2, sem):
    cols = bass.ds(b * L, L)
    for i in range(6):
        for t, part, first in ((qb, Q_PART[i], 0), (kb, K_PART[i], C)):
            src = A["qk_parts"][part][first:first + C, :].rearrange("(g r) t -> g r t", r=HD)
            sp.dma_start(t[HD * i:HD * i + HD, p, 0:L],
                         src[bass.ds(h2 * 2 + p, 1), :, cols].rearrange("g r t -> (g r) t")).then_inc(sem, 16)


def row_maxima(nc, sems, A):
    NKC = L // CH
    with ExitStack() as ctx:
        m = Place(nc, "max", ctx, sems)
        qb, kb = m.sb("qb", [128, 2, LP], BF16), m.sb("kb", [128, 2, LP], BF16)
        ident, ident_low = m.sb("ident", [128, 128], BF16), m.sb("ident_low", [128, 128], BF16)
        stair = m.sb("stair", [128, 2 * STAIR + CH], BF16)
        ident_f = m.sb("ident_f", [128, 128])
        pm, mx = m.sb("pm", [128, 2, 2, NKT]), m.sb("mx", [128, 2, NKT])
        neg, rest = m.sb("neg", [NKT, 2, KT]), m.sb("rest", [NKT, KT])
        parts = m.sb("parts", [NKT, 2, 2, KT], BF16)
        ps = [ctx.enter_context(nc.psum_tensor(f"max_ps{i}", [128, 4, 512], F32)) for i in range(2)]
        ps_t = ps[1][0:NKT, 3, 0:KT]
        w_in, filled = m.sem("w_in"), m.sem("filled")
        op_in = [m.sem(f"op_in{p}") for p in range(2)]
        out = [m.sem(f"out{p}") for p in range(2)]
        mm, reduced, joined, turned = m.done("mm"), m.done("reduced"), m.done("joined"), m.done("turned")
        neg_done, split, steps = m.done("neg_done"), m.done("split"), m.sem("steps")
        block = ctx.enter_context(nc.Block())
        half = L // 2

        @block.sync
        def _(sp):
            for t, a in ((ident, "c_ident_b"), (ident_low, "c_ident_low"), (stair, "c_stair_qk"), (ident_f, "c_ident")):
                sp.dma_start(t[:], A[a]).then_inc(w_in, 16)
            sp.wait_ge(filled, 2)
            for p in range(2):
                sp.dma_start(qb[ROW_TOP:ROW_TOP + 1, p, 0:L], A["c_qrow"]).then_inc(w_in, 16)
                sp.dma_start(kb[ROW_TOP:KROWS, p, 0:L], A["c_krows"]).then_inc(w_in, 16)
            for it, b, h2 in heads(sp):
                for p in range(2):
                    n = it * 2 + p
                    joined.wait_free(sp, n)
                    load_operands(sp, A, qb, kb, p, b, h2, op_in[p])

        @block.tensor
        def _(pe):
            mm.start(pe)
            turned.start(pe)
            pe.wait_ge(w_in, 16 * 8)
            for it, b, h2 in heads(pe):
                for p in range(2):
                    n = it * 2 + p
                    pe.wait_ge(op_in[p], it * 192 + 192)
                    for qt in range(NKT):
                        q0 = qt * KT
                        for side, chunks in ((0, range(4)), (1, range(4, NKC))):
                            reduced.wait_free(pe, n * (2 * NKT) + (2 * qt + side))
                            if qt == 0 and side == 1:
                                neg_done.wait_free(pe, n, 1)
                            for kc in chunks:
                                dst = ps[side][:, kc - chunks[0], 0:CH]
                                k0 = kc * CH
                                masked = q0 + KT > half and k0 + CH - 1 > max(q0, half)
                                mult = pe.matmul(dst, qb[:, p, q0:q0 + KT], kb[:, p, k0:k0 + CH],
                                                 start=True, stop=not masked)
                                if masked:
                                    at = STAIR + k0 - q0
                                    mult = pe.matmul(dst, (ident_low if q0 < half else ident)[:],
                                                     stair[:, at:at + CH], start=False, stop=True)
                            mult.then_inc(mm.sem, 1)
                    joined.wait(pe, n)
                    pe.matmul(ps_t, mx[:, p, :], ident_f[:], start=True, stop=True).then_inc(turned.sem, 1)

        @block.vector
        def _(dve):
            for d in (reduced, joined, neg_done, split):
                d.start(dve)
            dve.memset(qb[:], 0.0).then_inc(filled, 1)
            dve.memset(kb[:], 0.0).then_inc(filled, 1)
            order = Order(dve, steps, 2)
            for it, b, h2 in heads(dve):
                order.at(it)
                for p in range(2):
                    n = it * 2 + p
                    for qt in range(NKT):
                        for side in range(2):
                            s = n * (2 * NKT) + (2 * qt + side)
                            mm.wait(dve, s)
                            if qt == 0:
                                joined.wait_free(dve, n)
                            dve.tensor_reduce(pm[:, p, side, qt:qt + 1], ps[side][:, 0:4 - side, 0:CH],
                                              mybir.AxisListType.XY, ALU.max).then_inc(reduced.sem, 1)
                    reduced.wait(dve, n * (2 * NKT) + (2 * NKT - 1))
                    turned.wait_free(dve, n)
                    dve.tensor_tensor(mx[:, p, :], pm[:, p, 0, :], pm[:, p, 1, :], ALU.max).then_inc(joined.sem, 1)
                    turned.wait(dve, n)
                    dve.tensor_scalar(neg[:, p, :], ps_t, -1.0, None, ALU.mult).then_inc(neg_done.sem, 1)
                    dve.wait_ge(out[p], it * 16)
                    neg_done.wait(dve, n)
                    order(dve.tensor_copy(parts[:, p, 0, :], neg[:, p, :]))
                    dve.tensor_tensor(parts[:, p, 1, :], neg[:, p, :], parts[:, p, 0, :],
                                      ALU.subtract).then_inc(split.sem, 1)

        @block.gpsimd
        def _(pool):
            for it, b, h2 in heads(pool):
                for p in range(2):
                    split.wait(pool, it * 2 + p)
                    dst = A["neg_max"][bass.ds(it * 2 + p, 1)].rearrange("g a (t q) -> t (g a) q", q=KT)
                    pool.dma_start(dst, parts[:, p, :, :]).then_inc(out[p], 16)
            for p in range(2):
                pool.wait_ge(out[p], 16 * (B * HEADS // 2))


def attend(nc, sems, A):
    GROUPS = [list(range(g, min(g + 2, NKT))) for g in range(0, NKT, 2)]
    NQC, NG = L // CH, len(GROUPS)
    PER = NQC * NG
    with ExitStack() as ctx:
        m = Place(nc, "att", ctx, sems)
        qb, kb = m.sb("qb", [128, 2, LP], BF16), m.sb("kb", [128, 2, LP], BF16)
        vh = m.sb("vh", [128, 2, NKT, 32])
        ident, stair = m.sb("ident", [128, 128], BF16), m.sb("stair", [128, 2 * STAIR + CH], BF16)
        join = m.sb("join", [128, 9])
        NP, NS = 4, 3
        prob = m.sb("prob", [128, NP, 2, CH])
        o4, o9 = m.sb("o4", [128, 2, CH]), m.sb("o9", [HD + 1, 2, CH])
        ps_s = [ctx.enter_context(nc.psum_tensor(f"att_ps_s{i}", [128, 2, 512], F32)) for i in range(NS)]
        ps_o = [m.bank(f"ps_o{i}") for i in range(2)]
        w_in, filled = m.sem("w_in"), m.sem("filled")
        op_in = [m.sem(f"op_in{p}") for p in range(2)]
        out = [m.sem(f"out{c}") for c in range(2)]
        score_mm, exps, pv_mm = m.done("score_mm", 6), m.done("exps", 6), m.done("pv_mm", 6)
        o4_done, join_mm, o9_done = m.done("o4_done", 2 * NQC), m.done("join_mm"), m.done("o9_done")
        block = ctx.enter_context(nc.Block())
        half = L // 2

        def slot(p, i, depth):
            idx, every = p * PER + i, 2 * PER
            back = depth if idx >= depth else next(
                d for d in range(1, 2 * depth) if (idx - d if idx >= d else (idx - d) % every) % depth == idx % depth)
            return idx % depth, back

        @block.sync
        def _(sp):
            for t, a in ((ident, "c_ident_b"), (stair, "c_stair_kq"), (join, "c_join")):
                sp.dma_start(t[:], A[a]).then_inc(w_in, 16)
            sp.wait_ge(filled, 2)
            for p in range(2):
                sp.dma_start(qb[ROW_TOP:ROW_TOP + 1, p, 0:L], A["c_qrow"]).then_inc(w_in, 16)
                sp.dma_start(kb[ROW_TOP:KROWS, p, 0:L], A["c_krows"]).then_inc(w_in, 16)
            for it, b, h2 in heads(sp):
                for p in range(2):
                    n = it * 2 + p
                    o4_done.wait_free(sp, n * NQC + (NQC - 1), 2 * NQC)
                    load_operands(sp, A, qb, kb, p, b, h2, op_in[p])
                    sp.dma_start(qb[ROW_MAX:KROWS, p, 0:L],
                                 A["neg_max"][bass.ds(n, 1), :, 0:L].rearrange("g a t -> (g a) t")).then_inc(op_in[p], 16)
                    sp.dma_start(vh[:, p, :, :].rearrange("k t d -> k (t d)"),
                                 A["vals"][bass.ds(n, 1)].rearrange("g k n -> (g k) n")).then_inc(op_in[p], 16)

        @block.tensor
        def _(pe):
            for d in (score_mm, pv_mm, join_mm):
                d.start(pe)
            pe.wait_ge(w_in, 16 * 7)

            def scores(n, p, i):
                c, g = divmod(i, NG)
                s, back = slot(p, i, NS)
                q0 = c * CH
                exps.wait_free(pe, n * PER + i, back)
                for u, kt in enumerate(GROUPS[g]):
                    k0 = kt * KT
                    masked = q0 + CH > half and k0 + KT - 1 > max(q0, half)
                    dst = ps_s[s][:, u, 0:CH]
                    mult = pe.matmul(dst, kb[:, p, k0:k0 + KT], qb[:, p, q0:q0 + CH], start=True, stop=not masked)
                    if masked:
                        lo = max(0, half - q0)
                        at = STAIR + q0 + lo - k0
                        mult = pe.matmul(dst[:, lo:CH], ident[:], stair[:, at:at + CH - lo], start=False, stop=True)
                mult.then_inc(score_mm.sem, 1)

            def weigh(n, p, i):
                c, g = divmod(i, NG)
                s, _ = slot(p, i, NP)
                bank = (p * NQC + c) % 2
                exps.wait(pe, n * PER + i)
                if g == 0:
                    o9_done.wait_free(pe, n * NQC + c)
                for u, kt in enumerate(GROUPS[g]):
                    q = kt % 4
                    mult = pe.matmul(ps_o[bank][32 * q:32 * q + 32, 0:CH], vh[:, p, kt, :], prob[:, s, u, :],
                                     start=kt < 4, stop=kt >= NKT - 4, tile_position=(0, 32 * q))
                mult.then_inc(pv_mm.sem, 1)

            def join_up(n, p, c):
                bank = (p * NQC + c) % 2
                o4_done.wait(pe, n * NQC + c)
                pe.matmul(ps_o[bank][0:HD + 1, 0:CH], join[:], o4[:, bank, :], start=True,
                          stop=True).then_inc(join_mm.sem, 1)

            for it, b, h2 in heads(pe):
                for p in range(2):
                    n = it * 2 + p
                    pe.wait_ge(op_in[p], it * 224 + 224)
                    for i in range(PER + 2):
                        if i < PER:
                            scores(n, p, i)
                        if i >= 2:
                            weigh(n, p, i - 2)
                        if i % NG == 4 and i > NG:
                            join_up(n, p, i // NG - 1)
                    join_up(n, p, NQC - 1)

        @block.scalar
        def _(act):
            exps.start(act)
            act.preload_act_table_set("exp_and_others")
            for it, b, h2 in heads(act):
                for p in range(2):
                    n = it * 2 + p
                    for i in range(PER):
                        s, _ = slot(p, i, NS)
                        s2, back = slot(p, i, NP)
                        u = len(GROUPS[i % NG])
                        score_mm.wait(act, n * PER + i)
                        pv_mm.wait_free(act, n * PER + i, back)
                        act.activation(prob[:, s2, 0:u, :], ps_s[s][:, 0:u, 0:CH], ACT.Exp).then_inc(exps.sem, 1)

        @block.vector
        def _(dve):
            o4_done.start(dve)
            o9_done.start(dve)
            dve.memset(qb[:], 0.0).then_inc(filled, 1)
            dve.memset(kb[:], 0.0).then_inc(filled, 1)
            for it, b, h2 in heads(dve):
                for p in range(2):
                    n = it * 2 + p
                    for c in range(NQC):
                        bank = (p * NQC + c) % 2
                        step = n * NQC + c
                        pv_mm.wait(dve, n * PER + (c * NG + NG - 1))
                        join_mm.wait_free(dve, step)
                        dve.tensor_copy(o4[:, bank, :], ps_o[bank][:, 0:CH]).then_inc(o4_done.sem, 1)
                        join_mm.wait(dve, step)
                        dve.wait_ge(out[bank], it * 112 + 16 * ((p * NQC + c) // 2))
                        dve.tensor_copy(o9[:, bank, :], ps_o[bank][0:HD + 1, 0:CH]).then_inc(o9_done.sem, 1)

        @block.gpsimd
        def _(pool):
            for it, b, h2 in heads(pool):
                for p in range(2):
                    n = it * 2 + p
                    for c in range(NQC):
                        bank = (p * NQC + c) % 2
                        o9_done.wait(pool, n * NQC + c)
                        dst = A["att"].rearrange("(h r) t -> h r t", r=HD + 1)[
                            bass.ds(h2 * 2 + p, 1), :, bass.ds(b * L + c * CH, CH)].rearrange("g r t -> (g r) t")
                        pool.dma_start(dst, o9[:, bank, :]).then_inc(out[bank], 16)
            for c in range(2):
                pool.wait_ge(out[c], 16 * NQC * B * HEADS // 2)
def add_attention(nc, sems, A):
    R = HEADS * (HD + 1)
    with ExitStack() as ctx:
        m = Place(nc, "norm", ctx, sems)
        pick, spread = m.sb("pick", [R, C]), m.sb("spread", [R, C])
        o, x = m.sb("o", [R, 2, CH]), m.sb("x", [C, 2, CH])
        rec, y, t3 = m.sb("rec", [C, 2, CH]), m.sb("y", [C, 2, CH]), m.sb("t3", [C, 2, CH])
        ps_n = [m.bank(f"ps_n{p}") for p in range(2)]
        ps_d = [m.bank(f"ps_d{p}") for p in range(2)]
        w_in, steps = m.sem("w_in"), m.sem("steps")
        x_in = [m.sem(f"x_in{p}") for p in range(2)]
        out = [m.sem(f"out{p}") for p in range(2)]
        mm, added = m.done("mm"), m.done("added")
        block = ctx.enter_context(nc.Block())
        K = T // CH // 2

        @block.sync
        def _(sp):
            for t, a in ((pick, "c_pick"), (spread, "c_spread")):
                sp.dma_start(t[:], A[a]).then_inc(w_in, 16)
            with sp.Fori(0, K) as k:
                for p in range(2):
                    added.wait_free(sp, k * 2 + p)
                    for t, a in ((o, "att"), (x, "a2")):
                        sp.dma_start(t[:, p, :], A[a][:, bass.ds(k * (2 * CH) + p * CH, CH)]).then_inc(x_in[p], 16)

        @block.tensor
        def _(pe):
            mm.start(pe)
            pe.wait_ge(w_in, 32)
            with pe.Fori(0, K) as k:
                for p in range(2):
                    pe.wait_ge(x_in[p], k * 32 + 32)
                    added.wait_free(pe, k * 2 + p)
                    pe.matmul(ps_n[p][0:C, 0:CH], pick[:], o[:, p, :], start=True, stop=True)
                    pe.matmul(ps_d[p][0:C, 0:CH], spread[:], o[:, p, :], start=True, stop=True).then_inc(mm.sem, 1)

        @block.vector
        def _(dve):
            added.start(dve)
            order = Order(dve, steps, 4)
            with dve.Fori(0, K) as k:
                order.at(k)
                for p in range(2):
                    mm.wait(dve, k * 2 + p)
                    order(dve.reciprocal(rec[:, p, :], ps_d[p][0:C, 0:CH]))
                    order(dve.tensor_tensor(y[:, p, :], ps_n[p][0:C, 0:CH], rec[:, p, :], ALU.mult))
                    dve.wait_ge(out[p], k * 16)
                    dve.tensor_tensor(t3[:, p, :], y[:, p, :], x[:, p, :], ALU.add).then_inc(added.sem, 1)

        @block.gpsimd
        def _(pool):
            with pool.Fori(0, K) as k:
                for p in range(2):
                    added.wait(pool, k * 2 + p)
                    pool.dma_start(A["t3"][:, bass.ds(k * (2 * CH) + p * CH, CH)], t3[:, p, :]).then_inc(out[p], 16)
            for p in range(2):
                pool.wait_ge(out[p], 16 * K)


def route(nc, sems, A):
    with ExitStack() as ctx:
        m = Place(nc, "rout", ctx, sems)
        wr, br = m.sb("wr", [C, 128]), m.sb("br", [1, 1])
        x, w = m.sb("x", [C, 2, CH]), m.sb("w", [1, 2, CH])
        ps = [m.bank(f"ps{p}") for p in range(2)]
        w_in = m.sem("w_in")
        x_in = [m.sem(f"x_in{p}") for p in range(2)]
        out = [m.sem(f"out{p}") for p in range(2)]
        mm, added = m.done("mm"), m.done("added")
        block = ctx.enter_context(nc.Block())
        K = T // CH // 2

        @block.sync
        def _(sp):
            for t, a in ((wr, "wr"), (br, "br")):
                sp.dma_start(t[:], A[a]).then_inc(w_in, 16)
            with sp.Fori(0, K) as k:
                for p in range(2):
                    mm.wait_free(sp, k * 2 + p)
                    sp.dma_start(x[:, p, :], A["a3"][:, bass.ds(k * (2 * CH) + p * CH, CH)]).then_inc(x_in[p], 16)

        @block.tensor
        def _(pe):
            mm.start(pe)
            pe.wait_ge(w_in, 32)
            with pe.Fori(0, K) as k:
                for p in range(2):
                    pe.wait_ge(x_in[p], k * 16 + 16)
                    added.wait_free(pe, k * 2 + p)
                    pe.matmul(ps[p][:, 0:CH], wr[:], x[:, p, :], start=True, stop=True).then_inc(mm.sem, 1)

        @block.vector
        def _(dve):
            added.start(dve)
            dve.wait_ge(w_in, 32)
            with dve.Fori(0, K) as k:
                for p in range(2):
                    mm.wait(dve, k * 2 + p)
                    dve.wait_ge(out[p], k * 16)
                    dve.tensor_scalar(w[:, p, :], ps[p][0:1, 0:CH], br[:], None, ALU.add).then_inc(added.sem, 1)

        @block.gpsimd
        def _(pool):
            with pool.Fori(0, K) as k:
                for p in range(2):
                    added.wait(pool, k * 2 + p)
                    pool.dma_start(A["w"][:, bass.ds(k * (2 * CH) + p * CH, CH)], w[:, p, :]).then_inc(out[p], 16)
            for p in range(2):
                pool.wait_ge(out[p], 16 * K)


N_SEL = L // 2 - 1


def pick_tokens(nc, sems, A):
    W = L // 32
    with ExitStack() as ctx:
        m = Place(nc, "pick", ctx, sems)
        w, hit = m.sb("w", [128, W]), m.sb("hit", [128, W])
        group, before = m.sb("group", [128, 128]), m.sb("before", [128, 128])
        key, bit = m.sb("key", [128, 1], U32), m.sb("bit", [128, 1], U32)
        cand, flip, edge = m.sb("cand", [128, 1], U32), m.sb("flip", [128, 1], U32), m.sb("edge", [128, 1], U32)
        count, enough = m.sb("count", [128, 1]), m.sb("enough", [128, 1], U32)
        above, equal = m.sb("above", [128, W]), m.sb("equal", [128, W])
        n_above, n_equal = m.sb("n_above", [128, 1]), m.sb("n_equal", [128, 1])
        zeros, upto = m.sb("zeros", [128, W]), m.sb("upto", [128, W])
        room, take, ws = m.sb("room", [128, 1]), m.sb("take", [128, W]), m.sb("ws", [128, W])
        ps, ps2 = m.bank("ps"), m.bank("ps2")
        w_in, counted, summed, steps, done, out = (m.sem("w_in"), m.sem("counted"), m.sem("summed"),
                                                   m.sem("steps"), m.sem("done"), m.sem("out"))
        block = ctx.enter_context(nc.Block())
        BITS = 32

        @block.sync
        def _(sp):
            sp.dma_start(w[:], A["w"].rearrange("a (p c) -> (a p) c", c=W)).then_inc(w_in, 16)
            sp.dma_start(group[:], A["c_group"]).then_inc(w_in, 16)
            sp.dma_start(before[:], A["c_before"]).then_inc(w_in, 16)
            sp.dma_start(bit[:], A["c_top_bit"]).then_inc(w_in, 16)
            sp.wait_ge(done, 1)
            sp.dma_start(A["ws"].rearrange("a (p c) -> (a p) c", c=W), ws[:]).then_inc(out, 16)
            sp.wait_ge(out, 16)

        @block.tensor
        def _(pe):
            pe.wait_ge(w_in, 64)
            with pe.Fori(0, BITS) as i:
                pe.wait_ge(counted, i + 1)
                pe.matmul(ps[:, 0:1], group[:], count[:], start=True, stop=True).then_inc(summed, 1)
            pe.wait_ge(counted, BITS + 1)
            pe.matmul(ps[:, 0:1], group[:], n_above[:], start=True, stop=True)
            pe.matmul(ps2[:, 0:1], before[:], n_equal[:], start=True, stop=True).then_inc(summed, 1)

        @block.vector
        def _(dve):
            dve.memset(key[:], 0).then_inc(steps, 1)
            dve.memset(zeros[:], 0.0).then_inc(steps, 1)
            dve.wait_ge(steps, 2)
            dve.wait_ge(w_in, 64)

            def after(ins, n):
                ins.then_inc(steps, 1)
                dve.wait_ge(steps, n)

            STEPS = 7
            with dve.Fori(0, BITS) as i:
                base = i * STEPS + 2
                after(dve.tensor_tensor(cand[:], key[:], bit[:], ALU.bitwise_or), base + 1)
                after(dve.tensor_scalar(flip[:], cand[:], 31, 0xFFFFFFFF, ALU.arith_shift_right,
                                        ALU.bitwise_xor), base + 2)
                after(dve.tensor_scalar(flip[:], flip[:], 0x80000000, None, ALU.bitwise_or), base + 3)
                after(dve.tensor_tensor(edge[:], cand[:], flip[:], ALU.bitwise_xor), base + 4)
                dve.tensor_scalar(hit[:], w[:], edge[:].bitcast(F32), 0.0, ALU.is_ge, ALU.add,
                                  accum_out=count[:]).then_inc(counted, 1)
                dve.wait_ge(summed, i + 1)
                after(dve.tensor_scalar(enough[:], ps[:, 0:1], float(N_SEL), None, ALU.is_ge), base + 5)
                dve.tensor_scalar(bit[:], bit[:], 1, None, ALU.logical_shift_right).then_inc(steps, 1)
                after(dve.copy_predicated(key[:], enough[:], cand[:]), base + 7)
            n = BITS * STEPS + 2
            after(dve.tensor_scalar(flip[:], key[:], 31, 0xFFFFFFFF, ALU.arith_shift_right, ALU.bitwise_xor), n + 1)
            after(dve.tensor_scalar(flip[:], flip[:], 0x80000000, None, ALU.bitwise_or), n + 2)
            after(dve.tensor_tensor(edge[:], key[:], flip[:], ALU.bitwise_xor), n + 3)
            last = edge[:].bitcast(F32)
            after(dve.tensor_scalar(above[:], w[:], last, 0.0, ALU.is_gt, ALU.add, accum_out=n_above[:]), n + 4)
            dve.tensor_scalar(equal[:], w[:], last, 0.0, ALU.is_equal, ALU.add,
                              accum_out=n_equal[:]).then_inc(counted, 1)
            dve.wait_ge(counted, BITS + 1)
            after(dve.tensor_tensor_scan(upto[:], equal[:], zeros[:], 0.0, ALU.add, ALU.add), n + 5)
            dve.wait_ge(summed, BITS + 1)
            after(dve.tensor_scalar(room[:], ps[:, 0:1], -1.0, float(N_SEL), ALU.mult, ALU.add), n + 6)
            after(dve.tensor_tensor(room[:], room[:], ps2[:, 0:1], ALU.subtract), n + 7)
            after(dve.scalar_tensor_tensor(take[:], upto[:], room[:], equal[:], ALU.is_le, ALU.mult), n + 8)
            after(dve.tensor_tensor(take[:], take[:], above[:], ALU.add), n + 9)
            dve.tensor_tensor(ws[:], take[:], w[:], ALU.mult).then_inc(done, 1)


def build(nc, A):
    def run(stage, *args, **kwargs):
        sems = []
        stage(nc, sems, A, *args, **kwargs)
        nc.clear_and_free_semaphores(sems)
        nc.all_engine_barrier()

    run(pad_image)
    run(tokenize)
    run(layer_norm, "ln1", "h0", "hn", ("norm1_g", "norm1_b"), 2)
    run(in_projection)
    run(step_sizes)
    run(selective_scan)
    run(out_projection)
    run(layer_norm, "ln2", "h1", "m2", ("norm2_g", "norm2_b"))
    run(mlp, "mlp0", "m2", ("h0", "h1"), "t1", ("mlp_w1", "mlp_b1", "mlp_w2", "mlp_b2"),
        ACT.Gelu, "gelu_and_others")
    run(layer_norm, "ln3", "t1", "a1")
    run(experts)
    run(layer_norm, "ln4", "t2", "a2")
    run(qkv_parts)
    run(values)
    run(row_maxima)
    run(attend)
    run(add_attention)
    run(layer_norm, "ln5", "t3", "a3")
    run(route)
    run(pick_tokens)
    run(mlp, "mlp1", "a3", ("a3", "a3"), "t4", ("ffn_w1", "ffn_b1", "ffn_w2", "ffn_b2"),
        ACT.Gelu_apprx_tanh, "gelu_apprx_tanh_and_others", gate="ws")
    run(layer_norm, "ln6", "t4", "out")


def constants(bf16):
    blocks = np.kron(np.eye(2), np.ones((C, C)) / C)
    m = np.arange(128)
    sel, ysel = np.zeros((96, 8, 128)), np.zeros((128, 8, 32))
    for r in range(8):
        for part in range(3):
            sel[part * 32 + 4 * r + m // 32, r, m] = 1
        ysel[m, r, 4 * r + m // 32] = 1
    x, q = np.arange(2 * STAIR + CH)[None, :] - STAIR, m[:, None]
    tok = np.arange(L)
    ident_low = np.eye(128)
    ident_low[:L // 2 % KT] = 0
    krows = np.ones((3, L))
    krows[0] = np.where(tok >= L // 2, -1000.0, 0.0)
    join = np.zeros((128, HD + 1))
    pick, spread = np.zeros((HEADS * (HD + 1), C)), np.zeros((HEADS * (HD + 1), C))
    for d in range(HD + 1):
        join[32 * np.arange(4) + d, d] = 1
    for c in range(C):
        pick[c // HD * (HD + 1) + c % HD, c] = 1
        spread[c // HD * (HD + 1) + HD, c] = 1
    same = m[:, None] // 32 == m[None, :] // 32
    f = {"c_center": np.eye(128) - blocks, "c_mean": blocks, "c_eps": np.full((128, 1), EPS), "c_ysel": ysel,
         "c_ident": np.eye(128), "c_rank": np.broadcast_to(N_EXP - np.arange(N_EXP), (112, 4, N_EXP)),
         "c_join": join, "c_pick": pick, "c_spread": spread, "c_group": same,
         "c_before": same & (m[:, None] < m[None, :]),
         "c_qscale": np.repeat([[SCALE], [1.0]], C, axis=0)}
    h = {"c_sel": sel, "c_ident_b": np.eye(128), "c_ident_low": ident_low,
         "c_stair_qk": np.where(x > q, -1000.0, 0.0), "c_stair_kq": np.where(x < q, -1000.0, 0.0),
         "c_qrow": (tok < L // 2)[None, :], "c_krows": krows}
    out = {k: np.ascontiguousarray(v, np.float32) for k, v in f.items()}
    out |= {k: np.ascontiguousarray(np.asarray(v, np.float32).astype(bf16)) for k, v in h.items()}
    out["c_top_bit"] = np.full((128, 1), 1 << 31, np.uint32)
    return out


SCRATCH = {"xpad": (B, C, PW * PW), "h0": (C, T), "hn": (C, B * (L + 4)), "sz": (E, T), "u": (E, T),
           "Bn": (128, T), "Cn": (128, T), "dtp": (E, T), "yz": (E, T), "h1": (C, T), "m2": (C, T),
           "t1": (C, T), "a1": (C, T), "t2": (C, T), "a2": (C, T), "vals": (B * HEADS, 128, NKT * 32),
           "att": (HEADS * (HD + 1), T), "t3": (C, T), "a3": (C, T), "w": (1, T), "ws": (1, T), "t4": (C, T)}
PARTS = {"dt_parts": (E, T), "du_parts": (E, T), "qk_parts": (2 * C, T)}


def program(nc, arrays):
    A = {n: nc.dram_tensor(f"in_{n}", a.shape, mybir.dt.from_np(a.dtype), kind="ExternalInput").ap()
         for n, a in arrays.items()}
    A["out"] = nc.dram_tensor("out_0_dram", (C, T), F32, kind="ExternalOutput").ap()
    for n, shape in SCRATCH.items():
        A[n] = nc.dram_tensor(f"mid_{n}", shape, F32).ap()
    for n, shape in PARTS.items():
        A[n] = [nc.dram_tensor(f"mid_{n}{i}", shape, BF16).ap() for i in range(3)]
    A["neg_max"] = nc.dram_tensor("mid_neg_max", (B * HEADS, 2, LP), BF16).ap()
    build(nc, A)


def layouts(v):
    taps = [0, 1, 3, 4, 6, 7, 2, 5, 8]

    def by_tap(w):
        return w.reshape(C, 9, -1)[:, taps].transpose(1, 0, 2).reshape(9 * C, -1)

    def col(a):
        return a.reshape(-1, 1)

    def row(a):
        return a.reshape(1, -1)

    tok = lambda n: v["L0_tok_" + n]
    att = lambda n: v["L0_attn_" + n]
    moe = lambda n: v["L0_ffn_" + n]
    ffn = lambda n: v["L1_ffn_" + n]
    xp, qkv, bqkv = att("x_proj_w"), v["L1_attn_W_qkv"], v["L1_attn_b_qkv"]
    out = {
        "x": v["x"], "tok_W1": by_tap(tok("W1")), "tok_b1": col(tok("b1")),
        "tok_W2": np.pad(by_tap(tok("W2").T).T, ((0, 0), (0, C))), "tok_b2": by_tap(col(tok("b2"))),
        "tok_W3": np.pad(by_tap(tok("W3")), ((0, 0), (0, C))), "tok_b3": col(tok("b3")),
        "norm1_g": col(att("norm1_g")), "norm1_b": col(att("norm1_b")), "norm2_g": col(att("norm2_g")),
        "norm2_b": col(att("norm2_b")), "conv_w": att("conv_w").reshape(C, 3), "conv_b": col(att("conv_b")),
        "in_proj_w": att("in_proj_w").T, "ssm_conv_w": att("ssm_conv_w").reshape(E, 4),
        "ssm_conv_b": col(att("ssm_conv_b")), "xp_dt": xp[:DT_RANK].T,
        "xp_b": np.tile(xp[DT_RANK:DT_RANK + N_STATE].T, (1, 4)), "xp_c": np.tile(xp[DT_RANK + N_STATE:].T, (1, 4)),
        "dt_proj_w": att("dt_proj_w").T, "dt_proj_b": col(att("dt_proj_b")),
        "A_log": att("A_log").reshape(E // 4, 128).T, "Dp": col(att("Dp")), "out_proj_w": att("out_proj_w").T,
        "mlp_w1": att("mlp_w1").T, "mlp_b1": col(att("mlp_b1")), "mlp_w2": att("mlp_w2").T,
        "mlp_b2": col(att("mlp_b2")), "moe_W1": moe("W1"), "moe_b1": col(moe("b1")), "moe_Wg": moe("Wg"),
        "moe_bg": row(moe("bg")), "moe_Wd": moe("Wd").transpose(1, 0, 2).reshape(HID, N_EXP * C),
        "moe_bd": row(moe("bd")), "W_qk": qkv[:, :2 * C], "b_qk": col(bqkv[:2 * C]), "W_v": qkv[:, 2 * C:],
        "b_v": row(bqkv[2 * C:]), "wr": np.pad(ffn("wr"), ((0, 0), (0, 127))), "br": row(ffn("br")), "ffn_w1": ffn("w1"),
        "ffn_b1": col(ffn("b1")), "ffn_w2": ffn("w2"), "ffn_b2": col(ffn("b2")),
    }
    return {k: np.ascontiguousarray(a) for k, a in out.items()}


def kernel(**inputs):
    import numpy as _np
    import concourse.bacc as _bacc
    from ml_dtypes import bfloat16 as _bf16
    from concourse.bass_utils import run_bass_kernel_spmd as _run

    arrays = layouts({k: _np.asarray(a) for k, a in inputs.items()}) | constants(_bf16)
    nc = _bacc.Bacc("TRN2", target_bir_lowering=False, num_devices=1)
    program(nc, arrays)
    r = _run(nc, [{f"in_{n}": a for n, a in arrays.items()}], core_ids=[0])
    out = r.results[0]["out_0_dram"]
    return _np.ascontiguousarray(out.reshape(C, B, L).transpose(1, 2, 0))
```

```python
from contextlib import ExitStack

import concourse.bass as bass
import numpy as np
from concourse import mybir

ALU = mybir.AluOpType
ACT = mybir.ActivationFunctionType
F32 = mybir.dt.float32
BF16 = mybir.dt.bfloat16
U32 = mybir.dt.uint32
AX_X = mybir.AxisListType.X

B, C, IMG = 4, 64, 56
L = IMG * IMG
T = B * L
ROWS = 8
CH = ROWS * IMG
NJ = L // CH
PW = IMG + 2
E, N_STATE, DT_RANK = 128, 32, 4
HID = 256
N_EXP = 8
HEADS, HD = 8, 8
EPS = 1e-5
LEAD = 2


def pairs(eng):
    with eng.Fori(0, 2) as half:
        with eng.Fori(0, NJ) as j:
            yield half * NJ + j, half, j


class Done:

    def __init__(self, sem, lead=LEAD):
        self.sem, self.lead = sem, lead

    def start(self, eng):
        eng.sem_inc(self.sem, self.lead)

    def wait(self, eng, n):
        eng.wait_ge(self.sem, n + (1 + self.lead))

    def wait_free(self, eng, n, depth=None):
        eng.wait_ge(self.sem, n + (1 + self.lead - (depth or self.lead)))


class Order:

    def __init__(self, eng, sem, per_iteration):
        self.eng, self.sem, self.per = eng, sem, per_iteration

    def at(self, iteration):
        self.base, self.k = iteration * self.per, 0

    def __call__(self, ins):
        ins.then_inc(self.sem, 1)
        self.k += 1
        assert self.k <= self.per
        self.eng.wait_ge(self.sem, self.base + self.k)


class Place:

    def __init__(self, nc, stage, ctx, sems):
        self.nc, self.stage, self.ctx, self.sems = nc, stage, ctx, sems

    def sb(self, name, shape, dt=F32):
        return self.ctx.enter_context(self.nc.sbuf_tensor(f"sb_{self.stage}_{name}", shape, dt))

    def bank(self, name, dt=F32):
        return self.ctx.enter_context(self.nc.psum_tensor(f"{self.stage}_{name}", [128, 512], dt))

    def sem(self, name):
        self.sems.append(self.nc.alloc_semaphore(name=f"{self.stage}_{name}"))
        return self.sems[-1]

    def done(self, name, lead=LEAD):
        return Done(self.sem(name), lead)


def pad_image(nc, sems, A):
    with ExitStack() as ctx:
        m = Place(nc, "pad", ctx, sems)
        img = m.sb("img", [128, 2, PW, PW])
        zeroed, loaded, stored = m.sem("zeroed"), m.sem("loaded"), m.sem("stored")
        block = ctx.enter_context(nc.Block())

        @block.vector
        def _(dve):
            dve.memset(img[:], 0.0).then_inc(zeroed, 1)

        @block.sync
        def _(sp):
            sp.wait_ge(zeroed, 1)
            for h in range(2):
                for s in range(2):
                    sp.dma_start(img[C * s:C * s + C, h, 1:1 + IMG, 1:1 + IMG],
                                 A["x"][2 * h + s]).then_inc(loaded, 16)
            sp.wait_ge(loaded, 64)
            for h in range(2):
                sp.dma_start(A["xpad"][2 * h:2 * h + 2].rearrange("b c n -> (b c) n"),
                             img[:, h, :, :].rearrange("p a b -> p (a b)")).then_inc(stored, 16)
            sp.wait_ge(stored, 32)


def tokenize(nc, sems, A):
    NT = 5
    with ExitStack() as ctx:
        m = Place(nc, "tok", ctx, sems)
        w1, w3 = m.sb("w1", [128, NT, C]), m.sb("w3", [128, NT, 128])
        w2, b2 = m.sb("w2", [C, NT * 128]), m.sb("b2", [128, NT])
        b1, b3 = m.sb("b1", [C, 1]), m.sb("b3", [C, 1])
        left, right = m.sb("left", [128, 2, 10 * PW]), m.sb("right", [128, 2, 10 * PW])
        h1 = m.sb("h1", [C, 2, CH])
        gate, gated = m.sb("gate", [128, 2, CH]), m.sb("gated", [128, 2, CH])
        h0 = m.sb("h0", [C, 2, CH])
        psH = [m.bank(f"psH{i}") for i in range(2)]
        psS = [m.bank(f"psS{i}") for i in range(2)]
        psO = [m.bank(f"psO{i}") for i in range(2)]
        w_in = m.sem("w_in")
        patches_in = [m.sem(f"patches_in{p}") for p in range(2)]
        h0_out = [m.sem(f"h0_out{p}") for p in range(2)]
        hidden_mm, hidden, score_mm = m.done("hidden_mm"), m.done("hidden"), m.done("score_mm")
        gates, prods, out_mm, h0_done = m.done("gates"), m.done("prods"), m.done("out_mm", 2 * NT), m.done("h0_done")
        block = ctx.enter_context(nc.Block())
        rows = [128] * 4 + [64]

        def patch(p, k):
            src, off = (left, k * PW) if k < 3 else (right, 0 if k == 3 else 2 * PW)
            v = src[0:rows[k], p, off:off + ROWS * PW]
            return v.rearrange("c (r w) -> c r w", w=PW)[:, :, 0:IMG]

        @block.sync
        def _(sp):
            for k in range(NT):
                r = slice(128 * k, 128 * k + rows[k])
                sp.dma_start(w1[0:rows[k], k, :], A["tok_W1"][r, :]).then_inc(w_in, 16)
                sp.dma_start(w3[0:rows[k], k, :], A["tok_W3"][r, :]).then_inc(w_in, 16)
                sp.dma_start(b2[0:rows[k], k:k + 1], A["tok_b2"][r, :]).then_inc(w_in, 16)
            sp.dma_start(w2[:], A["tok_W2"]).then_inc(w_in, 16)
            sp.dma_start(b1[:], A["tok_b1"]).then_inc(w_in, 16)
            sp.dma_start(b3[:], A["tok_b3"]).then_inc(w_in, 16)
            for it, half, j in pairs(sp):
                for p in range(2):
                    n = it * 2 + p
                    out_mm.wait_free(sp, n * NT + (NT - 1), 2 * NT)
                    base = j * (ROWS * PW)
                    img = A["xpad"].rearrange("b c n -> c b n")
                    for tile, lo, off, ln in ((left, 0, 0, 580), (left, 64, 1, 579),
                                              (right, 0, 2, 578), (right, 64, PW + 2, 520)):
                        sp.dma_start(tile[lo:lo + 64, p, 0:ln],
                                     img[:, half * 2 + p, bass.ds(base + off, ln)]).then_inc(patches_in[p], 16)

        @block.tensor
        def _(pe):
            for d in (hidden_mm, score_mm, out_mm):
                d.start(pe)
            pe.wait_ge(w_in, 16 * 18)
            for it, half, j in pairs(pe):
                for p in range(2):
                    n = it * 2 + p
                    pe.wait_ge(patches_in[p], it * 64 + 64)
                    hidden.wait_free(pe, n)
                    for k in range(NT):
                        mm = pe.matmul(psH[p][0:C, 0:CH], w1[0:rows[k], k, :], patch(p, k),
                                       start=k == 0, stop=k == NT - 1)
                    mm.then_inc(hidden_mm.sem, 1)
                    hidden.wait(pe, n)
                    h0_done.wait_free(pe, n)
                    for k in range(NT + 1):
                        if k < NT:
                            q = n * NT + k
                            s = (p * NT + k) % 2
                            gates.wait_free(pe, q)
                            pe.matmul(psS[s][:, 0:CH], w2[:, 128 * k:128 * k + 128], h1[:, p, :],
                                      start=True, stop=True).then_inc(score_mm.sem, 1)
                        if k:
                            q = n * NT + (k - 1)
                            s = (p * NT + k - 1) % 2
                            prods.wait(pe, q)
                            pe.matmul(psO[p][:, 0:CH], w3[0:rows[k - 1], k - 1, :], gated[0:rows[k - 1], s, :],
                                      start=k == 1, stop=k == NT).then_inc(out_mm.sem, 1)

        @block.scalar
        def _(act):
            for d in (hidden, gates, h0_done):
                d.start(act)
            act.preload_act_table_set("sigmoid_and_others")
            act.wait_ge(w_in, 16 * 18)
            for it, half, j in pairs(act):
                for p in range(2):
                    n = it * 2 + p
                    hidden_mm.wait(act, n)
                    act.activation(h1[:, p, :], psH[p][0:C, 0:CH], ACT.Relu, bias=b1[:]).then_inc(hidden.sem, 1)
                    for k in range(NT):
                        q = n * NT + k
                        s = (p * NT + k) % 2
                        score_mm.wait(act, q)
                        prods.wait_free(act, q)
                        act.activation(gate[0:rows[k], s, :], psS[s][0:rows[k], 0:CH], ACT.Sigmoid,
                                       bias=b2[0:rows[k], k:k + 1]).then_inc(gates.sem, 1)
                    out_mm.wait(act, n * NT + (NT - 1))
                    act.wait_ge(h0_out[p], it * 16)
                    act.activation(h0[:, p, :], psO[p][0:C, 0:CH], ACT.Identity,
                                   bias=b3[:]).then_inc(h0_done.sem, 1)

        @block.vector
        def _(dve):
            prods.start(dve)
            for it, half, j in pairs(dve):
                for p in range(2):
                    n = it * 2 + p
                    dve.wait_ge(patches_in[p], it * 64 + 64)
                    for k in range(NT):
                        q = n * NT + k
                        s = (p * NT + k) % 2
                        gates.wait(dve, q)
                        out_mm.wait_free(dve, q, 2)
                        r = rows[k]
                        dve.tensor_tensor(gated[0:r, s, :].rearrange("c (r w) -> c r w", w=IMG), patch(p, k),
                                          gate[0:r, s, :].rearrange("c (r w) -> c r w", w=IMG),
                                          ALU.mult).then_inc(prods.sem, 1)

        @block.gpsimd
        def _(pool):
            for it, half, j in pairs(pool):
                for p in range(2):
                    h0_done.wait(pool, it * 2 + p)
                    pool.dma_start(A["h0"][:, bass.ds((half * 2 + p) * L + j * CH, CH)],
                                   h0[:, p, :]).then_inc(h0_out[p], 16)
            for p in range(2):
                pool.wait_ge(h0_out[p], 16 * 2 * NJ)


def layer_norm(nc, sems, A, name, src, dst, affine=None, pad=0):
    with ExitStack() as ctx:
        m = Place(nc, name, ctx, sems)
        center, mean = m.sb("center", [128, 128]), m.sb("mean", [128, 128])
        eps, gb, zero = m.sb("eps", [128, 1]), m.sb("gb", [128, 2]), m.sb("zero", [C, 2])
        x, sq, y = m.sb("x", [128, 2, CH]), m.sb("sq", [128, 2, CH]), m.sb("y", [128, 2, CH])
        std, rstd, nrm = m.sb("std", [128, 2, CH]), m.sb("rstd", [128, 2, CH]), m.sb("nrm", [128, 2, CH])
        ps_cen = [m.bank(f"ps_cen{p}") for p in range(2)]
        ps_var = [m.bank(f"ps_var{p}") for p in range(2)]
        w_in, ready = m.sem("w_in"), m.sem("ready")
        x_in = [m.sem(f"x_in{p}") for p in range(2)]
        y_out = [m.sem(f"y_out{p}") for p in range(2)]
        cen_mm, var_mm, squares, stds = m.done("cen_mm"), m.done("var_mm"), m.done("squares"), m.done("stds")
        y_done, steps = m.done("y_done"), m.sem("steps")
        block = ctx.enter_context(nc.Block())
        n_w = 3 if affine is None else 7
        span = L + 2 * pad

        @block.sync
        def _(sp):
            sp.dma_start(center[:], A["c_center"]).then_inc(w_in, 16)
            sp.dma_start(mean[:], A["c_mean"]).then_inc(w_in, 16)
            sp.dma_start(eps[:], A["c_eps"]).then_inc(w_in, 16)
            if affine is not None:
                for i, a in enumerate(affine):
                    for s in range(2):
                        sp.dma_start(gb[C * s:C * s + C, i:i + 1], A[a]).then_inc(w_in, 16)
            with sp.Fori(0, NJ) as j:
                for p in range(2):
                    cen_mm.wait_free(sp, j * 2 + p)
                    for s in range(2):
                        sp.dma_start(x[C * s:C * s + C, p, :],
                                     A[src][:, bass.ds(j * CH + (2 * s + p) * L, CH)]).then_inc(x_in[p], 16)

        @block.tensor
        def _(pe):
            cen_mm.start(pe)
            var_mm.start(pe)
            pe.wait_ge(w_in, 16 * n_w)
            with pe.Fori(0, NJ) as j:
                for p in range(2):
                    pe.wait_ge(x_in[p], j * 32 + 32)
                    y_done.wait_free(pe, j * 2 + p)
                    pe.matmul(ps_cen[p][:, 0:CH], center[:], x[:, p, :], start=True,
                              stop=True).then_inc(cen_mm.sem, 1)
                for p in range(2):
                    squares.wait(pe, j * 2 + p)
                    stds.wait_free(pe, j * 2 + p)
                    pe.matmul(ps_var[p][:, 0:CH], mean[:], sq[:, p, :], start=True,
                              stop=True).then_inc(var_mm.sem, 1)

        @block.scalar
        def _(act):
            squares.start(act)
            stds.start(act)
            act.preload_act_table_set("sqrt_and_others")
            act.wait_ge(w_in, 16 * n_w)
            with act.Fori(0, NJ) as j:
                for p in range(2):
                    cen_mm.wait(act, j * 2 + p)
                    var_mm.wait_free(act, j * 2 + p)
                    act.activation(sq[:, p, :], ps_cen[p][:, 0:CH], ACT.Square).then_inc(squares.sem, 1)
                for p in range(2):
                    var_mm.wait(act, j * 2 + p)
                    y_done.wait_free(act, j * 2 + p)
                    act.activation(std[:, p, :], ps_var[p][:, 0:CH], ACT.Sqrt, bias=eps[:]).then_inc(stds.sem, 1)

        @block.vector
        def _(dve):
            y_done.start(dve)
            if pad:
                dve.memset(zero[:], 0.0).then_inc(ready, 1)
            dve.wait_ge(w_in, 16 * n_w)
            per = 2 if affine is None else 4
            order = Order(dve, steps, per)
            with dve.Fori(0, NJ) as j:
                order.at(j)
                for p in range(2):
                    squares.wait(dve, j * 2 + p)
                    stds.wait(dve, j * 2 + p)
                    order(dve.reciprocal(rstd[:, p, :], std[:, p, :]))
                    dve.wait_ge(y_out[p], j * 32)
                    if affine is None:
                        dve.tensor_tensor(y[:, p, :], ps_cen[p][:, 0:CH], rstd[:, p, :],
                                          ALU.mult).then_inc(y_done.sem, 1)
                    else:
                        order(dve.tensor_tensor(nrm[:, p, :], ps_cen[p][:, 0:CH], rstd[:, p, :], ALU.mult))
                        dve.tensor_scalar(y[:, p, :], nrm[:, p, :], gb[:, 0:1], gb[:, 1:2], ALU.mult,
                                          ALU.add).then_inc(y_done.sem, 1)

        @block.gpsimd
        def _(pool):
            padded = m.sem("padded")
            if pad:
                pool.wait_ge(ready, 1)
                for b in range(B):
                    for at in (b * span, b * span + pad + L):
                        pool.dma_start(A[dst][:, at:at + pad], zero[:, 0:pad],).then_inc(padded, 16)
                pool.wait_ge(padded, 16 * 2 * B)
            with pool.Fori(0, NJ) as j:
                for p in range(2):
                    y_done.wait(pool, j * 2 + p)
                    for s in range(2):
                        pool.dma_start(A[dst][:, bass.ds(j * CH + (2 * s + p) * span + pad, CH)],
                                       y[C * s:C * s + C, p, :]).then_inc(y_out[p], 16)
            for p in range(2):
                pool.wait_ge(y_out[p], 32 * NJ)
def in_projection(nc, sems, A):
    with ExitStack() as ctx:
        m = Place(nc, "inp", ctx, sems)
        cw, cb = m.sb("cw", [C, 3]), m.sb("cb", [C, 1])
        w_in_proj = m.sb("w_in_proj", [C, 2 * E])
        sw, sbias = m.sb("sw", [E, 4]), m.sb("sbias", [E, 1])
        w_b, w_c = m.sb("w_b", [E, 128]), m.sb("w_c", [E, 128])
        w_dtr, w_dt, dt_b = m.sb("w_dtr", [E, DT_RANK]), m.sb("w_dt", [DT_RANK, E]), m.sb("dt_b", [E, 1])
        win = m.sb("win", [C, 2, CH + 2])
        acc = m.sb("acc", [C, 2, CH])
        hc = m.sb("hc", [C, 2, CH])
        xin = m.sb("xin", [E, B, CH + 3])
        cacc = m.sb("cacc", [E, 2, CH])
        u, sz = m.sb("u", [E, 2, CH]), m.sb("sz", [E, 2, CH])
        bb, cc = m.sb("bb", [128, 2, CH]), m.sb("cc", [128, 2, CH])
        dtr, dtp = m.sb("dtr", [DT_RANK, 2, CH]), m.sb("dtp", [E, 2, CH])
        ps_x = [m.bank(f"ps_x{p}") for p in range(2)]
        ps_z = [m.bank(f"ps_z{p}") for p in range(2)]
        ps_b, ps_c, ps_r, ps_d = m.bank("ps_b"), m.bank("ps_c"), m.bank("ps_r"), m.bank("ps_d")
        w_in = m.sem("w_in")
        win_in = [m.sem(f"win_in{p}") for p in range(2)]
        out = [m.sem(f"out{p}") for p in range(2)]
        hc_done, xz_mm, x_read, u_done = m.done("hc_done"), m.done("xz_mm"), m.done("x_read"), m.done("u_done")
        conv_done, z_done = m.done("conv_done"), m.done("z_done")
        bcr_mm, bc_done, dtr_done, dt_mm, dt_done = (m.done("bcr_mm"), m.done("bc_done"), m.done("dtr_done"),
                                                     m.done("dt_mm"), m.done("dt_done"))
        dve_steps, cleared = m.sem("dve_steps"), m.sem("cleared")
        block = ctx.enter_context(nc.Block())
        weights = [(cw, "conv_w"), (cb, "conv_b"), (w_in_proj, "in_proj_w"), (sw, "ssm_conv_w"),
                   (sbias, "ssm_conv_b"), (w_b, "xp_b"), (w_c, "xp_c"), (w_dtr, "xp_dt"),
                   (w_dt, "dt_proj_w"), (dt_b, "dt_proj_b")]
        NW = 16 * len(weights)

        @block.sync
        def _(sp):
            for t, a in weights:
                sp.dma_start(t[:], A[a]).then_inc(w_in, 16)
            with sp.Fori(0, NJ) as j:
                for b in range(B):
                    hc_done.wait_free(sp, j * B + b)
                    sp.dma_start(win[:, b % 2, :],
                                 A["hn"][:, bass.ds(j * CH + b * (L + 4) + 1, CH + 2)]).then_inc(win_in[b % 2], 16)

        @block.vector
        def _(dve):
            for d in (hc_done, x_read, conv_done):
                d.start(dve)
            dve.memset(xin[:, :, CH:CH + 3], 0.0).then_inc(cleared, 1)
            dve.wait_ge(cleared, 1)
            dve.wait_ge(w_in, NW)
            order = Order(dve, dve_steps, 7 * B)
            with dve.Fori(0, NJ) as j:
                order.at(j)
                for b in range(B):
                    p, n = b % 2, j * B + b
                    dve.wait_ge(win_in[p], j * 32 + 16 * (b // 2 + 1))
                    a = acc[:, p, :]
                    order(dve.tensor_scalar(a, win[:, p, 0:CH], cw[:, 0:1], cb[:, 0:1], ALU.mult, ALU.add))
                    order(dve.scalar_tensor_tensor(a, win[:, p, 1:CH + 1], cw[:, 1:2], a, ALU.mult, ALU.add))
                    order(dve.scalar_tensor_tensor(a, win[:, p, 2:CH + 2], cw[:, 2:3], a, ALU.mult, ALU.add))
                    xz_mm.wait_free(dve, n)
                    dve.tensor_tensor(hc[:, p, :], a, win[:, p, 1:CH + 1], ALU.add).then_inc(hc_done.sem, 1)
                    order(dve.tensor_copy(xin[:, b, 0:3], xin[:, b, CH:CH + 3]))
                    xz_mm.wait(dve, n)
                    dve.tensor_copy(xin[:, b, 3:CH + 3], ps_x[p][:, 0:CH]).then_inc(x_read.sem, 1)
                    x_read.wait(dve, n)
                    u_done.wait_free(dve, n)
                    a = cacc[:, p, :]
                    order(dve.tensor_scalar(a, xin[:, b, 0:CH], sw[:, 0:1], sbias[:], ALU.mult, ALU.add))
                    for k in (1, 2):
                        order(dve.scalar_tensor_tensor(a, xin[:, b, k:CH + k], sw[:, k:k + 1], a,
                                                       ALU.mult, ALU.add))
                    dve.scalar_tensor_tensor(a, xin[:, b, 3:CH + 3], sw[:, 3:4], a, ALU.mult,
                                             ALU.add).then_inc(conv_done.sem, 1)

        @block.tensor
        def _(pe):
            for d in (xz_mm, bcr_mm, dt_mm):
                d.start(pe)
            pe.wait_ge(w_in, NW)
            with pe.Fori(0, NJ) as j:
                for b in range(B):
                    p, n = b % 2, j * B + b
                    hc_done.wait(pe, n)
                    x_read.wait_free(pe, n)
                    z_done.wait_free(pe, n)
                    pe.matmul(ps_x[p][:, 0:CH], w_in_proj[:, 0:E], hc[:, p, :], start=True, stop=True)
                    pe.matmul(ps_z[p][:, 0:CH], w_in_proj[:, E:2 * E], hc[:, p, :], start=True,
                              stop=True).then_inc(xz_mm.sem, 1)
                    u_done.wait(pe, n)
                    bc_done.wait_free(pe, n, 1)
                    dtr_done.wait_free(pe, n, 1)
                    pe.matmul(ps_b[:, 0:CH], w_b[:], u[:, p, :], start=True, stop=True)
                    pe.matmul(ps_c[:, 0:CH], w_c[:], u[:, p, :], start=True, stop=True)
                    pe.matmul(ps_r[0:DT_RANK, 0:CH], w_dtr[:], u[:, p, :], start=True,
                              stop=True).then_inc(bcr_mm.sem, 1)
                    dtr_done.wait(pe, n)
                    dt_done.wait_free(pe, n, 1)
                    pe.matmul(ps_d[:, 0:CH], w_dt[:], dtr[:, p, :], start=True, stop=True).then_inc(dt_mm.sem, 1)

        @block.scalar
        def _(act):
            for d in (u_done, z_done, bc_done, dtr_done, dt_done):
                d.start(act)
            act.preload_act_table_set("silu_and_others")
            act.wait_ge(w_in, NW)
            with act.Fori(0, NJ) as j:
                for b in range(B):
                    p, n = b % 2, j * B + b
                    stored = 80 * (j * 2 + b // 2)
                    xz_mm.wait(act, n)
                    act.wait_ge(out[p], stored)
                    act.activation(sz[:, p, :], ps_z[p][:, 0:CH], ACT.Silu).then_inc(z_done.sem, 1)
                    conv_done.wait(act, n)
                    act.activation(u[:, p, :], cacc[:, p, :], ACT.Silu).then_inc(u_done.sem, 1)
                    bcr_mm.wait(act, n)
                    act.activation(dtr[:, p, :], ps_r[0:DT_RANK, 0:CH], ACT.Copy).then_inc(dtr_done.sem, 1)
                    act.activation(bb[:, p, :], ps_b[:, 0:CH], ACT.Copy)
                    act.activation(cc[:, p, :], ps_c[:, 0:CH], ACT.Copy).then_inc(bc_done.sem, 1)
                    dt_mm.wait(act, n)
                    act.activation(dtp[:, p, :], ps_d[:, 0:CH], ACT.Identity, bias=dt_b[:]).then_inc(dt_done.sem, 1)

        @block.gpsimd
        def _(pool):
            with pool.Fori(0, NJ) as j:
                for b in range(B):
                    p, n = b % 2, j * B + b
                    cols = bass.ds(j * CH + b * L, CH)
                    dt_done.wait(pool, n)
                    for t, a in ((sz, "sz"), (u, "u"), (bb, "Bn"), (cc, "Cn"), (dtp, "dtp")):
                        pool.dma_start(A[a][:, cols], t[:, p, :]).then_inc(out[p], 16)
            for p in range(2):
                pool.wait_ge(out[p], 80 * 2 * NJ)


def step_sizes(nc, sems, A):
    with ExitStack() as ctx:
        m = Place(nc, "dts", ctx, sems)
        x, u = m.sb("x", [E, 2, CH]), m.sb("u", [E, 2, CH])
        e, w, lw = m.sb("e", [E, 2, CH]), m.sb("w", [E, 2, CH]), m.sb("lw", [E, 2, CH])
        one, den = m.sb("one", [E, CH]), m.sb("den", [E, CH])
        val = m.sb("val", [E, 2, CH])
        rest = m.sb("rest", [E, 2, CH])
        parts = m.sb("parts", [E, 2, 2, 3, CH], BF16)
        x_in = [m.sem(f"x_in{p}") for p in range(2)]
        out = [m.sem(f"out{p}") for p in range(2)]
        e_done, w_done, l_done, all_done = m.done("e_done"), m.done("w_done"), m.done("l_done"), m.done("all_done")
        act_steps, dve_steps = m.sem("act_steps"), m.sem("dve_steps")
        block = ctx.enter_context(nc.Block())

        @block.sync
        def _(sp):
            with sp.Fori(0, T // CH // 2) as k:
                for p in range(2):
                    all_done.wait_free(sp, k * 2 + p)
                    for t, a in ((x, "dtp"), (u, "u")):
                        sp.dma_start(t[:, p, :], A[a][:, bass.ds(k * (2 * CH) + p * CH, CH)]).then_inc(x_in[p], 16)

        @block.scalar
        def _(act):
            e_done.start(act)
            l_done.start(act)
            act.preload_act_table_set("natural_log_exp_and_others")
            order = Order(act, act_steps, 2)
            with act.Fori(0, T // CH // 2) as k:
                order.at(k)
                for p in range(2):
                    act.wait_ge(x_in[p], k * 32 + 32)
                    all_done.wait_free(act, k * 2 + p)
                    order(act.activation(e[:, p, :], x[:, p, :], ACT.Abs))
                    act.activation(e[:, p, :], e[:, p, :], ACT.Exp, scale=-1.0).then_inc(e_done.sem, 1)
                for p in range(2):
                    w_done.wait(act, k * 2 + p)
                    act.activation(lw[:, p, :], w[:, p, :], ACT.Ln).then_inc(l_done.sem, 1)

        @block.vector
        def _(dve):
            w_done.start(dve)
            all_done.start(dve)
            order = Order(dve, dve_steps, 22)
            with dve.Fori(0, T // CH // 2) as k:
                order.at(k)
                for p in range(2):
                    e_done.wait(dve, k * 2 + p)
                    dve.tensor_scalar(w[:, p, :], e[:, p, :], 1.0, None, ALU.add).then_inc(w_done.sem, 1)
                for p in range(2):
                    w_done.wait(dve, k * 2 + p)
                    order(dve.tensor_scalar(one[:], w[:, p, :], 1.0, None, ALU.is_equal))
                    order(dve.scalar_tensor_tensor(den[:], w[:, p, :], -1.0, one[:], ALU.add, ALU.add))
                    order(dve.reciprocal(den[:], den[:]))
                    l_done.wait(dve, k * 2 + p)
                    order(dve.tensor_tensor(one[:], lw[:, p, :], one[:], ALU.add))
                    order(dve.tensor_tensor(one[:], one[:], den[:], ALU.mult))
                    order(dve.tensor_tensor(one[:], one[:], e[:, p, :], ALU.mult))
                    order(dve.scalar_tensor_tensor(val[:, 0, :], x[:, p, :], 0.0, one[:], ALU.max, ALU.add))
                    order(dve.tensor_tensor(val[:, 1, :], val[:, 0, :], u[:, p, :], ALU.mult))
                    dve.wait_ge(out[p], k * 96)
                    order(dve.tensor_copy(parts[:, p, :, 0, :], val[:]))
                    order(dve.tensor_tensor(rest[:], val[:], parts[:, p, :, 0, :], ALU.subtract))
                    order(dve.tensor_copy(parts[:, p, :, 1, :], rest[:]))
                    dve.tensor_tensor(parts[:, p, :, 2, :], rest[:], parts[:, p, :, 1, :],
                                      ALU.subtract).then_inc(all_done.sem, 1)

        @block.gpsimd
        def _(pool):
            with pool.Fori(0, T // CH // 2) as k:
                for p in range(2):
                    all_done.wait(pool, k * 2 + p)
                    for v, a in enumerate(("dt_parts", "du_parts")):
                        for i in range(3):
                            pool.dma_start(A[a][i][:, bass.ds(k * (2 * CH) + p * CH, CH)],
                                           parts[:, p, v, i, :]).then_inc(out[p], 16)
            for p in range(2):
                pool.wait_ge(out[p], 96 * (T // CH // 2))


def selective_scan(nc, sems, A):
    G = E // DT_RANK
    order_of = [8 * (i % 4) + i // 4 for i in range(G)]
    with ExitStack() as ctx:
        m = Place(nc, "scan", ctx, sems)
        sel = m.sb("sel", [96, 8, 128], BF16)
        ysel = m.sb("ysel", [128, 8, 32])
        a_neg, dp = m.sb("a_neg", [128, G]), m.sb("dp", [E, 1])
        dtq, duq = m.sb("dtq", [96, 2, 4, CH], BF16), m.sb("duq", [96, 2, 4, CH], BF16)
        bn, cn = m.sb("bn", [128, 2, CH]), m.sb("cn", [128, 2, CH])
        u, sz = m.sb("u", [E, 2, CH]), m.sb("sz", [E, 2, CH])
        last = m.sb("last", [128, B * G])
        decay = m.sb("decay", [128, 4, CH])
        drive = m.sb("drive", [128, 4, CH])
        h = m.sb("h", [128, 4, CH])
        ch = m.sb("ch", [128, 4, CH])
        y1, yz = m.sb("y1", [E, 2, CH]), m.sb("yz", [E, 2, CH])
        ps_dt = [m.bank(f"ps_dt{i}") for i in range(2)]
        ps_du = [m.bank(f"ps_du{i}") for i in range(4)]
        ps_y = [m.bank(f"ps_y{i}") for i in range(2)]
        w_in, a_ready, cleared = m.sem("w_in"), m.sem("a_ready"), m.sem("cleared")
        c_in = [m.sem(f"c_in{p}") for p in range(2)]
        out = [m.sem(f"out{p}") for p in range(2)]
        spread, driven, decays = m.done("spread"), m.done("driven", 4), m.done("decays")
        scans, weighted, y_mm = m.done("scans", 4), m.done("weighted", 4), m.done("y_mm", 4)
        kept = m.done("kept", B * G)
        y_done, steps = m.done("y_done"), m.sem("steps")
        block = ctx.enter_context(nc.Block())

        @block.sync
        def _(sp):
            for t, a in ((sel, "c_sel"), (ysel, "c_ysel"), (a_neg, "A_log"), (dp, "Dp")):
                sp.dma_start(t[:], A[a]).then_inc(w_in, 16)
            with sp.Fori(0, NJ) as j:
                for b in range(B):
                    p, n = b % 2, j * B + b
                    cols = bass.ds(j * CH + b * L, CH)
                    y_done.wait_free(sp, n)
                    for i in range(3):
                        for t, a in ((dtq, "dt_parts"), (duq, "du_parts")):
                            sp.dma_start(t[32 * i:32 * i + 32, p, :, :],
                                         A[a][i].rearrange("(q r) t -> r q t", r=32)[:, :, cols]).then_inc(c_in[p], 16)
                    for t, a in ((bn, "Bn"), (cn, "Cn"), (u, "u"), (sz, "sz")):
                        sp.dma_start(t[:, p, :], A[a][:, cols]).then_inc(c_in[p], 16)

        @block.tensor
        def _(pe):
            spread.start(pe)
            y_mm.start(pe)
            pe.wait_ge(w_in, 64)
            with pe.Fori(0, NJ) as j:
                for b in range(B):
                    p, n = b % 2, j * B + b
                    pe.wait_ge(c_in[p], (j * 2 + b // 2 + 1) * 160)
                    y_done.wait_free(pe, n)
                    for i in range(G + 3):
                        if i < G:
                            s = n * G + i
                            g = order_of[i]
                            decays.wait_free(pe, s)
                            driven.wait_free(pe, s)
                            pe.matmul(ps_dt[i % 2][:, 0:CH], sel[:, g % 8, :], dtq[:, p, g // 8, :],
                                      start=True, stop=True)
                            pe.matmul(ps_du[i % 4][:, 0:CH], sel[:, g % 8, :], duq[:, p, g // 8, :],
                                      start=True, stop=True).then_inc(spread.sem, 1)
                        if i >= 3:
                            s, i2 = n * G + (i - 3), i - 3
                            g = order_of[i2]
                            q, r = g // 8, g % 8
                            weighted.wait(pe, s)
                            pe.matmul(ps_y[p][32 * q:32 * q + 32, 0:CH], ysel[:, r, :], ch[:, i2 % 4, :],
                                      start=r == 0, stop=r == 7, tile_position=(0, 32 * q)).then_inc(y_mm.sem, 1)

        @block.scalar
        def _(act):
            decays.start(act)
            act.preload_act_table_set("natural_log_exp_and_others")
            act.wait_ge(w_in, 64)
            act.activation(a_neg[:], a_neg[:], ACT.Exp).then_inc(a_ready, 1)
            act.wait_ge(a_ready, 1)
            act.mul(a_neg[:], a_neg[:], -1.0).then_inc(a_ready, 1)
            act.wait_ge(a_ready, 2)
            act.wait_ge(cleared, 1)
            kept.start(act)
            with act.Fori(0, NJ) as j:
                for b in range(B):
                    n = j * B + b
                    for i in range(G + 2):
                        if i < G:
                            s = n * G + i
                            g = order_of[i]
                            spread.wait(act, s)
                            scans.wait_free(act, s, 4)
                            act.activation(decay[:, i % 4, :], ps_dt[i % 2][:, 0:CH], ACT.Exp,
                                           scale=a_neg[:, g:g + 1]).then_inc(decays.sem, 1)
                        if i >= 2:
                            scans.wait(act, n * G + (i - 2))
                            act.activation(last[:, b * G + i - 2:b * G + i - 1], h[:, (i - 2) % 4, CH - 1:CH],
                                           ACT.Copy).then_inc(kept.sem, 1)

        @block.vector
        def _(dve):
            for d in (driven, scans, y_done):
                d.start(dve)
            dve.memset(last[:], 0.0).then_inc(cleared, 1)
            dve.wait_ge(w_in, 64)
            order = Order(dve, steps, B)
            with dve.Fori(0, NJ) as j:
                order.at(j)
                for b in range(B):
                    p, n = b % 2, j * B + b
                    dve.wait_ge(c_in[p], (j * 2 + b // 2 + 1) * 160)
                    for i in range(G + 1):
                        if i < G:
                            s = n * G + i
                            spread.wait(dve, s)
                            scans.wait_free(dve, s, 4)
                            dve.tensor_tensor(drive[:, i % 4, :], ps_du[i % 4][:, 0:CH], bn[:, p, :],
                                              ALU.mult).then_inc(driven.sem, 1)
                        if i >= 1:
                            i2 = i - 1
                            s = n * G + i2
                            driven.wait(dve, s)
                            decays.wait(dve, s)
                            kept.wait_free(dve, s, B * G)
                            weighted.wait_free(dve, s, 4)
                            dve.tensor_tensor_scan(h[:, i2 % 4, :], decay[:, i2 % 4, :], drive[:, i2 % 4, :],
                                                   last[:, b * G + i2:b * G + i2 + 1], ALU.mult,
                                                   ALU.add).then_inc(scans.sem, 1)
                    y_mm.wait(dve, n * G + (G - 1))
                    order(dve.scalar_tensor_tensor(y1[:, p, :], u[:, p, :], dp[:], ps_y[p][:, 0:CH],
                                                   ALU.mult, ALU.add))
                    dve.wait_ge(out[p], (j * 2 + b // 2) * 16)
                    dve.tensor_tensor(yz[:, p, :], y1[:, p, :], sz[:, p, :], ALU.mult).then_inc(y_done.sem, 1)

        @block.gpsimd
        def _(pool):
            weighted.start(pool)
            with pool.Fori(0, NJ) as j:
                for b in range(B):
                    p, n = b % 2, j * B + b
                    for i in range(G):
                        s = n * G + i
                        scans.wait(pool, s)
                        y_mm.wait_free(pool, s, 4)
                        pool.tensor_tensor(ch[:, i % 4, :], h[:, i % 4, :], cn[:, p, :],
                                           ALU.mult).then_inc(weighted.sem, 1)
                    y_done.wait(pool, n)
                    pool.dma_start(A["yz"][:, bass.ds(j * CH + b * L, CH)], yz[:, p, :]).then_inc(out[p], 16)
            for p in range(2):
                pool.wait_ge(out[p], 16 * 2 * NJ)
def out_projection(nc, sems, A):
    with ExitStack() as ctx:
        m = Place(nc, "outp", ctx, sems)
        w = m.sb("w", [E, C])
        yz, h0, h1 = m.sb("yz", [E, 2, CH]), m.sb("h0", [C, 2, CH]), m.sb("h1", [C, 2, CH])
        ps = [m.bank(f"ps{p}") for p in range(2)]
        w_in = m.sem("w_in")
        x_in = [m.sem(f"x_in{p}") for p in range(2)]
        out = [m.sem(f"out{p}") for p in range(2)]
        mm, added = m.done("mm"), m.done("added")
        block = ctx.enter_context(nc.Block())

        @block.sync
        def _(sp):
            sp.dma_start(w[:], A["out_proj_w"]).then_inc(w_in, 16)
            with sp.Fori(0, T // CH // 2) as k:
                for p in range(2):
                    added.wait_free(sp, k * 2 + p)
                    for t, a in ((yz, "yz"), (h0, "h0")):
                        sp.dma_start(t[:, p, :], A[a][:, bass.ds(k * (2 * CH) + p * CH, CH)]).then_inc(x_in[p], 16)

        @block.tensor
        def _(pe):
            mm.start(pe)
            pe.wait_ge(w_in, 16)
            with pe.Fori(0, T // CH // 2) as k:
                for p in range(2):
                    pe.wait_ge(x_in[p], k * 32 + 32)
                    added.wait_free(pe, k * 2 + p)
                    pe.matmul(ps[p][0:C, 0:CH], w[:], yz[:, p, :], start=True, stop=True).then_inc(mm.sem, 1)

        @block.vector
        def _(dve):
            added.start(dve)
            with dve.Fori(0, T // CH // 2) as k:
                for p in range(2):
                    dve.wait_ge(x_in[p], k * 32 + 32)
                    dve.wait_ge(out[p], k * 16)
                    mm.wait(dve, k * 2 + p)
                    dve.tensor_tensor(h1[:, p, :], ps[p][0:C, 0:CH], h0[:, p, :], ALU.add).then_inc(added.sem, 1)

        @block.gpsimd
        def _(pool):
            with pool.Fori(0, T // CH // 2) as k:
                for p in range(2):
                    added.wait(pool, k * 2 + p)
                    pool.dma_start(A["h1"][:, bass.ds(k * (2 * CH) + p * CH, CH)], h1[:, p, :]).then_inc(out[p], 16)
            for p in range(2):
                pool.wait_ge(out[p], 16 * (T // CH // 2))


def mlp(nc, sems, A, name, src, adds, dst, weights, func, table, gate=None):
    NA = len(adds)
    with ExitStack() as ctx:
        m = Place(nc, name, ctx, sems)
        w1, w2 = m.sb("w1", [C, HID]), m.sb("w2", [128, 2, C])
        b1, b2 = m.sb("b1", [128, 2]), m.sb("b2", [C, 1])
        ones = m.sb("ones", [1, C])
        x, more = m.sb("x", [C, 2, CH]), m.sb("more", [C, 2, NA, CH])
        g, gs = m.sb("g", [1, 2, CH]), m.sb("gs", [C, 2, CH])
        hid = m.sb("hid", [128, 2, 2, CH])
        y1, y2 = m.sb("y1", [C, 2, CH]), m.sb("y2", [C, 2, CH])
        ps_h = [[m.bank(f"ps_h{p}{i}") for i in range(2)] for p in range(2)]
        ps_y = [m.bank(f"ps_y{p}") for p in range(2)]
        ps_g = m.bank("ps_g")
        w_in, filled = m.sem("w_in"), m.sem("filled")
        x_in = [m.sem(f"x_in{p}") for p in range(2)]
        out = [m.sem(f"out{p}") for p in range(2)]
        hid_mm, hidden, y_mm, y_done = m.done("hid_mm"), m.done("hidden"), m.done("y_mm"), m.done("y_done")
        gate_mm, gates, steps = m.done("gate_mm"), m.done("gates"), m.sem("steps")
        block = ctx.enter_context(nc.Block())
        n_in = 16 * (1 + NA + (gate is not None))
        K = T // CH // 2

        @block.sync
        def _(sp):
            for t, a in ((w1, weights[0]), (b2, weights[3])):
                sp.dma_start(t[:], A[a]).then_inc(w_in, 16)
            for i in range(2):
                sp.dma_start(b1[:, i:i + 1], A[weights[1]][128 * i:128 * i + 128, :]).then_inc(w_in, 16)
                sp.dma_start(w2[:, i, :], A[weights[2]][128 * i:128 * i + 128, :]).then_inc(w_in, 16)
            with sp.Fori(0, K) as k:
                for p in range(2):
                    cols = bass.ds(k * (2 * CH) + p * CH, CH)
                    y_done.wait_free(sp, k * 2 + p)
                    sp.dma_start(x[:, p, :], A[src][:, cols]).then_inc(x_in[p], 16)
                    for i, a in enumerate(adds):
                        sp.dma_start(more[:, p, i, :], A[a][:, cols]).then_inc(x_in[p], 16)
                    if gate is not None:
                        sp.dma_start(g[:, p, :], A[gate][:, cols]).then_inc(x_in[p], 16)

        @block.tensor
        def _(pe):
            for d in (hid_mm, y_mm, gate_mm):
                d.start(pe)
            pe.wait_ge(w_in, 16 * 6)
            if gate is not None:
                pe.wait_ge(filled, 1)
            with pe.Fori(0, K) as k:
                for p in range(2):
                    n = k * 2 + p
                    pe.wait_ge(x_in[p], k * n_in + n_in)
                    hidden.wait_free(pe, n)
                    for i in range(2):
                        mm = pe.matmul(ps_h[p][i][:, 0:CH], w1[:, 128 * i:128 * i + 128], x[:, p, :],
                                       start=True, stop=True)
                    mm.then_inc(hid_mm.sem, 1)
                    if gate is not None:
                        gates.wait_free(pe, n, 1)
                        pe.matmul(ps_g[0:C, 0:CH], ones[:], g[:, p, :], start=True, stop=True).then_inc(gate_mm.sem, 1)
                for p in range(2):
                    n = k * 2 + p
                    hidden.wait(pe, n)
                    y_done.wait_free(pe, n)
                    for i in range(2):
                        mm = pe.matmul(ps_y[p][0:C, 0:CH], w2[:, i, :], hid[:, p, i, :], start=i == 0, stop=i == 1)
                    mm.then_inc(y_mm.sem, 1)

        @block.scalar
        def _(act):
            hidden.start(act)
            gates.start(act)
            act.preload_act_table_set(table)
            act.wait_ge(w_in, 16 * 6)
            with act.Fori(0, K) as k:
                for p in range(2):
                    n = k * 2 + p
                    hid_mm.wait(act, n)
                    y_mm.wait_free(act, n)
                    for i in range(2):
                        a = act.activation(hid[:, p, i, :], ps_h[p][i][:, 0:CH], func, bias=b1[:, i:i + 1])
                    a.then_inc(hidden.sem, 1)
                    if gate is not None:
                        gate_mm.wait(act, n)
                        y_done.wait_free(act, n)
                        act.activation(gs[:, p, :], ps_g[0:C, 0:CH], ACT.Copy).then_inc(gates.sem, 1)

        @block.vector
        def _(dve):
            y_done.start(dve)
            if gate is not None:
                dve.memset(ones[:], 1.0).then_inc(filled, 1)
            dve.wait_ge(w_in, 16 * 6)
            per = 1 + (gate is not None) + (NA - 1)
            order = Order(dve, steps, 2 * per)
            with dve.Fori(0, K) as k:
                order.at(k)
                for p in range(2):
                    n = k * 2 + p
                    y_mm.wait(dve, n)
                    order(dve.tensor_scalar(y1[:, p, :], ps_y[p][0:C, 0:CH], b2[:], None, ALU.add))
                    if gate is not None:
                        gates.wait(dve, n)
                        order(dve.tensor_tensor(y1[:, p, :], y1[:, p, :], gs[:, p, :], ALU.mult))
                    for i in range(NA - 1):
                        order(dve.tensor_tensor(y1[:, p, :], y1[:, p, :], more[:, p, i, :], ALU.add))
                    dve.wait_ge(out[p], k * 16)
                    dve.tensor_tensor(y2[:, p, :], y1[:, p, :], more[:, p, NA - 1, :], ALU.add).then_inc(y_done.sem, 1)

        @block.gpsimd
        def _(pool):
            with pool.Fori(0, K) as k:
                for p in range(2):
                    y_done.wait(pool, k * 2 + p)
                    pool.dma_start(A[dst][:, bass.ds(k * (2 * CH) + p * CH, CH)], y2[:, p, :]).then_inc(out[p], 16)
            for p in range(2):
                pool.wait_ge(out[p], 16 * K)


def experts(nc, sems, A):
    TT, NTT = 112, 4
    with ExitStack() as ctx:
        m = Place(nc, "moe", ctx, sems)
        w1, b1 = m.sb("w1", [C, HID]), m.sb("b1", [128, 2])
        wg, bg = m.sb("wg", [128, 2, N_EXP]), m.sb("bg", [1, N_EXP])
        wd, bd = m.sb("wd", [128, 2, N_EXP * C]), m.sb("bd", [1, N_EXP * C])
        ones, ident = m.sb("ones", [1, TT]), m.sb("ident", [128, 128])
        rank = m.sb("rank", [TT, NTT, N_EXP])
        x, hid = m.sb("x", [C, 2, CH]), m.sb("hid", [128, 2, 2, CH])
        mx, sh, ex = m.sb("mx", [TT, NTT]), m.sb("sh", [TT, NTT, N_EXP]), m.sb("ex", [TT, NTT, N_EXP])
        sm, pm, first = m.sb("sm", [TT, NTT]), m.sb("pm", [TT, NTT]), m.sb("first", [TT, NTT])
        eq, wt = m.sb("eq", [TT, NTT, N_EXP]), m.sb("wt", [TT, NTT, N_EXP])
        picked, o = m.sb("picked", [TT, 2, N_EXP, C]), m.sb("o", [TT, 2, NTT, C])
        t2 = m.sb("t2", [C, 2, CH])
        ps_h = [m.bank(f"ps_h{i}") for i in range(2)]
        ps_l, ps_t = m.bank("ps_l"), [m.bank(f"ps_t{i}") for i in range(2)]
        ps_y = [m.bank(f"ps_y{i}") for i in range(2)]
        w_in, filled = m.sem("w_in"), m.sem("filled")
        x_in = [m.sem(f"x_in{p}") for p in range(2)]
        out = [m.sem(f"out{p}") for p in range(2)]
        hid_mm, hidden, logit_mm, shifted, exps = (m.done("hid_mm"), m.done("hidden"), m.done("logit_mm"),
                                                   m.done("shifted"), m.done("exps"))
        y_mm, y_read, wt_done, reduced, o_mm, t2_done = (m.done("y_mm"), m.done("y_read"), m.done("wt_done"),
                                                         m.done("reduced"), m.done("o_mm"), m.done("t2_done"))
        steps = m.sem("steps")
        block = ctx.enter_context(nc.Block())
        K = T // CH // 2
        NW = 16 * 11

        def bcast(a):
            return a.unsqueeze(2).broadcast_to([TT, NTT, N_EXP])

        @block.sync
        def _(sp):
            for t, a in ((w1, "moe_W1"), (bg, "moe_bg"), (bd, "moe_bd"), (ident, "c_ident"),
                         (rank, "c_rank")):
                sp.dma_start(t[:], A[a]).then_inc(w_in, 16)
            for i in range(2):
                r = slice(128 * i, 128 * i + 128)
                sp.dma_start(b1[:, i:i + 1], A["moe_b1"][r, :]).then_inc(w_in, 16)
                sp.dma_start(wg[:, i, :], A["moe_Wg"][r, :]).then_inc(w_in, 16)
                sp.dma_start(wd[:, i, :], A["moe_Wd"][r, :]).then_inc(w_in, 16)
            with sp.Fori(0, K) as k:
                for p in range(2):
                    t2_done.wait_free(sp, k * 2 + p)
                    sp.dma_start(x[:, p, :], A["a1"][:, bass.ds(k * (2 * CH) + p * CH, CH)]).then_inc(x_in[p], 16)

        @block.tensor
        def _(pe):
            for d in (hid_mm, logit_mm, y_mm, o_mm):
                d.start(pe)
            pe.wait_ge(w_in, NW)
            pe.wait_ge(filled, 1)
            with pe.Fori(0, K) as k:
                for p in range(2):
                    n = k * 2 + p
                    pe.wait_ge(x_in[p], k * 16 + 16)
                    hidden.wait_free(pe, n, 1)
                    for i in range(2):
                        mm = pe.matmul(ps_h[i][:, 0:CH], w1[:, 128 * i:128 * i + 128], x[:, p, :],
                                       start=True, stop=True)
                    mm.then_inc(hid_mm.sem, 1)
                    hidden.wait(pe, n)
                    shifted.wait_free(pe, n, 1)
                    for t in range(NTT):
                        tok = slice(TT * t, TT * t + TT)
                        dst = ps_l[0:TT, N_EXP * t:N_EXP * t + N_EXP]
                        for i in range(2):
                            pe.matmul(dst, hid[:, p, i, tok], wg[:, i, :], start=i == 0, stop=False)
                        mm = pe.matmul(dst, ones[:], bg[:], start=False, stop=True)
                    mm.then_inc(logit_mm.sem, 1)
                    for t in range(NTT):
                        tok = slice(TT * t, TT * t + TT)
                        y_read.wait_free(pe, n * NTT + t)
                        for i in range(2):
                            pe.matmul(ps_y[t % 2][0:TT, :], hid[:, p, i, tok], wd[:, i, :], start=i == 0, stop=False)
                        pe.matmul(ps_y[t % 2][0:TT, :], ones[:], bd[:], start=False, stop=True).then_inc(y_mm.sem, 1)
                    reduced.wait(pe, n * NTT + (NTT - 1))
                    t2_done.wait_free(pe, n)
                    for t in range(NTT):
                        mm = pe.matmul(ps_t[p][0:C, TT * t:TT * t + TT], o[:, p, t, :], ident[0:TT, 0:TT],
                                       start=True, stop=True)
                    mm.then_inc(o_mm.sem, 1)

        @block.scalar
        def _(act):
            hidden.start(act)
            exps.start(act)
            act.wait_ge(w_in, NW)
            with act.Fori(0, K) as k:
                for p in range(2):
                    n = k * 2 + p
                    hid_mm.wait(act, n)
                    for i in range(2):
                        a = act.activation(hid[:, p, i, :], ps_h[i][:, 0:CH], ACT.Gelu, bias=b1[:, i:i + 1])
                    a.then_inc(hidden.sem, 1)
                    shifted.wait(act, n)
                    act.activation(ex[:], sh[:], ACT.Exp).then_inc(exps.sem, 1)

        @block.vector
        def _(dve):
            for d in (shifted, y_read, wt_done, reduced, t2_done):
                d.start(dve)
            dve.memset(ones[:], 1.0).then_inc(filled, 1)
            dve.wait_ge(w_in, NW)
            order = Order(dve, steps, 2 * 9)
            with dve.Fori(0, K) as k:
                order.at(k)
                for p in range(2):
                    n = k * 2 + p
                    logit_mm.wait(dve, n)
                    logits = ps_l[0:TT, 0:NTT * N_EXP].rearrange("p (t e) -> p t e", e=N_EXP)
                    order(dve.reduce_max(mx[:], logits, AX_X))
                    dve.tensor_tensor(sh[:], logits, bcast(mx[:]), ALU.subtract).then_inc(shifted.sem, 1)
                    exps.wait(dve, n)
                    order(dve.reduce_sum(sm[:], ex[:], AX_X))
                    order(dve.reciprocal(sm[:], sm[:]))
                    order(dve.reduce_max(mx[:], ex[:], AX_X))
                    order(dve.tensor_tensor(eq[:], ex[:], bcast(mx[:]), ALU.is_ge))
                    order(dve.tensor_tensor(eq[:], eq[:], rank[:], ALU.mult))
                    order(dve.reduce_max(first[:], eq[:], AX_X))
                    order(dve.tensor_tensor(eq[:], eq[:], bcast(first[:]), ALU.is_equal))
                    order(dve.tensor_tensor(pm[:], mx[:], sm[:], ALU.mult))
                    dve.tensor_tensor(wt[:], eq[:], bcast(pm[:]), ALU.mult).then_inc(wt_done.sem, 1)
                    wt_done.wait(dve, n)
                    for t in range(NTT + 1):
                        if t < NTT:
                            y_mm.wait(dve, n * NTT + t)
                            reduced.wait_free(dve, n * NTT + t)
                            dve.tensor_tensor(picked[:, t % 2, :, :],
                                              ps_y[t % 2][0:TT, :].rearrange("p (e c) -> p e c", c=C),
                                              wt[:, t, :].unsqueeze(2).broadcast_to([TT, N_EXP, C]),
                                              ALU.mult).then_inc(y_read.sem, 1)
                        if t:
                            t1 = t - 1
                            y_read.wait(dve, n * NTT + t1)
                            if t == 1:
                                o_mm.wait_free(dve, n)
                            dve.reduce_sum(o[:, p, t1, :], picked[:, t1 % 2, :, :].rearrange("p e c -> p c e"),
                                           AX_X).then_inc(reduced.sem, 1)
                    dve.wait_ge(out[p], k * 16)
                    o_mm.wait(dve, n)
                    dve.tensor_tensor(t2[:, p, :], ps_t[p][0:C, 0:CH], x[:, p, :], ALU.add).then_inc(t2_done.sem, 1)

        @block.gpsimd
        def _(pool):
            with pool.Fori(0, K) as k:
                for p in range(2):
                    t2_done.wait(pool, k * 2 + p)
                    pool.dma_start(A["t2"][:, bass.ds(k * (2 * CH) + p * CH, CH)], t2[:, p, :]).then_inc(out[p], 16)
            for p in range(2):
                pool.wait_ge(out[p], 16 * K)
KT = 128
NKT = -(-L // KT)
LP = NKT * KT
PROD = 6 * HD
ROW_TOP, ROW_MAX = PROD, PROD + 1
KROWS = PROD + 3
STAIR = 1664
SCALE = HD ** -0.5
MAX_SCORE = 400.0
I32 = mybir.dt.int32


def qkv_parts(nc, sems, A):
    with ExitStack() as ctx:
        m = Place(nc, "qk", ctx, sems)
        w, b, sc = m.sb("w", [C, 2 * C]), m.sb("b", [2 * C, 1]), m.sb("sc", [2 * C, 1])
        x = m.sb("x", [C, 2, CH])
        qk, rest = m.sb("qk", [2 * C, 2, CH]), m.sb("rest", [2 * C, 2, CH])
        parts = m.sb("parts", [2 * C, 2, 3, CH], BF16)
        ps = [m.bank(f"ps{p}") for p in range(2)]
        w_in, steps = m.sem("w_in"), m.sem("steps")
        x_in = [m.sem(f"x_in{p}") for p in range(2)]
        out = [m.sem(f"out{p}") for p in range(2)]
        mm, read, split = m.done("mm"), m.done("read"), m.done("split")
        ident_f, now, peak = m.sb("ident", [128, 128]), m.sb("now", [128, 2]), m.sb("peak", [128, 1])
        both, flag = m.sb("both", [1, 2]), m.sb("flag", [1, 1], I32)
        ps_peak = m.bank("ps_peak")
        peaks, turned, flagged, stored = m.sem("peaks"), m.sem("turned"), m.sem("flagged"), m.sem("stored")
        block = ctx.enter_context(nc.Block())
        K = T // CH // 2

        @block.sync
        def _(sp):
            for t, a in ((w, "W_qk"), (b, "b_qk"), (sc, "c_qscale"), (ident_f, "c_ident")):
                sp.dma_start(t[:], A[a]).then_inc(w_in, 16)
            for k, half, j in pairs(sp):
                for p in range(2):
                    mm.wait_free(sp, k * 2 + p)
                    sp.dma_start(x[:, p, :], A["a2"][:, bass.ds((half * 2 + p) * L + j * CH, CH)]).then_inc(x_in[p], 16)
            sp.wait_ge(flagged, 4)
            sp.dma_start(A["masks_vanish"], flag[:]).then_inc(stored, 16)
            sp.wait_ge(stored, 16)

        @block.tensor
        def _(pe):
            mm.start(pe)
            pe.wait_ge(w_in, 64)
            for k, half, j in pairs(pe):
                for p in range(2):
                    pe.wait_ge(x_in[p], k * 16 + 16)
                    read.wait_free(pe, k * 2 + p)
                    pe.matmul(ps[p][:, 0:CH], w[:], x[:, p, :], start=True, stop=True).then_inc(mm.sem, 1)
            pe.wait_ge(peaks, T // CH + 1)
            pe.matmul(ps_peak[0:1, 0:2 * C], peak[:], ident_f[:], start=True, stop=True).then_inc(turned, 1)

        @block.vector
        def _(dve):
            read.start(dve)
            split.start(dve)
            dve.memset(peak[:], 0.0).then_inc(peaks, 1)
            dve.wait_ge(w_in, 64)
            order = Order(dve, steps, 8)
            for k, half, j in pairs(dve):
                order.at(k)
                for p in range(2):
                    n = k * 2 + p
                    mm.wait(dve, n)
                    dve.tensor_scalar(qk[:, p, :], ps[p][:, 0:CH], b[:], sc[:], ALU.add, ALU.mult).then_inc(read.sem, 1)
                    dve.wait_ge(out[p], k * 96)
                    read.wait(dve, n)
                    order(dve.tensor_copy(parts[:, p, 0, :], qk[:, p, :]))
                    order(dve.tensor_tensor(rest[:, p, :], qk[:, p, :], parts[:, p, 0, :], ALU.subtract))
                    order(dve.tensor_copy(parts[:, p, 1, :], rest[:, p, :]))
                    dve.tensor_tensor(parts[:, p, 2, :], rest[:, p, :], parts[:, p, 1, :],
                                      ALU.subtract).then_inc(split.sem, 1)
                    dve.wait_ge(peaks, n + 1)
                    order(dve.tensor_reduce(now[:, p:p + 1], qk[:, p, :], AX_X, ALU.max,
                                            apply_absolute_value=True))
                    dve.tensor_tensor(peak[:], peak[:], now[:, p:p + 1], ALU.max).then_inc(peaks, 1)
            dve.wait_ge(turned, 1)
            dve.tensor_reduce(both[:, 0:1], ps_peak[0:1, 0:C], AX_X, ALU.max).then_inc(flagged, 1)
            dve.tensor_reduce(both[:, 1:2], ps_peak[0:1, C:2 * C], AX_X, ALU.max).then_inc(flagged, 1)
            dve.wait_ge(flagged, 2)
            dve.tensor_tensor(both[:, 0:1], both[:, 0:1], both[:, 1:2], ALU.mult).then_inc(flagged, 1)
            dve.wait_ge(flagged, 3)
            dve.tensor_scalar(flag[:], both[:, 0:1], MAX_SCORE / HD, None, ALU.is_le).then_inc(flagged, 1)

        @block.gpsimd
        def _(pool):
            for k, half, j in pairs(pool):
                for p in range(2):
                    split.wait(pool, k * 2 + p)
                    for s in range(2):
                        for i in range(3):
                            pool.dma_start(A["qk_rows"][s][bass.ds((half * 2 + p) * HEADS, HEADS), i, :,
                                                           bass.ds(j * CH, CH)],
                                           parts[C * s:C * s + C, p, i, :]).then_inc(out[p], 16)
            for p in range(2):
                pool.wait_ge(out[p], 96 * K)


def values(nc, sems, A):
    with ExitStack() as ctx:
        m = Place(nc, "val", ctx, sems)
        w, bv, ones = m.sb("w", [C, C]), m.sb("bv", [1, C]), m.sb("ones", [1, KT])
        x = m.sb("x", [C, 2, LP])
        v = m.sb("v", [128, HEADS, NKT, 32])
        ps = [m.bank(f"ps{i}") for i in range(2)]
        w_in, out, filled = m.sem("w_in"), m.sem("out"), m.sem("filled")
        x_in = [m.sem(f"x_in{p}") for p in range(2)]
        mm, read = m.done("mm"), m.done("read")
        block = ctx.enter_context(nc.Block())
        groups = [range(g, min(g + 4, NKT)) for g in range(0, NKT, 4)]
        NG = len(groups)
        last_rows = L - (NKT - 1) * KT

        @block.sync
        def _(sp):
            sp.dma_start(w[:], A["W_v"]).then_inc(w_in, 16)
            sp.dma_start(bv[:], A["b_v"]).then_inc(w_in, 16)
            sp.wait_ge(filled, 2)
            for b in range(B):
                if b >= 2:
                    mm.wait(sp, (b - 1) * NG - 1)
                sp.dma_start(x[:, b % 2, 0:L], A["a2"][:, b * L:b * L + L]).then_inc(x_in[b % 2], 16)

        @block.tensor
        def _(pe):
            mm.start(pe)
            pe.wait_ge(w_in, 32)
            pe.wait_ge(filled, 4)
            for b in range(B):
                pe.wait_ge(x_in[b % 2], 16 * (b // 2 + 1))
                for g, tiles in enumerate(groups):
                    read.wait_free(pe, b * NG + g)
                    bank = ps[(b * NG + g) % 2]
                    for i, t in enumerate(tiles):
                        pe.matmul(bank[:, C * i:C * i + C], x[:, b % 2, KT * t:KT * t + KT], w[:],
                                  start=True, stop=False)
                        last = pe.matmul(bank[:, C * i:C * i + C], ones[:], bv[:], start=False, stop=True)
                    last.then_inc(mm.sem, 1)

        @block.vector
        def _(dve):
            read.start(dve)
            dve.memset(x[:, :, L:LP], 0.0).then_inc(filled, 2)
            dve.memset(v[:], 0.0).then_inc(filled, 1)
            dve.memset(ones[:], 1.0).then_inc(filled, 1)
            dve.wait_ge(filled, 4)
            dve.memset(v[:, :, 0:NKT - 1, HD:HD + 1], 1.0)
            dve.memset(v[0:last_rows, :, NKT - 1:NKT, HD:HD + 1], 1.0)
            for b in range(B):
                if b:
                    dve.wait_ge(out, 16 * b)
                for g, tiles in enumerate(groups):
                    mm.wait(dve, b * NG + g)
                    bank = ps[(b * NG + g) % 2]
                    full = [t for t in tiles if t < NKT - 1]
                    rows, n = (128, len(full)) if full else (last_rows, 1)
                    dve.tensor_copy(v[0:rows, :, tiles[0]:tiles[0] + n, 0:HD],
                                    bank[0:rows, 0:C * n].rearrange("p (t h d) -> p h t d", h=HEADS,
                                                                    d=HD)).then_inc(read.sem, 1)

        @block.gpsimd
        def _(pool):
            for b in range(B):
                read.wait(pool, b * NG + NG - 1)
                pool.dma_start(A["vals"][b * HEADS:b * HEADS + HEADS].rearrange("h p n -> p h n"),
                               v[:].rearrange("p h t d -> p h (t d)")).then_inc(out, 16)
            pool.wait_ge(out, 16 * B)


class Cut:

    def __init__(self, skip):
        half = L // 2
        self.maxima = []
        for t in range(NKT):
            keys = L
            if skip:
                keys = half if (t + 1) * KT <= half else min(L, (t + 1) * KT)
            n = -(-keys // 512)
            w = -(-keys // n)
            self.maxima += [(t, k, min(k + w, keys)) for k in range(0, keys, w)]
        self.parts = max(sum(t == u for u, _, _ in self.maxima) for t in range(NKT))
        self.groups = []
        for c in range(NJ):
            last_query = (c + 1) * CH - 1
            n = -(-max(half, last_query + 1) // KT) if skip else NKT
            self.groups += [(c, list(range(g, min(g + 2, n))), n) for g in range(0, n, 2)]
        self.NM, self.NG = len(self.maxima), len(self.groups)
        self.first = [i == 0 or g[0] != self.groups[i - 1][0] for i, g in enumerate(self.groups)]
        self.last = self.first[1:] + [True]

    def order(self, attend=True, maxima=True):
        done, end, joined_at = 0, 0.95 * self.NG, None
        for i in range(self.NG + 2 if attend else 0):
            for h in range(2):
                if h == 0 and i < self.NG:
                    yield "scores", i
                if h == 1 and i >= 2:
                    yield "weigh", i - 2
                    if self.last[i - 2]:
                        yield "copy", i - 2
                upto = min(self.NM, round(self.NM * (i + h / 2 + 0.5) / end)) if maxima else 0
                for r in range(done, upto):
                    yield "maxima", r
                if maxima and done < self.NM <= upto:
                    yield "join", 0
                    joined_at = i
                done = upto
            if i - 1 == joined_at:
                yield "turn", 0
        if not attend:
            yield from (("maxima", r) for r in range(self.NM))
            yield "join", 0
            yield "turn", 0


def slot(p, i, per, depth):
    idx, every = p * per + i, 2 * per
    back = depth if idx >= depth else next(
        d for d in range(1, 2 * depth + 1) if (idx - d if idx >= d else (idx - d) % every) % depth == idx % depth)
    return idx % depth, back


def attention(nc, sems, A):
    half, n_heads = L // 2, B * HEADS
    with ExitStack() as ctx:
        m = Place(nc, "att", ctx, sems)
        qb1, kb1 = m.sb("qb1", [128, 2, LP], BF16), m.sb("kb1", [128, 2, LP], BF16)
        qb2, kb2 = m.sb("qb2", [128, 2, LP], BF16), m.sb("kb2", [128, 2, LP], BF16)
        vh = m.sb("vh", [128, 2, NKT, 32])
        ident, ident_low = m.sb("ident", [128, 128], BF16), m.sb("ident_low", [128, 128], BF16)
        stair_qk, stair_kq = m.sb("stair_qk", [128, 2 * STAIR + CH], BF16), m.sb("stair_kq", [128, 2 * STAIR + CH], BF16)
        ident_f = m.sb("ident_f", [128, 128])
        pm, mx = m.sb("pm", [128, 2, NKT, 7]), m.sb("mx", [128, 2, NKT])
        neg, parts = m.sb("neg", [NKT, 2, KT]), m.sb("parts", [NKT, 2, 2, KT], BF16)
        NP, NS, NR = 4, 2, 2
        prob = m.sb("prob", [128, NP, 2, CH])
        o4 = m.sb("o4", [128, 2, CH])
        ps_s = [ctx.enter_context(nc.psum_tensor(f"att_ps_s{i}", [128, 2, 512], F32)) for i in range(NS)]
        ps_m = [m.bank(f"ps_m{i}") for i in range(NR)]
        ps_o = [m.bank(f"ps_o{i}") for i in range(2)]
        w_in, filled = m.sem("w_in"), m.sem("filled")
        op1_in = [m.sem(f"op1_in{p}") for p in range(2)]
        op2_in = [m.sem(f"op2_in{p}") for p in range(2)]
        neg_in = [m.sem(f"neg_in{p}") for p in range(2)]
        out = [m.sem(f"out{c}") for c in range(2)]
        score_mm, exps, pv_mm = m.done("score_mm", 8), m.done("exps", 8), m.done("pv_mm", 8)
        max_mm, max_read = m.done("max_mm", 8), m.done("max_read", 8)
        joined, split, copied, steps = m.done("joined"), m.done("split"), m.done("copied"), m.sem("steps")
        block = ctx.enter_context(nc.Block())
        loads1 = loads2 = 16 * 9

        def run_heads(eng, head):
            head(-1, -1, 1, False, True, True)
            with eng.Fori(0, n_heads // 2 - 1) as it:
                for p in range(2):
                    head(it * 2 + p, it, p, True, True, True)
            head(n_heads - 2, n_heads // 2 - 1, 0, True, True, False)
            head(n_heads - 1, n_heads // 2 - 1, 1, True, False, False)

        def load_parts(sp, qb, kb, p, n, sem):
            row = 0
            for run in (3, 2, 1):
                for i in range(run):
                    sp.dma_start(qb[row + HD * i:row + HD * i + HD, p, 0:L],
                                 A["qk_rows"][0][bass.ds(n, 1), 3 - run].rearrange("g r t -> (g r) t")).then_inc(sem, 16)
                sp.dma_start(kb[row:row + HD * run, p, 0:L],
                             A["qk_rows"][1][bass.ds(n, 1), 0:run].rearrange("g i r t -> (g i r) t")).then_inc(sem, 16)
                row += HD * run

        def work(cut):
            NM, NG, NR1 = cut.NM, cut.NG, cut.NM + 1

            def sp_head(sp, n, it, p, attend, maxima, load):
                if maxima:
                    q = 1 - p
                    if attend:
                        pv_mm.wait(sp, n * NG - 1)
                    load_parts(sp, qb2, kb2, q, n + 1, op2_in[q])
                    sp.dma_start(vh[:, q, :, :].rearrange("k t d -> k (t d)"),
                                 A["vals"][bass.ds(n + 1, 1)].rearrange("g k n -> (g k) n")).then_inc(op2_in[q], 16)
                if load:
                    if attend:
                        max_mm.wait(sp, n * NR1 + NM)
                    load_parts(sp, qb1, kb1, p, n + 2, op1_in[p])
                if maxima:
                    split.wait(sp, n + 1)
                    for a in range(2):
                        sp.dma_start(qb2[ROW_MAX + a:ROW_MAX + a + 1, q, :], parts[:, q, a, :]).then_inc(neg_in[q], 16)

            def pe_head(pe, n, it, p, attend, maxima, load):
                q = 1 - p
                turn = it + p + 1
                if attend:
                    pe.wait_ge(op2_in[p], it * (loads2 + 16) + (loads2 + 16))
                    pe.wait_ge(neg_in[p], it * 32 + 32)
                if maxima:
                    pe.wait_ge(op1_in[q], turn * loads1)
                for step, i in cut.order(attend, maxima):
                    if step == "scores":
                        c, tiles, _ = cut.groups[i]
                        s, back = slot(p, i, NG, NS)
                        q0 = c * CH
                        exps.wait_free(pe, n * NG + i, back)
                        for u, kt in enumerate(tiles):
                            k0 = kt * KT
                            lo, hi = max(q0, half), min(q0 + CH, k0 + KT)
                            dst = ps_s[s][:, u, 0:CH]
                            mult = pe.matmul(dst, kb2[:, p, k0:k0 + KT], qb2[:, p, q0:q0 + CH],
                                             start=True, stop=lo >= hi)
                            if lo < hi:
                                at = STAIR + lo - k0
                                mult = pe.matmul(dst[:, lo - q0:hi - q0], ident[:], stair_kq[:, at:at + hi - lo],
                                                 start=False, stop=True)
                        mult.then_inc(score_mm.sem, 1)
                    elif step == "weigh":
                        c, tiles, n_tiles = cut.groups[i]
                        s, _ = slot(p, i, NG, NP)
                        bank = (p * NJ + c) % 2
                        exps.wait(pe, n * NG + i)
                        if cut.first[i]:
                            copied.wait_free(pe, n * NJ + c)
                        for u, kt in enumerate(tiles):
                            k = kt % 4
                            mult = pe.matmul(ps_o[bank][32 * k:32 * k + 32, 0:CH], vh[:, p, kt, :], prob[:, s, u, :],
                                             start=kt < 4, stop=kt >= n_tiles - 4, tile_position=(0, 32 * k))
                        mult.then_inc(pv_mm.sem, 1)
                    elif step == "maxima":
                        t, k0, k1 = cut.maxima[i]
                        s, back = slot(q, i, NR1, NR)
                        q0 = t * KT
                        max_read.wait_free(pe, n * NR1 + (NR1 + i), back)
                        lo = max(k0, q0, half)
                        masked = q0 + KT > half and lo < k1
                        mult = pe.matmul(ps_m[s][:, 0:k1 - k0], qb1[:, q, q0:q0 + KT], kb1[:, q, k0:k1],
                                         start=True, stop=not masked)
                        if masked:
                            at = STAIR + lo - q0
                            mult = pe.matmul(ps_m[s][:, lo - k0:k1 - k0], (ident_low if q0 < half else ident)[:],
                                             stair_qk[:, at:at + k1 - lo], start=False, stop=True)
                        mult.then_inc(max_mm.sem, 1)
                    elif step == "turn":
                        s, back = slot(q, NM, NR1, NR)
                        joined.wait(pe, n + 1)
                        max_read.wait_free(pe, n * NR1 + (NR1 + NM), back)
                        pe.matmul(ps_m[s][0:NKT, 0:KT], mx[:, q, :], ident_f[:], start=True,
                                  stop=True).then_inc(max_mm.sem, 1)

            def act_head(act, n, it, p, attend, maxima, load):
                for step, i in cut.order(attend, maxima):
                    if step == "scores":
                        s, _ = slot(p, i, NG, NS)
                        s2, back = slot(p, i, NG, NP)
                        u = len(cut.groups[i][1])
                        score_mm.wait(act, n * NG + i)
                        pv_mm.wait_free(act, n * NG + i, back)
                        act.activation(prob[:, s2, 0:u, :], ps_s[s][:, 0:u, 0:CH], ACT.Exp).then_inc(exps.sem, 1)

            def dve_head(dve, n, it, p, attend, maxima, load):
                q = 1 - p
                for step, i in cut.order(attend, maxima):
                    if step == "maxima":
                        t, k0, k1 = cut.maxima[i]
                        s, _ = slot(q, i, NR1, NR)
                        if i == 0:
                            joined.wait_free(dve, n + 1)
                        max_mm.wait(dve, n * NR1 + (NR1 + i))
                        k = sum(t == u for u, _, _ in cut.maxima[:i])
                        dve.tensor_reduce(pm[:, q, t, k:k + 1], ps_m[s][:, 0:k1 - k0], AX_X,
                                          ALU.max).then_inc(max_read.sem, 1)
                    elif step == "join":
                        max_read.wait(dve, n * NR1 + (NR1 + NM - 1))
                        dve.tensor_reduce(mx[:, q, :], pm[:, q, :, 0:cut.parts], AX_X,
                                          ALU.max).then_inc(joined.sem, 1)
                    elif step == "turn":
                        s, _ = slot(q, NM, NR1, NR)
                        max_mm.wait(dve, n * NR1 + (NR1 + NM))
                        dve.tensor_scalar(neg[:, q, :], ps_m[s][0:NKT, 0:KT], -1.0, None,
                                          ALU.mult).then_inc(max_read.sem, 1)
                        dve.wait_ge(neg_in[q], (it + p) * 32)
                        max_read.wait(dve, n * NR1 + (NR1 + NM))
                        dve.tensor_copy(parts[:, q, 0, :], neg[:, q, :]).then_inc(steps, 1)
                        dve.wait_ge(steps, n + 2)
                        dve.tensor_tensor(parts[:, q, 1, :], neg[:, q, :], parts[:, q, 0, :],
                                          ALU.subtract).then_inc(split.sem, 1)
                    elif step == "copy":
                        c = cut.groups[i][0]
                        bank = (p * NJ + c) % 2
                        pv_mm.wait(dve, n * NG + i)
                        dve.wait_ge(out[bank], it * (64 * NJ) + 64 * ((p * NJ + c) // 2))
                        dve.tensor_copy(o4[:, bank, :], ps_o[bank][:, 0:CH]).then_inc(copied.sem, 1)

            def pool_head(pool, n, it, p, attend, maxima, load):
                for c in range(NJ if attend else 0):
                    bank = (p * NJ + c) % 2
                    copied.wait(pool, n * NJ + c)
                    for k in range(4):
                        pool.dma_start(A["att"][bass.ds(n * 4 + k, 1), :, c * CH:c * CH + CH].rearrange("g r t -> (g r) t"),
                                       o4[32 * k:32 * k + HD + 1, bank, :]).then_inc(out[bank], 16)

            return {"sp": sp_head, "pe": pe_head, "act": act_head, "dve": dve_head, "pool": pool_head}

        masked, full = work(Cut(True)), work(Cut(False))

        def engine(eng, name):
            vanish = eng.value_load(A["masks_vanish"], min_val=0, max_val=1)
            with eng.If(vanish == 1):
                run_heads(eng, lambda *a: masked[name](eng, *a))
            with eng.Else():
                run_heads(eng, lambda *a: full[name](eng, *a))

        @block.sync
        def _(sp):
            for t, a in ((ident, "c_ident_b"), (ident_low, "c_ident_low"), (stair_qk, "c_stair_qk"),
                         (stair_kq, "c_stair_kq"), (ident_f, "c_ident")):
                sp.dma_start(t[:], A[a]).then_inc(w_in, 16)
            sp.wait_ge(filled, 5)
            for p in range(2):
                for qb, kb in ((qb1, kb1), (qb2, kb2)):
                    sp.dma_start(qb[ROW_TOP:ROW_TOP + 1, p, 0:L], A["c_qrow"]).then_inc(w_in, 16)
                    sp.dma_start(kb[ROW_TOP:KROWS, p, 0:L], A["c_krows"]).then_inc(w_in, 16)
            load_parts(sp, qb1, kb1, 0, 0, op1_in[0])
            engine(sp, "sp")

        @block.tensor
        def _(pe):
            for d in (score_mm, pv_mm, max_mm):
                d.start(pe)
            pe.wait_ge(w_in, 16 * 13)
            engine(pe, "pe")

        @block.scalar
        def _(act):
            exps.start(act)
            act.preload_act_table_set("exp_and_others")
            engine(act, "act")

        @block.vector
        def _(dve):
            for d in (max_read, joined, split, copied):
                d.start(dve)
            for t in (qb1, kb1, qb2, kb2):
                dve.memset(t[:], 0.0).then_inc(filled, 1)
            dve.memset(pm[:], -3e38).then_inc(filled, 1)
            dve.wait_ge(filled, 5)
            engine(dve, "dve")

        @block.gpsimd
        def _(pool):
            engine(pool, "pool")
            for c in range(2):
                pool.wait_ge(out[c], 64 * NJ * n_heads // 2)
def add_attention(nc, sems, A):
    R, NR = 96, HEADS * 4 * (HD + 1) // 96
    with ExitStack() as ctx:
        m = Place(nc, "norm", ctx, sems)
        pick, spread = m.sb("pick", [R, NR, 128]), m.sb("spread", [R, NR, 128])
        o, x = m.sb("o", [R, 2, NR, CH]), m.sb("x", [C, 2, CH])
        rec, y, t3 = m.sb("rec", [C, 2, CH]), m.sb("y", [C, 2, CH]), m.sb("t3", [C, 2, CH])
        ps_n = [m.bank(f"ps_n{p}") for p in range(2)]
        ps_d = [m.bank(f"ps_d{p}") for p in range(2)]
        w_in, steps = m.sem("w_in"), m.sem("steps")
        x_in = [m.sem(f"x_in{p}") for p in range(2)]
        out = [m.sem(f"out{p}") for p in range(2)]
        mm, added = m.done("mm"), m.done("added")
        block = ctx.enter_context(nc.Block())

        @block.sync
        def _(sp):
            for t, a in ((pick, "c_pick"), (spread, "c_spread")):
                sp.dma_start(t[:], A[a]).then_inc(w_in, 16)
            for k, half, j in pairs(sp):
                for p in range(2):
                    b = half * 2 + p
                    added.wait_free(sp, k * 2 + p)
                    for i in range(NR):
                        sp.dma_start(o[:, p, i, :], A["att"].rearrange("(b n) r t -> b (n r) t", b=B)[bass.ds(b, 1), R * i:R * i + R,
                                                                  bass.ds(j * CH, CH)].rearrange("b r t -> (b r) t")).then_inc(x_in[p], 16)
                    sp.dma_start(x[:, p, :], A["a2"][:, bass.ds(b * L + j * CH, CH)]).then_inc(x_in[p], 16)

        @block.tensor
        def _(pe):
            mm.start(pe)
            pe.wait_ge(w_in, 32)
            for k, half, j in pairs(pe):
                for p in range(2):
                    pe.wait_ge(x_in[p], k * 64 + 64)
                    added.wait_free(pe, k * 2 + p)
                    for i in range(NR):
                        pe.matmul(ps_d[p][:, 0:CH], spread[:, i, :], o[:, p, i, :], start=i == 0, stop=i == NR - 1)
                    for i in range(NR):
                        mult = pe.matmul(ps_n[p][:, 0:CH], pick[:, i, :], o[:, p, i, :], start=i == 0, stop=i == NR - 1)
                    mult.then_inc(mm.sem, 1)

        @block.vector
        def _(dve):
            added.start(dve)
            order = Order(dve, steps, 4)
            for k, half, j in pairs(dve):
                order.at(k)
                for p in range(2):
                    mm.wait(dve, k * 2 + p)
                    order(dve.reciprocal(rec[:, p, :], ps_d[p][0:C, 0:CH]))
                    order(dve.tensor_tensor(y[:, p, :], ps_n[p][0:C, 0:CH], rec[:, p, :], ALU.mult))
                    dve.wait_ge(out[p], k * 16)
                    dve.tensor_tensor(t3[:, p, :], y[:, p, :], x[:, p, :], ALU.add).then_inc(added.sem, 1)

        @block.scalar
        def _(act):
            for k, half, j in pairs(act):
                for p in range(2):
                    added.wait(act, k * 2 + p)
                    act.dma_start(A["t3"][:, bass.ds((half * 2 + p) * L + j * CH, CH)], t3[:, p, :]).then_inc(out[p], 16)
            for p in range(2):
                act.wait_ge(out[p], 16 * 2 * NJ)


def route(nc, sems, A):
    with ExitStack() as ctx:
        m = Place(nc, "rout", ctx, sems)
        wr, br = m.sb("wr", [C, 128]), m.sb("br", [1, 1])
        x, w = m.sb("x", [C, 2, CH]), m.sb("w", [1, 2, CH])
        ps = [m.bank(f"ps{p}") for p in range(2)]
        w_in = m.sem("w_in")
        x_in = [m.sem(f"x_in{p}") for p in range(2)]
        out = [m.sem(f"out{p}") for p in range(2)]
        mm, added = m.done("mm"), m.done("added")
        block = ctx.enter_context(nc.Block())
        K = T // CH // 2

        @block.sync
        def _(sp):
            for t, a in ((wr, "wr"), (br, "br")):
                sp.dma_start(t[:], A[a]).then_inc(w_in, 16)
            with sp.Fori(0, K) as k:
                for p in range(2):
                    mm.wait_free(sp, k * 2 + p)
                    sp.dma_start(x[:, p, :], A["a3"][:, bass.ds(k * (2 * CH) + p * CH, CH)]).then_inc(x_in[p], 16)

        @block.tensor
        def _(pe):
            mm.start(pe)
            pe.wait_ge(w_in, 32)
            with pe.Fori(0, K) as k:
                for p in range(2):
                    pe.wait_ge(x_in[p], k * 16 + 16)
                    added.wait_free(pe, k * 2 + p)
                    pe.matmul(ps[p][:, 0:CH], wr[:], x[:, p, :], start=True, stop=True).then_inc(mm.sem, 1)

        @block.vector
        def _(dve):
            added.start(dve)
            dve.wait_ge(w_in, 32)
            with dve.Fori(0, K) as k:
                for p in range(2):
                    mm.wait(dve, k * 2 + p)
                    dve.wait_ge(out[p], k * 16)
                    dve.tensor_scalar(w[:, p, :], ps[p][0:1, 0:CH], br[:], None, ALU.add).then_inc(added.sem, 1)

        @block.gpsimd
        def _(pool):
            with pool.Fori(0, K) as k:
                for p in range(2):
                    added.wait(pool, k * 2 + p)
                    pool.dma_start(A["w"][:, bass.ds(k * (2 * CH) + p * CH, CH)], w[:, p, :]).then_inc(out[p], 16)
            for p in range(2):
                pool.wait_ge(out[p], 16 * K)


N_SEL = L // 2 - 1


def pick_tokens(nc, sems, A):
    W = L // 32
    with ExitStack() as ctx:
        m = Place(nc, "pick", ctx, sems)
        w, hit = m.sb("w", [128, W]), m.sb("hit", [128, W])
        group, before = m.sb("group", [128, 128]), m.sb("before", [128, 128])
        key, bit = m.sb("key", [128, 1], U32), m.sb("bit", [128, 1], U32)
        cand, flip, edge = m.sb("cand", [128, 1], U32), m.sb("flip", [128, 1], U32), m.sb("edge", [128, 1], U32)
        count, enough = m.sb("count", [128, 1]), m.sb("enough", [128, 1], U32)
        above, equal = m.sb("above", [128, W]), m.sb("equal", [128, W])
        n_above, n_equal = m.sb("n_above", [128, 1]), m.sb("n_equal", [128, 1])
        zeros, upto = m.sb("zeros", [128, W]), m.sb("upto", [128, W])
        room, take, ws = m.sb("room", [128, 1]), m.sb("take", [128, W]), m.sb("ws", [128, W])
        ps, ps2 = m.bank("ps"), m.bank("ps2")
        w_in, counted, summed, steps, done, out = (m.sem("w_in"), m.sem("counted"), m.sem("summed"),
                                                   m.sem("steps"), m.sem("done"), m.sem("out"))
        block = ctx.enter_context(nc.Block())
        BITS = 32

        @block.sync
        def _(sp):
            sp.dma_start(w[:], A["w"].rearrange("a (p c) -> (a p) c", c=W)).then_inc(w_in, 16)
            sp.dma_start(group[:], A["c_group"]).then_inc(w_in, 16)
            sp.dma_start(before[:], A["c_before"]).then_inc(w_in, 16)
            sp.dma_start(bit[:], A["c_top_bit"]).then_inc(w_in, 16)
            sp.wait_ge(done, 1)
            sp.dma_start(A["ws"].rearrange("a (p c) -> (a p) c", c=W), ws[:]).then_inc(out, 16)
            sp.wait_ge(out, 16)

        @block.tensor
        def _(pe):
            pe.wait_ge(w_in, 64)
            with pe.Fori(0, BITS) as i:
                pe.wait_ge(counted, i + 1)
                pe.matmul(ps[:, 0:1], group[:], count[:], start=True, stop=True).then_inc(summed, 1)
            pe.wait_ge(counted, BITS + 1)
            pe.matmul(ps[:, 0:1], group[:], n_above[:], start=True, stop=True)
            pe.matmul(ps2[:, 0:1], before[:], n_equal[:], start=True, stop=True).then_inc(summed, 1)

        @block.vector
        def _(dve):
            dve.memset(key[:], 0).then_inc(steps, 1)
            dve.memset(zeros[:], 0.0).then_inc(steps, 1)
            dve.wait_ge(steps, 2)
            dve.wait_ge(w_in, 64)

            def after(ins, n):
                ins.then_inc(steps, 1)
                dve.wait_ge(steps, n)

            STEPS = 7
            with dve.Fori(0, BITS) as i:
                base = i * STEPS + 2
                after(dve.tensor_tensor(cand[:], key[:], bit[:], ALU.bitwise_or), base + 1)
                after(dve.tensor_scalar(flip[:], cand[:], 31, 0xFFFFFFFF, ALU.arith_shift_right,
                                        ALU.bitwise_xor), base + 2)
                after(dve.tensor_scalar(flip[:], flip[:], 0x80000000, None, ALU.bitwise_or), base + 3)
                after(dve.tensor_tensor(edge[:], cand[:], flip[:], ALU.bitwise_xor), base + 4)
                dve.tensor_scalar(hit[:], w[:], edge[:].bitcast(F32), 0.0, ALU.is_ge, ALU.add,
                                  accum_out=count[:]).then_inc(counted, 1)
                dve.wait_ge(summed, i + 1)
                after(dve.tensor_scalar(enough[:], ps[:, 0:1], float(N_SEL), None, ALU.is_ge), base + 5)
                dve.tensor_scalar(bit[:], bit[:], 1, None, ALU.logical_shift_right).then_inc(steps, 1)
                after(dve.copy_predicated(key[:], enough[:], cand[:]), base + 7)
            n = BITS * STEPS + 2
            after(dve.tensor_scalar(flip[:], key[:], 31, 0xFFFFFFFF, ALU.arith_shift_right, ALU.bitwise_xor), n + 1)
            after(dve.tensor_scalar(flip[:], flip[:], 0x80000000, None, ALU.bitwise_or), n + 2)
            after(dve.tensor_tensor(edge[:], key[:], flip[:], ALU.bitwise_xor), n + 3)
            last = edge[:].bitcast(F32)
            after(dve.tensor_scalar(above[:], w[:], last, 0.0, ALU.is_gt, ALU.add, accum_out=n_above[:]), n + 4)
            dve.tensor_scalar(equal[:], w[:], last, 0.0, ALU.is_equal, ALU.add,
                              accum_out=n_equal[:]).then_inc(counted, 1)
            dve.wait_ge(counted, BITS + 1)
            after(dve.tensor_tensor_scan(upto[:], equal[:], zeros[:], 0.0, ALU.add, ALU.add), n + 5)
            dve.wait_ge(summed, BITS + 1)
            after(dve.tensor_scalar(room[:], ps[:, 0:1], -1.0, float(N_SEL), ALU.mult, ALU.add), n + 6)
            after(dve.tensor_tensor(room[:], room[:], ps2[:, 0:1], ALU.subtract), n + 7)
            after(dve.scalar_tensor_tensor(take[:], upto[:], room[:], equal[:], ALU.is_le, ALU.mult), n + 8)
            after(dve.tensor_tensor(take[:], take[:], above[:], ALU.add), n + 9)
            dve.tensor_tensor(ws[:], take[:], w[:], ALU.mult).then_inc(done, 1)


def build(nc, A):
    def run(stage, *args, **kwargs):
        sems = []
        stage(nc, sems, A, *args, **kwargs)
        nc.clear_and_free_semaphores(sems)
        nc.all_engine_barrier()

    run(pad_image)
    run(tokenize)
    run(layer_norm, "ln1", "h0", "hn", ("norm1_g", "norm1_b"), 2)
    run(in_projection)
    run(step_sizes)
    run(selective_scan)
    run(out_projection)
    run(layer_norm, "ln2", "h1", "m2", ("norm2_g", "norm2_b"))
    run(mlp, "mlp0", "m2", ("h0", "h1"), "t1", ("mlp_w1", "mlp_b1", "mlp_w2", "mlp_b2"),
        ACT.Gelu, "gelu_and_others")
    run(layer_norm, "ln3", "t1", "a1")
    run(experts)
    run(layer_norm, "ln4", "t2", "a2")
    run(qkv_parts)
    run(values)
    run(attention)
    run(add_attention)
    run(layer_norm, "ln5", "t3", "a3")
    run(route)
    run(pick_tokens)
    run(mlp, "mlp1", "a3", ("a3", "a3"), "t4", ("ffn_w1", "ffn_b1", "ffn_w2", "ffn_b2"),
        ACT.Gelu_apprx_tanh, "gelu_apprx_tanh_and_others", gate="ws")
    run(layer_norm, "ln6", "t4", "out")


def constants(bf16):
    blocks = np.kron(np.eye(2), np.ones((C, C)) / C)
    m = np.arange(128)
    sel, ysel = np.zeros((96, 8, 128)), np.zeros((128, 8, 32))
    for r in range(8):
        for part in range(3):
            sel[part * 32 + 4 * r + m // 32, r, m] = 1
        ysel[m, r, 4 * r + m // 32] = 1
    x, q = np.arange(2 * STAIR + CH)[None, :] - STAIR, m[:, None]
    tok = np.arange(L)
    ident_low = np.eye(128)
    ident_low[:L // 2 % KT] = 0
    krows = np.ones((3, L))
    krows[0] = np.where(tok >= L // 2, -1000.0, 0.0)
    pick, spread = np.zeros((HEADS, 4, HD + 1, 128)), np.zeros((HEADS, 4, HD + 1, 128))
    for c in range(C):
        pick[c // HD, :, c % HD, c] = 1
        spread[c // HD, :, HD, c] = 1
    pick, spread = (a.reshape(-1, 96, 128).transpose(1, 0, 2) for a in (pick, spread))
    same = m[:, None] // 32 == m[None, :] // 32
    f = {"c_center": np.eye(128) - blocks, "c_mean": blocks, "c_eps": np.full((128, 1), EPS), "c_ysel": ysel,
         "c_ident": np.eye(128), "c_rank": np.broadcast_to(N_EXP - np.arange(N_EXP), (112, 4, N_EXP)),
         "c_pick": pick, "c_spread": spread, "c_group": same,
         "c_before": same & (m[:, None] < m[None, :]),
         "c_qscale": np.repeat([[SCALE], [1.0]], C, axis=0)}
    h = {"c_sel": sel, "c_ident_b": np.eye(128), "c_ident_low": ident_low,
         "c_stair_qk": np.where(x > q, -1000.0, 0.0), "c_stair_kq": np.where(x < q, -1000.0, 0.0),
         "c_qrow": (tok < L // 2)[None, :], "c_krows": krows}
    out = {k: np.ascontiguousarray(v, np.float32) for k, v in f.items()}
    out |= {k: np.ascontiguousarray(np.asarray(v, np.float32).astype(bf16)) for k, v in h.items()}
    out["c_top_bit"] = np.full((128, 1), 1 << 31, np.uint32)
    return out


SCRATCH = {"xpad": (B, C, PW * PW), "h0": (C, T), "hn": (C, B * (L + 4)), "sz": (E, T), "u": (E, T),
           "Bn": (128, T), "Cn": (128, T), "dtp": (E, T), "yz": (E, T), "h1": (C, T), "m2": (C, T),
           "t1": (C, T), "a1": (C, T), "t2": (C, T), "a2": (C, T), "vals": (B * HEADS, 128, NKT * 32),
           "att": (B * HEADS * 4, HD + 1, L), "t3": (C, T), "a3": (C, T), "w": (1, T), "ws": (1, T), "t4": (C, T)}
PARTS = {"dt_parts": (E, T), "du_parts": (E, T)}


def program(nc, arrays):
    A = {n: nc.dram_tensor(f"in_{n}", a.shape, mybir.dt.from_np(a.dtype), kind="ExternalInput").ap()
         for n, a in arrays.items()}
    A["out"] = nc.dram_tensor("out_0_dram", (C, T), F32, kind="ExternalOutput").ap()
    for n, shape in SCRATCH.items():
        A[n] = nc.dram_tensor(f"mid_{n}", shape, F32).ap()
    for n, shape in PARTS.items():
        A[n] = [nc.dram_tensor(f"mid_{n}{i}", shape, BF16).ap() for i in range(3)]
    A["qk_rows"] = [nc.dram_tensor(f"mid_{n}_rows", (B * HEADS, 3, HD, L), BF16).ap() for n in "qk"]
    A["masks_vanish"] = nc.dram_tensor("mid_masks_vanish", (1, 1), I32).ap()
    build(nc, A)


def layouts(v):
    taps = [0, 1, 3, 4, 6, 7, 2, 5, 8]

    def by_tap(w):
        return w.reshape(C, 9, -1)[:, taps].transpose(1, 0, 2).reshape(9 * C, -1)

    def col(a):
        return a.reshape(-1, 1)

    def row(a):
        return a.reshape(1, -1)

    tok = lambda n: v["L0_tok_" + n]
    att = lambda n: v["L0_attn_" + n]
    moe = lambda n: v["L0_ffn_" + n]
    ffn = lambda n: v["L1_ffn_" + n]
    xp, qkv, bqkv = att("x_proj_w"), v["L1_attn_W_qkv"], v["L1_attn_b_qkv"]
    out = {
        "x": v["x"], "tok_W1": by_tap(tok("W1")), "tok_b1": col(tok("b1")),
        "tok_W2": np.pad(by_tap(tok("W2").T).T, ((0, 0), (0, C))), "tok_b2": by_tap(col(tok("b2"))),
        "tok_W3": np.pad(by_tap(tok("W3")), ((0, 0), (0, C))), "tok_b3": col(tok("b3")),
        "norm1_g": col(att("norm1_g")), "norm1_b": col(att("norm1_b")), "norm2_g": col(att("norm2_g")),
        "norm2_b": col(att("norm2_b")), "conv_w": att("conv_w").reshape(C, 3), "conv_b": col(att("conv_b")),
        "in_proj_w": att("in_proj_w").T, "ssm_conv_w": att("ssm_conv_w").reshape(E, 4),
        "ssm_conv_b": col(att("ssm_conv_b")), "xp_dt": xp[:DT_RANK].T,
        "xp_b": np.tile(xp[DT_RANK:DT_RANK + N_STATE].T, (1, 4)), "xp_c": np.tile(xp[DT_RANK + N_STATE:].T, (1, 4)),
        "dt_proj_w": att("dt_proj_w").T, "dt_proj_b": col(att("dt_proj_b")),
        "A_log": att("A_log").reshape(E // 4, 128).T, "Dp": col(att("Dp")), "out_proj_w": att("out_proj_w").T,
        "mlp_w1": att("mlp_w1").T, "mlp_b1": col(att("mlp_b1")), "mlp_w2": att("mlp_w2").T,
        "mlp_b2": col(att("mlp_b2")), "moe_W1": moe("W1"), "moe_b1": col(moe("b1")), "moe_Wg": moe("Wg"),
        "moe_bg": row(moe("bg")), "moe_Wd": moe("Wd").transpose(1, 0, 2).reshape(HID, N_EXP * C),
        "moe_bd": row(moe("bd")), "W_qk": qkv[:, :2 * C], "b_qk": col(bqkv[:2 * C]), "W_v": qkv[:, 2 * C:],
        "b_v": row(bqkv[2 * C:]), "wr": np.pad(ffn("wr"), ((0, 0), (0, 127))), "br": row(ffn("br")), "ffn_w1": ffn("w1"),
        "ffn_b1": col(ffn("b1")), "ffn_w2": ffn("w2"), "ffn_b2": col(ffn("b2")),
    }
    return {k: np.ascontiguousarray(a) for k, a in out.items()}


def kernel(**inputs):
    import numpy as _np
    import concourse.bacc as _bacc
    from ml_dtypes import bfloat16 as _bf16
    from concourse.bass_utils import run_bass_kernel_spmd as _run

    arrays = layouts({k: _np.asarray(a) for k, a in inputs.items()}) | constants(_bf16)
    nc = _bacc.Bacc("TRN2", target_bir_lowering=False, num_devices=1)
    program(nc, arrays)
    r = _run(nc, [{f"in_{n}": a for n, a in arrays.items()}], core_ids=[0])
    out = r.results[0]["out_0_dram"]
    return _np.ascontiguousarray(out.reshape(C, B, L).transpose(1, 2, 0))
```
